# Optimizing a Trainium2 kernel written in Bass

```python
import numpy as np
import jax
import jax.numpy as jnp

def _softmax(x, axis=-1):
    return jax.nn.softmax(x, axis=axis)

def _gelu(x):
    return jax.nn.gelu(x, approximate=True)

def _silu(x):
    return jax.nn.silu(x)

def _sigmoid(x):
    return jax.nn.sigmoid(x)

def _layernorm(x, axis=-1, eps=1e-05):
    m = jnp.mean(x, axis=axis, keepdims=True)
    v = jnp.var(x, axis=axis, keepdims=True)
    return (x - m) / jnp.sqrt(v + eps)

def _scatter_add(tgt, idx, src, axis=0):
    return tgt.at[idx].add(src)

def _segment_sum(src, seg, n):
    return jax.ops.segment_sum(src, seg, n)
kernel_name = 'mk_adj_preln_d4_adj_r2_9f3f6d'

def setup_inputs(seed: int=0):
    np.random.seed(seed)
    _w = jnp.asarray

    def _rec_inputs():
        import jax
        import jax.numpy as jnp
        _gk = jax.random.key(seed)
        x = -0.000929 + 1 * jax.random.normal(jax.random.fold_in(_gk, 1), (8, 1024, 64), jnp.float32)
        _a = jax.random.bernoulli(jax.random.fold_in(_gk, 2), 0.00390625, (1024, 1024))
        _a = jnp.logical_or(_a, jnp.eye(1024, dtype=bool))
        _af = _a.astype(jnp.float32)
        adj = _af
        return (x, adj)
    x, adj = _rec_inputs()

    def _L0_gnn_setup():
        import jax, jax.numpy as jnp
        import numpy as np
        NEG = -1000000000.0
        key = jax.random.key(seed)
        ks = jax.random.split(key, 14)
        B, N, E, NF, NH = (8, 1024, 64, 64, 64)
        x = jax.random.normal(ks[0], (B, N, NF), dtype=jnp.float32)
        base = jax.nn.one_hot(jax.random.randint(ks[1], (N,), 0, E), E, dtype=jnp.float32)
        extra = (jax.random.uniform(ks[2], (N, E)) < 0.03).astype(jnp.float32)
        H = jnp.clip(base + extra, 0.0, 1.0)
        adj = (jax.random.uniform(ks[3], (N, N)) < 0.01).astype(jnp.float32)
        adj = jnp.clip(adj + jnp.eye(N, dtype=jnp.float32), 0.0, 1.0)
        s_in = 1.0 / np.sqrt(NF)
        s_h = 1.0 / np.sqrt(NH)
        W = jax.random.normal(ks[4], (NF, NH), dtype=jnp.float32) * s_in
        W_ind = jax.random.normal(ks[5], (NF, NH), dtype=jnp.float32) * s_in
        a_node = jax.random.normal(ks[6], (NH,), dtype=jnp.float32) * s_h
        a_gn = jax.random.normal(ks[7], (NH,), dtype=jnp.float32) * s_h
        a_ge = jax.random.normal(ks[8], (NH,), dtype=jnp.float32) * s_h
        fcW = jax.random.normal(ks[9], (NH, 2 * NH), dtype=jnp.float32) * s_h
        fcb = jnp.zeros((2 * NH,), dtype=jnp.float32)
        av = jax.random.normal(ks[10], (2 * NH,), dtype=jnp.float32) / np.sqrt(2 * NH)
        return {'x': x, 'H': H, 'adj': adj, 'nhid': NH, 'W': W, 'W_ind': W_ind, 'a_node': a_node, 'a_gn': a_gn, 'a_ge': a_ge, 'fcW': fcW, 'fcb': fcb, 'av': av}
    _L0_gnn_all = _L0_gnn_setup()
    _L0_gnn_in = {k: v for k, v in _L0_gnn_all.items() if k in ('H', 'W', 'W_ind', 'a_node', 'a_gn', 'a_ge', 'fcW', 'fcb', 'av')}
    del _L0_gnn_all

    def _L1_gnn_setup():
        import jax, jax.numpy as jnp
        import numpy as np
        B, N, F_IN, F_OUT = (8, 1024, 64, 64)
        ALPHA = 0.2
        NEG = -9000000000000000.0
        key = jax.random.key(seed)
        k1, k2, k3, k4 = jax.random.split(key, 4)
        h = jax.random.normal(k1, (B, N, F_IN), dtype=jnp.float32)
        adj = jax.random.randint(k2, (N, N), 0, 2).astype(jnp.float32)
        W = jax.random.normal(k3, (F_OUT, F_IN), dtype=jnp.float32) * 0.05
        a = jax.random.normal(k4, (2 * F_OUT,), dtype=jnp.float32) * 0.05
        return {'h': h, 'adj': adj, 'W': W, 'a': a}
    _L1_gnn_all = _L1_gnn_setup()
    _L1_gnn_in = {k: v for k, v in _L1_gnn_all.items() if k in ('W', 'a')}
    del _L1_gnn_all

    def _L2_gnn_setup():
        import jax, jax.numpy as jnp
        import numpy as np
        B, N, F, L = (4, 4096, 64, 2)
        key = jax.random.key(seed)
        k1, k2, k3 = jax.random.split(key, 3)
        x = jax.random.normal(k1, (B, N, F), dtype=jnp.float32)
        net_params = jax.random.normal(k2, (L * F * F,), dtype=jnp.float32)
        A = jax.random.normal(k3, (N, N), dtype=jnp.float32)
        return {'x': x, 't': 0, 'net_params': net_params, 'A': A}
    _L2_gnn_all = _L2_gnn_setup()
    _L2_gnn_in = {k: v for k, v in _L2_gnn_all.items() if k in ('net_params',)}
    del _L2_gnn_all

    def _L3_gnn_setup():
        import jax, jax.numpy as jnp
        import numpy as np
        NEG_INF = -1e+16

        def gat_layer(x, graph, W, b):
            h = x @ W
            s = jnp.einsum('bnd,bmd->bnm', h, h) * graph
            s = jnp.where(s == 0.0, NEG_INF, s)
            a = jax.nn.softmax(s, axis=2)
            return jnp.einsum('bnm,bmd->bnd', a, h) + b
        key = jax.random.key(seed)
        k1, k2, k3, k4, k5, k6 = jax.random.split(key, 6)
        B, N, C_IN, HID, HEADS, C_OUT = (16, 512, 64, 128, 8, 64)
        flow_x = jax.random.normal(k1, (B, N, C_IN), dtype=jnp.float32)
        graph = jax.random.randint(k2, (N, N), 0, 2).astype(jnp.float32)
        Wh = jax.random.normal(k3, (HEADS, C_IN, HID), dtype=jnp.float32)
        bh = jax.random.normal(k4, (HEADS, HID), dtype=jnp.float32)
        W_out = jax.random.normal(k5, (HID * HEADS, C_OUT), dtype=jnp.float32)
        b_out = jax.random.normal(k6, (C_OUT,), dtype=jnp.float32)
        return {'flow_x': flow_x, 'graph': graph, 'Wh': Wh, 'bh': bh, 'W_out': W_out, 'b_out': b_out}
    _L3_gnn_all = _L3_gnn_setup()
    _L3_gnn_in = {k: v for k, v in _L3_gnn_all.items() if k in ('Wh', 'bh', 'W_out', 'b_out')}
    del _L3_gnn_all
    return {'x': x, 'adj': adj, 'L0_gnn_H': _L0_gnn_in['H'], 'L0_gnn_W': _L0_gnn_in['W'], 'L0_gnn_W_ind': _L0_gnn_in['W_ind'], 'L0_gnn_a_node': _L0_gnn_in['a_node'], 'L0_gnn_a_gn': _L0_gnn_in['a_gn'], 'L0_gnn_a_ge': _L0_gnn_in['a_ge'], 'L0_gnn_fcW': _L0_gnn_in['fcW'], 'L0_gnn_fcb': _L0_gnn_in['fcb'], 'L0_gnn_av': _L0_gnn_in['av'], 'L1_gnn_W': _L1_gnn_in['W'], 'L1_gnn_a': _L1_gnn_in['a'], 'L2_gnn_net_params': _L2_gnn_in['net_params'], 'L3_gnn_Wh': _L3_gnn_in['Wh'], 'L3_gnn_bh': _L3_gnn_in['bh'], 'L3_gnn_W_out': _L3_gnn_in['W_out'], 'L3_gnn_b_out': _L3_gnn_in['b_out']}

def reference(x, adj, L0_gnn_H, L0_gnn_W, L0_gnn_W_ind, L0_gnn_a_node, L0_gnn_a_gn, L0_gnn_a_ge, L0_gnn_fcW, L0_gnn_fcb, L0_gnn_av, L1_gnn_W, L1_gnn_a, L2_gnn_net_params, L3_gnn_Wh, L3_gnn_bh, L3_gnn_W_out, L3_gnn_b_out):
    import jax
    import jax.numpy as jnp

    def _L0_gnn_ref(x, H, adj, nhid, W, W_ind, a_node, a_gn, a_ge, fcW, fcb, av):
        import jax, jax.numpy as jnp
        import numpy as np
        NEG = -1000000000.0
        h = x @ W
        maskEN = H.T
        s = jax.nn.leaky_relu(h @ a_node, 0.2)
        logits = jnp.where(maskEN[None, :, :] > 0, s[:, None, :], NEG)
        alpha = jax.nn.softmax(logits, axis=-1)
        agg = jnp.einsum('ben,bnf->bef', alpha, h)
        beta = jax.nn.sigmoid((h @ a_gn)[:, None, :] + (agg @ a_ge)[:, :, None])
        all_he = beta[..., None] * h[:, None, :, :] + (1.0 - beta[..., None]) * agg[:, :, None, :]
        deg = jnp.maximum(adj.sum(-1), 1.0)[:, None]
        industry = jnp.einsum('nm,bmf->bnf', adj / deg, x @ W_ind)
        all_he = jax.nn.elu(all_he)
        he = jax.nn.elu(agg)

        def attn_scores(f):
            return jnp.tanh(f @ fcW + fcb) @ av
        se = attn_scores(he)
        logits2 = jnp.where(H[None, :, :] > 0, se[:, None, :], NEG)
        coefs1 = jax.nn.softmax(logits2, axis=-1)
        g = jnp.einsum('bne,benf->bnf', coefs1, all_he)
        pair = jnp.stack([industry, g], axis=2)
        coefs2 = jax.nn.softmax(attn_scores(pair), axis=-1)
        out = jnp.einsum('bnk,bnkf->bnf', coefs2, pair)
        return out

    def _L1_gnn_ref(h, adj, W, a):
        import jax, jax.numpy as jnp
        import numpy as np
        B, N, F_IN, F_OUT = (8, 1024, 64, 64)
        ALPHA = 0.2
        NEG = -9000000000000000.0
        Wh = jnp.einsum('bnf,of->bno', h, W)
        e1 = Wh @ a[:F_OUT]
        e2 = Wh @ a[F_OUT:]
        e = jax.nn.leaky_relu(e1[:, :, None] + e2[:, None, :], negative_slope=ALPHA)
        att = jnp.where(adj[None, :, :] > 0, e, NEG)
        att = jax.nn.softmax(att, axis=-1)
        h_prime = jnp.einsum('bij,bjo->bio', att, Wh)
        return jax.nn.elu(h_prime)

    def _L2_gnn_ref(x, t, net_params, A):
        import jax, jax.numpy as jnp
        import numpy as np
        B, N, F, L = (4, 4096, 64, 2)
        weights = net_params.reshape(L, F, F)
        z = x.reshape(-1, A.shape[1], F)
        for i in range(L):
            h = jnp.einsum('mn,bnf->bmf', A, z)
            z = jnp.einsum('bmf,fg->bmg', h, weights[i])
            z = jax.nn.relu(z)
        return z

    def _L3_gnn_ref(flow_x, graph, Wh, bh, W_out, b_out):
        import jax, jax.numpy as jnp
        import numpy as np
        NEG_INF = -1e+16

        def gat_layer(x, graph, W, b):
            h = x @ W
            s = jnp.einsum('bnd,bmd->bnm', h, h) * graph
            s = jnp.where(s == 0.0, NEG_INF, s)
            a = jax.nn.softmax(s, axis=2)
            return jnp.einsum('bnm,bmd->bnd', a, h) + b
        heads = jax.vmap(lambda W, b: gat_layer(flow_x, graph, W, b))(Wh, bh)
        H, B, N, D = heads.shape
        cat = jnp.moveaxis(heads, 0, 2).reshape(B, N, H * D)
        x = jax.nn.leaky_relu(cat, negative_slope=0.01)
        out = gat_layer(x, graph, W_out, b_out)
        return jax.nn.leaky_relu(out, negative_slope=0.01)
    h = jnp.maximum(_layernorm(x, axis=-1), 0.0)
    x = x + _L0_gnn_ref(h, L0_gnn_H, adj, 64, L0_gnn_W, L0_gnn_W_ind, L0_gnn_a_node, L0_gnn_a_gn, L0_gnn_a_ge, L0_gnn_fcW, L0_gnn_fcb, L0_gnn_av)
    h = jnp.maximum(_layernorm(x, axis=-1), 0.0)
    x = x + _L1_gnn_ref(h, adj, L1_gnn_W, L1_gnn_a)
    h = jnp.maximum(_layernorm(x, axis=-1), 0.0)
    x = x + _L2_gnn_ref(h, 0, L2_gnn_net_params, adj)
    h = jnp.maximum(_layernorm(x, axis=-1), 0.0)
    x = x + _L3_gnn_ref(h, adj, L3_gnn_Wh, L3_gnn_bh, L3_gnn_W_out, L3_gnn_b_out)
    return x

_drawn_inputs = setup_inputs


def setup_inputs(seed=0):
    import zlib

    import numpy as np

    out = dict(_drawn_inputs(seed))
    spreads = {'L0_gnn_fcb': (0.0, 2.0)}
    factors = {'L0_gnn_H': 11.103, 'L0_gnn_a_node': 3.179, 'L1_gnn_a': 8.0, 'L3_gnn_b_out': 26.576}
    for name, (base, spread) in spreads.items():
        noise = np.random.default_rng([zlib.crc32(name.encode()), seed]).standard_normal(out[name].shape)
        drawn = base * np.exp(spread * noise) if base else spread * noise
        out[name] = jnp.asarray(drawn.astype(out[name].dtype))
    for name, factor in factors.items():
        out[name] = (out[name] * factor).astype(out[name].dtype)
    return out
```

```python
from contextlib import ExitStack, contextmanager

import concourse.bass as bass
from concourse import mybir

ALU = mybir.AluOpType
ACT = mybir.ActivationFunctionType
F32 = mybir.dt.float32
F32R = mybir.dt.float32r
BF16 = mybir.dt.bfloat16
AX = mybir.AxisListType.X

P = 128
B, N, F = 8, 1024, 64
NT = N // P
HALF = N // 2
HEADS, HID = 8, 128
NEG = -1.0e16
HUGE = 3.0e38
EPS = 1.0e-5


class Chain:

    def __init__(self, eng, sem, base=0):
        self.eng, self.sem, self.base, self.n = eng, sem, base, 0

    def __call__(self, ins):
        self.n += 1
        ins.then_inc(self.sem, 1)
        self.eng.wait_ge(self.sem, self.base + self.n)


@contextmanager
def fresh_semaphores(nc):
    before = nc.snapshot_sems()
    yield
    nc.clear_and_free_semaphores(nc.allocated_since(before))
    nc.all_engine_barrier()


class Mem:
    pass


def layer_norm(nc, m, name):
    with ExitStack() as ctx:
        rows = B * NT
        mean = ctx.enter_context(nc.sbuf_tensor(name + "_mean", [P, rows], F32))
        var = ctx.enter_context(nc.sbuf_tensor(name + "_var", [P, rows], F32))
        sq = ctx.enter_context(nc.sbuf_tensor(name + "_sq", [P, rows, F], F32))
        step = nc.alloc_semaphore(name + "_step")
        centred = nc.alloc_semaphore(name + "_centred")
        squared = nc.alloc_semaphore(name + "_squared")
        var_ready = nc.alloc_semaphore(name + "_var_ready")
        std_ready = nc.alloc_semaphore(name + "_std_ready")
        x = m.x[:].rearrange("p t b f -> p (t b) f")
        h = m.h[:].rearrange("p t b f -> p (t b) f")
        parts = 4
        rp = rows // parts
        block = ctx.enter_context(nc.Block())

        @block.vector
        def _(dve):
            link = Chain(dve, step)
            for q in range(parts):
                r = slice(q * rp, (q + 1) * rp)
                link(dve.tensor_reduce(mean[:, r], x[:, r, :], AX, ALU.add))
                link(dve.tensor_scalar(mean[:, r], mean[:, r], 1.0 / F, None, ALU.mult))
                dve.tensor_tensor(h[:, r, :], x[:, r, :],
                                  mean[:, r].unsqueeze(2).to_broadcast([P, rp, F]),
                                  ALU.subtract).then_inc(centred, 1)
            for q in range(parts):
                r = slice(q * rp, (q + 1) * rp)
                dve.wait_ge(squared, q + 1)
                ins = dve.tensor_reduce(var[:, r], sq[:, r, :], AX, ALU.add)
                link(ins)
            dve.tensor_scalar(var[:], var[:], 1.0 / F, EPS, ALU.mult, ALU.add).then_inc(var_ready, 1)
            dve.wait_ge(std_ready, 1)
            link(dve.reciprocal(var[:], var[:]))
            dve.wait_ge(centred, parts)
            dve.scalar_tensor_tensor(out=h, in0=h, scalar=0.0,
                                     in1=var[:].unsqueeze(2).to_broadcast([P, rows, F]),
                                     op0=ALU.max, op1=ALU.mult)

        @block.scalar
        def _(act):
            for q in range(parts):
                r = slice(q * rp, (q + 1) * rp)
                act.wait_ge(centred, q + 1)
                act.activation(sq[:, r, :], h[:, r, :], ACT.Square).then_inc(squared, 1)
            act.wait_ge(var_ready, 1)
            act.activation(var[:], var[:], ACT.Sqrt).then_inc(std_ready, 1)


def attention_pipeline(nc, m, ctx, name):
    a = Mem()

    def sb(n, shape, dt=F32):
        return ctx.enter_context(nc.sbuf_tensor(f"{name}_{n}", shape, dt))

    def sem(n):
        return nc.alloc_semaphore(f"{name}_{n}")

    a.masked = sb("masked", [P, 2, N])
    a.weights = sb("weights", [P, 3, N])
    a.weights_t = sb("weights_t", [P, NT, N])
    a.neg_max = sb("neg_max", [P, 2, NT])
    a.row_sum = sb("row_sum", [P, 2, NT])
    a.row_inv = sb("row_inv", [P, 2, NT])
    a.inv_cols = sb("inv_cols", [P, HALF])
    a.z = sb("z", [P, 2, HALF])
    a.scores_ready = sem("scores_ready")
    a.tile_free = sem("tile_free")
    a.masked_ready = sem("masked_ready")
    a.exp_ready = sem("exp_ready")
    a.turned = [sem("turned0"), sem("turned1")]
    a.copied = [sem("copied0"), sem("copied1")]
    a.inv_ready = sem("inv_ready")
    a.inv_turned = sem("inv_turned")
    a.inv_copied = sem("inv_copied")
    a.z_ready = sem("z_ready")
    a.z_normed = sem("z_normed")
    return a



def pe_turn(pe, m, a, g, par, t, first):
    pe.wait_ge(a.exp_ready, g * NT + t + 1)
    for half in range(2):
        if not (first and t == 0):
            pe.wait_ge(a.copied[half], g * NT + t)
        for k in range(4):
            j = half * 4 + k
            ins = pe.transpose(m.ps_turn[:, half, k * P:(k + 1) * P],
                               a.weights[:, t % 3, j * P:(j + 1) * P], m.ident[:])
        ins.then_inc(a.turned[half], 1)


def pe_inverse_rows(pe, m, a, g, par):
    pe.wait_ge(a.inv_ready, g + 1)
    for t in range(NT):
        half = t // 4
        ins = pe.matmul(m.ps_misc[half * F:(half + 1) * F, 1, (t % 4) * P:(t % 4 + 1) * P],
                        a.row_inv[:, par, t:t + 1].to_broadcast([P, F]), m.ident[:],
                        start=True, stop=True)
    ins.then_inc(a.inv_turned, 1)


def pe_values(pe, m, a, g, par, values):
    for half in range(2):
        pe.wait_ge(a.copied[half], g * NT + NT)
    for j in range(NT):
        for half in range(2):
            ins = pe.matmul(m.ps_misc[half * F:(half + 1) * F, 0, :], values(j),
                            a.weights_t[:, j, half * HALF:(half + 1) * HALF],
                            start=(j == 0), stop=(j == NT - 1))
    ins.then_inc(a.z_ready, 1)


def dve_mask(dve, m, a, g, par, t, scores, mask, first, alone=False):
    dve.wait_ge(a.scores_ready, g * NT + t + 1)
    if not (first and t < 2):
        dve.wait_ge(a.exp_ready, g * NT + t - 1)
    if alone:
        dve.nop().then_inc(a.tile_free, 1)
    dve.tensor_tensor_reduce(a.masked[:, t % 2, :], scores, mask, -1.0, HUGE, ALU.add, ALU.min,
                             a.neg_max[:, par, t:t + 1]).then_inc(a.masked_ready, 1)


def dve_copy_turned(dve, m, a, g, par, t):
    dve.wait_ge(a.turned[1], g * NT + t + 1)
    dve.tensor_copy(a.weights_t[:, 4:8, t * P:(t + 1) * P],
                    m.ps_turn[:, 1, :].rearrange("p (k i) -> p k i", k=4)).then_inc(a.copied[1], 1)


def dve_inverse(dve, m, a, g, par):
    dve.wait_ge(a.exp_ready, g * NT + NT)
    dve.reciprocal(a.row_inv[:, par, :], a.row_sum[:, par, :]).then_inc(a.inv_ready, 1)


def dve_normalise(dve, m, a, g, par):
    dve.wait_ge(a.z_ready, g + 1)
    dve.wait_ge(a.inv_copied, g + 1)
    dve.tensor_tensor(a.z[:, par, :], m.ps_misc[:, 0, :], a.inv_cols[:], ALU.mult)\
       .then_inc(a.z_normed, 1)


def act_exp(act, m, a, g, par, t, first):
    act.wait_ge(a.masked_ready, g * NT + t + 1)
    if not (first and t < 3):
        act.wait_ge(a.turned[1], g * NT + t - 2)
    act.activation(a.weights[:, t % 3, :], a.masked[:, t % 2, :], ACT.Exp, scale=-1.0,
                   bias=a.neg_max[:, par, t:t + 1],
                   accum_out=a.row_sum[:, par, t:t + 1]).then_inc(a.exp_ready, 1)


def act_copy_turned(act, m, a, g, par, t):
    act.wait_ge(a.turned[0], g * NT + t + 1)
    act.copy(a.weights_t[:, 0:4, t * P:(t + 1) * P],
             m.ps_turn[:, 0, :].rearrange("p (k i) -> p k i", k=4)).then_inc(a.copied[0], 1)


def act_copy_inverse(act, m, a, g, par):
    act.wait_ge(a.inv_turned, g + 1)
    act.copy(a.inv_cols[:], m.ps_misc[:, 1, :]).then_inc(a.inv_copied, 1)


def split(nc, ctx, name, shape):
    return (ctx.enter_context(nc.sbuf_tensor(name + "_hi", shape, F32R)),
            ctx.enter_context(nc.sbuf_tensor(name + "_lo", shape, F32R)))


def hidden_attention(nc, m, d):
    name = "hid"
    with ExitStack() as ctx:
        a = attention_pipeline(nc, m, ctx, name)

        def sb(n, shape, dt=F32):
            return ctx.enter_context(nc.sbuf_tensor(f"{name}_{n}", shape, dt))

        def sem(n):
            return nc.alloc_semaphore(f"{name}_{n}")

        wh_t = sb("wh_t", [HID, HEADS, 2, F])
        gram = split(nc, ctx, name + "_gram", [P, HEADS, P])
        wz = sb("wz", [P, 2, HEADS, HID])
        wo = sb("wo", [HID, HEADS, F])
        bias = sb("bias", [HID, HEADS])
        x2 = sb("x2", [P, NT, 2, F])
        xs = sb("xs", [P, N], F32R)
        x_hi = sb("x_hi", [P, N], F32R)
        y = [split(nc, ctx, f"{name}_y{i}", [P, N]) for i in range(2)]
        ones = sb("ones", [P, P], F32R)
        zero_row = sb("zero_row", [P, NT])
        zero_col = sb("zero_col", [P, N])
        mask = sb("mask", [P, NT, N], BF16)
        hidden = sb("hidden", [P, N])

        loaded = sem("loaded")
        cleared = sem("cleared")
        gram_ready = sem("gram_ready")
        gram_hi = sem("gram_hi")
        gram_split = sem("gram_split")
        staged = sem("staged")
        x_turned = sem("x_turned")
        x_hi_ready = sem("x_hi_ready")
        x_split = sem("x_split")
        sums_ready = sem("sums_ready")
        prepared = sem("prepared")
        step = sem("step")
        y_ready = sem("y_ready")
        y_hi = sem("y_hi")
        y_split = sem("y_split")
        hidden_ready = sem("hidden_ready")
        hidden_biased = sem("hidden_biased")
        hidden_done = sem("hidden_done")
        out_ready = sem("out_ready")
        out_added = sem("out_added")

        block = ctx.enter_context(nc.Block())

        @block.sync
        def _(sp):
            for k in range(2):
                sp.dma_start(wh_t[:, :, k, :], d["wh_t"].rearrange("h d f -> d h f")).then_inc(loaded, 16)
            sp.wait_ge(cleared, 1)
            for k in range(2):
                sp.dma_start(wz[k * F:(k + 1) * F, k, :, :],
                             d["L3_gnn_Wh"].rearrange("h f d -> f h d")).then_inc(loaded, 16)
            sp.dma_start(wo[:], d["L3_gnn_W_out"].rearrange("(h d) f -> d h f", d=HID)).then_inc(loaded, 16)
            sp.dma_start(bias[:], d["bh_t"]).then_inc(loaded, 16)

        @block.tensor
        def _(pe):
            pe.wait_ge(loaded, 96)
            for h in range(HEADS):
                if h > 1:
                    pe.wait_ge(gram_split, h - 1)
                w2 = wh_t[:, h, :, :].rearrange("p a f -> p (a f)")
                pe.matmul(m.ps_misc[:, h % 2, 0:P], w2, w2, start=True, stop=True).then_inc(gram_ready, 1)
            pe.wait_ge(gram_split, HEADS)

            def project(g, u):
                if u > 1:
                    pe.wait_ge(out_added, g - 1)
                for half in range(2):
                    for k in range(2):
                        ins = pe.matmul(m.ps_misc[:, half, :], gram[k][:, u, :],
                                        xs[:, half * HALF:(half + 1) * HALF],
                                        start=(k == 0), stop=(k == 1))
                ins.then_inc(y_ready, 1)

            def score(g, u, t):
                if t == 0:
                    pe.wait_ge(y_split, g + 1)
                if not (u == 0 and t < 2):
                    pe.wait_ge(a.masked_ready, g * NT + t - 1)
                for half in range(2):
                    for k in range(2):
                        ins = pe.matmul(m.ps_score[:, t % 2, half * HALF:(half + 1) * HALF],
                                        xs[:, t * P:(t + 1) * P],
                                        y[u % 2][k][:, half * HALF:(half + 1) * HALF],
                                        start=(k == 0), stop=(k == 1))
                ins.then_inc(a.scores_ready, 1)

            def head_out(g, u):
                pe.wait_ge(a.z_normed, g + 1)
                for half in range(2):
                    ins = pe.matmul(m.ps_misc[:, half, :], wz[:, half, u, :], a.z[:, u % 2, :],
                                    start=True, stop=True)
                ins.then_inc(hidden_ready, 1)

            def project_out(g, u):
                pe.wait_ge(hidden_done, g + 1)
                for half in range(2):
                    ins = pe.matmul(m.ps_misc[half * F:(half + 1) * F, 0, :], wo[:, u, :],
                                    hidden[:, half * HALF:(half + 1) * HALF],
                                    start=True, stop=True)
                ins.then_inc(out_ready, 1)

            with pe.Fori(0, B) as b:
                pe.wait_ge(staged, b + 1)
                for t in range(NT):
                    ins = pe.transpose(m.ps_score[:, 0, t * P:(t + 1) * P],
                                       x2[:, t, :, :].rearrange("p a f -> p (a f)"), m.ident[:])
                ins.then_inc(x_turned, 1)
                pe.wait_ge(x_split, 2 * b + 2)
                for half in range(2):
                    ins = pe.matmul(m.ps_score[:, 1, half * HALF:(half + 1) * HALF], ones[:],
                                    xs[:, half * HALF:(half + 1) * HALF], start=True, stop=True)
                ins.then_inc(sums_ready, 1)
                project(b * HEADS, 0)
                pe.wait_ge(prepared, b + 1)
                score(b * HEADS, 0, 0)
                score(b * HEADS, 0, 1)
                for u in range(HEADS):
                    g = b * HEADS + u
                    for t in range(NT):
                        pe_turn(pe, m, a, g, u % 2, t, u == 0)
                        if t + 2 < NT:
                            score(g, u, t + 2)
                        if u and t == 0:
                            head_out(g - 1, u - 1)
                        if u and t == 3:
                            project_out(g - 1, u - 1)
                        if t == 5 and u + 1 < HEADS:
                            project(g + 1, u + 1)
                    if u + 1 < HEADS:
                        score(g + 1, u + 1, 0)
                        score(g + 1, u + 1, 1)
                    pe_inverse_rows(pe, m, a, g, u % 2)
                    if u + 1 == HEADS:
                        pe.wait_ge(out_added, g)
                    pe_values(pe, m, a, g, u % 2, lambda j: x2[:, j, 0, :])
                g = b * HEADS + HEADS - 1
                head_out(g, HEADS - 1)
                project_out(g, HEADS - 1)

        @block.vector
        def _(dve):
            dve.memset(wz[:], 0.0).then_inc(cleared, 1)
            dve.memset(hidden[:, 0:P], 1.0).then_inc(step, 1)
            dve.wait_ge(step, 1)
            dve.tensor_copy(ones[:], hidden[:, 0:P]).then_inc(step, 1)
            for h in range(HEADS):
                dve.wait_ge(gram_hi, h + 1)
                dve.tensor_tensor(gram[1][:, h, :], m.ps_misc[:, h % 2, 0:P], gram[0][:, h, :],
                                  ALU.subtract).then_inc(gram_split, 1)
            setup_steps = 2
            per_batch = 5

            def split_y(g, u):
                dve.wait_ge(y_hi, g + 1)
                dve.tensor_tensor(y[u % 2][1][:], m.ps_misc[:].rearrange("p a n -> p (a n)"),
                                  y[u % 2][0][:], ALU.subtract).then_inc(y_split, 1)

            def leaky(g):
                dve.wait_ge(hidden_biased, g + 1)
                dve.scalar_tensor_tensor(out=hidden[:], in0=hidden[:], scalar=0.01, in1=hidden[:],
                                         op0=ALU.mult, op1=ALU.max).then_inc(hidden_done, 1)

            def add_out(b, g, u):
                dve.wait_ge(out_ready, g + 1)
                out = m.h2t[:, b, :]
                if u == 0:
                    dve.nop().then_inc(a.tile_free, 1)
                    dve.tensor_copy(out, m.ps_misc[:, 0, :]).then_inc(out_added, 1)
                else:
                    dve.wait_ge(out_added, g)
                    dve.tensor_tensor(out, out, m.ps_misc[:, 0, :], ALU.add).then_inc(out_added, 1)

            with dve.Fori(0, B) as b:
                link = Chain(dve, step, setup_steps + b * per_batch)
                link(dve.tensor_copy(x2[:, :, 0, :], m.h[:, :, b, :]))
                link(dve.tensor_copy(x2[:, :, 1, :], x2[:, :, 0, :]))
                dve.nop().then_inc(staged, 1)
                link(dve.tensor_reduce(zero_row[:], x2[:, :, 0, :], AX, ALU.max))
                link(dve.tensor_scalar(zero_row[:], zero_row[:], 0.0, NEG, ALU.is_equal, ALU.mult))
                dve.wait_ge(x_hi_ready, b + 1)
                dve.tensor_tensor(xs[F:P, :], m.ps_score[F:P, 0, :], x_hi[F:P, :],
                                  ALU.subtract).then_inc(x_split, 1)
                dve.wait_ge(sums_ready, b + 1)
                dve.tensor_scalar(zero_col[:], m.ps_score[:, 1, :], 0.0, NEG, ALU.is_equal,
                                  ALU.mult).then_inc(prepared, 1)
                dve.wait_ge(prepared, b + 1)
                for t in range(NT):
                    ins = dve.scalar_tensor_tensor(out=mask[:, t, :], in0=zero_col[:],
                                                   scalar=zero_row[:, t:t + 1], in1=m.mask[:, t, :],
                                                   op0=ALU.min, op1=ALU.min)
                link(ins)
                split_y(b * HEADS, 0)
                for u in range(HEADS):
                    g = b * HEADS + u
                    for t in range(NT):
                        dve_mask(dve, m, a, g, u % 2, t, m.ps_score[:, t % 2, :], mask[:, t, :], u == 0, True)
                        if t == 1 and u:
                            dve_normalise(dve, m, a, g - 1, (u - 1) % 2)
                        if t == 3 and u:
                            leaky(g - 1)
                        if t == 5 and u:
                            add_out(b, g - 1, u - 1)
                        if t >= 2:
                            dve_copy_turned(dve, m, a, g, u % 2, t - 2)
                    if u + 1 < HEADS:
                        split_y(g + 1, u + 1)
                    dve_copy_turned(dve, m, a, g, u % 2, NT - 2)
                    dve_copy_turned(dve, m, a, g, u % 2, NT - 1)
                    dve_inverse(dve, m, a, g, u % 2)
                g = b * HEADS + HEADS - 1
                dve_normalise(dve, m, a, g, 1)
                leaky(g)
                add_out(b, g, HEADS - 1)

        @block.scalar
        def _(act):
            for h in range(HEADS):
                act.wait_ge(gram_ready, h + 1)
                act.copy(gram[0][:, h, :], m.ps_misc[:, h % 2, 0:P]).then_inc(gram_hi, 1)

            def round_y(g, u):
                act.wait_ge(y_ready, g + 1)
                act.copy(y[u % 2][0][:], m.ps_misc[:].rearrange("p a n -> p (a n)")).then_inc(y_hi, 1)

            def add_bias(g, u):
                act.wait_ge(hidden_ready, g + 1)
                act.activation(hidden[:], m.ps_misc[:].rearrange("p a n -> p (a n)"), ACT.Identity,
                               bias=bias[:, u:u + 1]).then_inc(hidden_biased, 1)

            with act.Fori(0, B) as b:
                act.wait_ge(x_turned, b + 1)
                act.copy(x_hi[:], m.ps_score[:, 0, :]).then_inc(x_hi_ready, 1)
                act.copy(xs[0:F, :], m.ps_score[0:F, 0, :]).then_inc(x_split, 1)
                round_y(b * HEADS, 0)
                for u in range(HEADS):
                    g = b * HEADS + u
                    for t in range(NT):
                        act_exp(act, m, a, g, u % 2, t, u == 0)
                        if u and t == 0:
                            act_copy_inverse(act, m, a, g - 1, (u - 1) % 2)
                        if u and t == 2:
                            add_bias(g - 1, u - 1)
                        if t >= 1:
                            act_copy_turned(act, m, a, g, u % 2, t - 1)
                    if u + 1 < HEADS:
                        round_y(g + 1, u + 1)
                    act_copy_turned(act, m, a, g, u % 2, NT - 1)
                g = b * HEADS + HEADS - 1
                act_copy_inverse(act, m, a, g, 1)
                add_bias(g, HEADS - 1)


def out_attention(nc, m, d):
    name = "out"
    with ExitStack() as ctx:
        a = attention_pipeline(nc, m, ctx, name)

        def sb(n, shape, dt=F32):
            return ctx.enter_context(nc.sbuf_tensor(f"{name}_{n}", shape, dt))

        def sem(n):
            return nc.alloc_semaphore(f"{name}_{n}")

        x2 = sb("x2", [P, 2, NT, 2, F])
        x_hi = sb("x_hi", [P, 2, N], F32R)
        x_lo = sb("x_lo", [P, 2, N], F32R)
        xs = sb("xs", [P, 2, N], F32R)
        squares = sb("squares", [P, N], F32R)
        row_squares = sb("row_squares", [P, NT, F])
        ones = sb("ones", [P, P], F32R)
        ones_f = sb("ones_f", [P, P])
        zero_row = sb("zero_row", [P, 2, NT])
        zero_col = sb("zero_col", [P, 2, N])
        mask = sb("mask", [P, 2, N])
        bias = sb("bias", [P, 1])

        loaded = sem("loaded")
        step = sem("step")
        rows_ready = sem("rows_ready")
        rows_copied = sem("rows_copied")
        x_turned = sem("x_turned")
        x_hi_ready = sem("x_hi_ready")
        x_lo_ready = sem("x_lo_ready")
        xs_ready = sem("xs_ready")
        squared = sem("squared")
        sums_ready = sem("sums_ready")
        zeros_ready = sem("zeros_ready")
        activated = sem("activated")
        out_turned = sem("out_turned")
        added = sem("added")
        block = ctx.enter_context(nc.Block())

        @block.sync
        def _(sp):
            for k in range(2):
                sp.dma_start(bias[k * F:(k + 1) * F, :],
                             d["L3_gnn_b_out"].rearrange("(f a) -> f a", a=1)).then_inc(loaded, 16)

        @block.tensor
        def _(pe):
            def rows(u):
                if u:
                    pe.wait_ge(added, u - 1 if u > 1 else 0)
                for c in range(NT // 2):
                    ins = pe.transpose(m.ps_misc[:, 0, c * P:(c + 1) * P],
                                       m.h2t[:, u, c * P:(c + 1) * P], m.ident[:])
                ins.then_inc(rows_ready, 1)

            def turn_rows(u):
                pe.wait_ge(rows_copied, 2 * u + 2)
                for t in range(NT):
                    ins = pe.transpose(m.ps_misc[:, t // 4, (t % 4) * P:(t % 4 + 1) * P],
                                       x2[:, u % 2, t, :, :].rearrange("p a f -> p (a f)"), m.ident[:])
                ins.then_inc(x_turned, 1)

            def sum_squares(u):
                pe.wait_ge(squared, u + 1)
                pe.wait_ge(x_lo_ready, u + 1)
                for half in range(2):
                    ins = pe.matmul(m.ps_misc[:, half, :], ones[:],
                                    squares[:, half * HALF:(half + 1) * HALF], start=True, stop=True)
                ins.then_inc(sums_ready, 1)

            def score(u, t):
                if t == 0:
                    pe.wait_ge(xs_ready, 2 * u + 2)
                if not (u == 0 and t < 2):
                    pe.wait_ge(a.masked_ready, u * NT + t - 1)
                for half in range(2):
                    for k, part in enumerate((x_hi, x_lo)):
                        ins = pe.matmul(m.ps_score[:, t % 2, half * HALF:(half + 1) * HALF],
                                        xs[:, u % 2, t * P:(t + 1) * P],
                                        part[:, u % 2, half * HALF:(half + 1) * HALF],
                                        start=(k == 0), stop=(k == 1))
                ins.then_inc(a.scores_ready, 1)

            def turn_out(u):
                pe.wait_ge(activated, u + 1)
                for c in range(NT // 2):
                    ins = pe.transpose(m.ps_misc[:, 1, c * P:(c + 1) * P],
                                       a.z[:, u % 2, c * P:(c + 1) * P], m.ident[:])
                ins.then_inc(out_turned, 1)

            pe.wait_ge(step, 2)
            rows(0)
            turn_rows(0)
            sum_squares(0)
            score(0, 0)
            score(0, 1)
            for u in range(B):
                for t in range(NT):
                    pe_turn(pe, m, a, u, u % 2, t, u == 0)
                    if t + 2 < NT:
                        score(u, t + 2)
                    if u and t == 2:
                        turn_out(u - 1)
                    if u + 1 < B and t == 3:
                        if u:
                            pe.wait_ge(a.z_normed, u)
                        else:
                            pe.wait_ge(zeros_ready, 1)
                        rows(u + 1)
                    if u + 1 < B and t == 4:
                        if u:
                            pe.wait_ge(added, u)
                        turn_rows(u + 1)
                    if u + 1 < B and t == 6:
                        sum_squares(u + 1)
                if u + 1 < B:
                    score(u + 1, 0)
                    score(u + 1, 1)
                    pe.wait_ge(zeros_ready, u + 2)
                else:
                    pe.wait_ge(added, u)
                pe_inverse_rows(pe, m, a, u, u % 2)
                pe_values(pe, m, a, u, u % 2, lambda j: x2[:, u % 2, j, 0, :])
            turn_out(B - 1)

        @block.vector
        def _(dve):
            link = Chain(dve, step)
            link(dve.memset(ones_f[:], 1.0))
            link(dve.tensor_copy(ones[:], ones_f[:]))
            dve.wait_ge(loaded, 32)

            def copy_rows(u):
                dve.wait_ge(rows_copied, 2 * u + 1)
                dve.tensor_copy(x2[:, u % 2, :, 1, :], x2[:, u % 2, :, 0, :]).then_inc(rows_copied, 1)
                link(dve.tensor_tensor(row_squares[:], x2[:, u % 2, :, 0, :], x2[:, u % 2, :, 0, :], ALU.mult))
                link(dve.tensor_reduce(zero_row[:, u % 2, :], row_squares[:], AX, ALU.max))
                link(dve.tensor_scalar(zero_row[:, u % 2, :], zero_row[:, u % 2, :], 0.0, NEG,
                                       ALU.is_equal, ALU.mult))

            def split_x(u):
                dve.wait_ge(x_hi_ready, u + 1)
                dve.tensor_tensor(x_lo[:, u % 2, :], m.ps_misc[:].rearrange("p a n -> p (a n)"),
                                  x_hi[:, u % 2, :], ALU.subtract).then_inc(x_lo_ready, 1)
                dve.wait_ge(x_lo_ready, u + 1)
                dve.tensor_copy(xs[F:P, u % 2, :], x_lo[F:P, u % 2, :]).then_inc(xs_ready, 1)

            def find_zeros(u):
                dve.wait_ge(sums_ready, u + 1)
                dve.tensor_scalar(zero_col[:, u % 2, :], m.ps_misc[:].rearrange("p a n -> p (a n)"),
                                  0.0, NEG, ALU.is_equal, ALU.mult).then_inc(zeros_ready, 1)

            def mask_tile(u, t):
                if t == 0:
                    dve.wait_ge(zeros_ready, u + 1)
                link(dve.scalar_tensor_tensor(out=mask[:, t % 2, :], in0=zero_col[:, u % 2, :],
                                              scalar=zero_row[:, u % 2, t:t + 1], in1=m.mask[:, t, :],
                                              op0=ALU.min, op1=ALU.min))
                dve_mask(dve, m, a, u, u % 2, t, m.ps_score[:, t % 2, :], mask[:, t % 2, :], u == 0)

            def activate(u):
                dve_normalise(dve, m, a, u, u % 2)
                dve.wait_ge(a.z_normed, u + 1)
                z = a.z[:, u % 2, :]
                link(dve.tensor_scalar(z, z, bias[:, 0:1], None, ALU.add))
                dve.scalar_tensor_tensor(out=z, in0=z, scalar=0.01, in1=z, op0=ALU.mult,
                                         op1=ALU.max).then_inc(activated, 1)

            def add(u):
                dve.wait_ge(out_turned, u + 1)
                src = m.ps_misc[:, 1, :].rearrange("p (c a f) -> p c a f", c=4, a=2)
                x = m.x[:, :, u, :].rearrange("p (a c) f -> p c a f", a=2)
                link(dve.tensor_tensor(x[:, :, 0, :], x[:, :, 0, :], src[:, :, 0, :], ALU.add))
                dve.tensor_tensor(x[:, :, 1, :], x[:, :, 1, :], src[:, :, 1, :], ALU.add).then_inc(added, 1)

            copy_rows(0)
            split_x(0)
            find_zeros(0)
            for u in range(B):
                for t in range(NT):
                    mask_tile(u, t)
                    if u and t == 1:
                        activate(u - 1)
                    if u and t == 4:
                        add(u - 1)
                    if t >= 2:
                        dve_copy_turned(dve, m, a, u, u % 2, t - 2)
                    if u + 1 < B and t == 5:
                        copy_rows(u + 1)
                    if u + 1 < B and t == 6:
                        split_x(u + 1)
                dve_copy_turned(dve, m, a, u, u % 2, NT - 2)
                if u + 1 < B:
                    find_zeros(u + 1)
                dve_copy_turned(dve, m, a, u, u % 2, NT - 1)
                dve_inverse(dve, m, a, u, u % 2)
            activate(B - 1)
            add(B - 1)

        @block.scalar
        def _(act):
            def copy_rows(u):
                act.wait_ge(rows_ready, u + 1)
                dst = x2[:, u % 2, :, 0, :].rearrange("p (a c) f -> p a c f", a=2)
                src = m.ps_misc[:, 0, :].rearrange("p (c a f) -> p a c f", c=4, a=2)
                act.copy(dst, src).then_inc(rows_copied, 1)

            def split_x(u):
                act.wait_ge(x_turned, u + 1)
                ps = m.ps_misc[:].rearrange("p a n -> p (a n)")
                act.copy(x_hi[:, u % 2, :], ps).then_inc(x_hi_ready, 1)
                act.wait_ge(x_hi_ready, u + 1)
                act.copy(xs[0:F, u % 2, :], x_hi[0:F, u % 2, :]).then_inc(xs_ready, 1)
                act.activation(squares[:], x_hi[:, u % 2, :], ACT.Square).then_inc(squared, 1)

            copy_rows(0)
            split_x(0)
            for u in range(B):
                for t in range(NT):
                    act_exp(act, m, a, u, u % 2, t, u == 0)
                    if u and t == 0:
                        act_copy_inverse(act, m, a, u - 1, (u - 1) % 2)
                    if t >= 1:
                        act_copy_turned(act, m, a, u, u % 2, t - 1)
                    if u + 1 < B and t == 4:
                        copy_rows(u + 1)
                    if u + 1 < B and t == 5:
                        split_x(u + 1)
                act_copy_turned(act, m, a, u, u % 2, NT - 1)
            act_copy_inverse(act, m, a, B - 1, 1)


def project(nc, m, ctx, name, weight, width, dests):
    turned = ctx.enter_context(nc.sbuf_tensor(name + "_turned", [P, B // 2, N], F32))
    ready = nc.alloc_semaphore(name + "_ready")
    copied = nc.alloc_semaphore(name + "_copied")
    done = nc.alloc_semaphore(name + "_done")
    taken = [nc.alloc_semaphore(f"{name}_taken{i}") for i in range(2)]
    with ExitStack() as inner:
        block = inner.enter_context(nc.Block())
        pairs = [(q, t) for q in range(B // 2) for t in range(NT)]

        @block.tensor
        def _(pe):
            for q in range(B // 2):
                if q >= 2:
                    pe.wait_ge(copied, q - 1)
                for t in range(NT):
                    ins = pe.transpose(m.ps_score[:, q % 2, t * P:(t + 1) * P],
                                       m.h[:, t, 2 * q:2 * q + 2, :].rearrange("p a f -> p (a f)"),
                                       m.ident[:])
                ins.then_inc(ready, 1)
            for i, (q, t) in enumerate(pairs):
                if t == 0:
                    pe.wait_ge(copied, q + 1)
                if i >= 4:
                    pe.wait_ge(taken[i % 2], (i - 4) // 2 + 1)
                bank = m.ps_misc[:, i % 4 // 2, 0:width] if i % 2 else m.ps_turn[:, i % 4 // 2, 0:width]
                pe.matmul(bank, turned[:, q, t * P:(t + 1) * P], weight, start=True,
                          stop=True).then_inc(done, 1)

        def take(eng, copy, parity):
            for q in range(parity, B // 2, 2):
                eng.wait_ge(ready, q + 1)
                if q >= 1:
                    eng.wait_ge(copied, q)
                copy(turned[:, q, :], m.ps_score[:, q % 2, :]).then_inc(copied, 1)
            for i, (q, t) in enumerate(pairs):
                if i % 2 != parity:
                    continue
                eng.wait_ge(done, i + 1)
                bank = m.ps_misc if i % 2 else m.ps_turn
                for lo, hi, place in dests:
                    ins = copy(place(q, t), bank[:, i % 4 // 2, lo:hi])
                ins.then_inc(taken[parity], 1)

        @block.vector
        def _(dve):
            take(dve, dve.tensor_copy, 0)

        @block.scalar
        def _(act):
            take(act, act.copy, 1)
    return turned


def mix(nc, m, ctx, name, values, finish, act_finish=None):
    hi, lo = split(nc, ctx, name + "_v", [P, NT, B * F])
    rounded = nc.alloc_semaphore(name + "_rounded")
    parted = nc.alloc_semaphore(name + "_parted")
    mixed = nc.alloc_semaphore(name + "_mixed")
    finished = nc.alloc_semaphore(name + "_finished")
    with ExitStack() as inner:
        block = inner.enter_context(nc.Block())

        def bank(t):
            return m.ps_misc[:, t % 2, :]

        @block.scalar
        def _(act):
            for t in range(NT):
                act.copy(hi[:, t, :], values(t)).then_inc(rounded, 1)

        @block.tensor
        def _(pe):
            for t in range(NT):
                if t >= 2:
                    pe.wait_ge(finished, t - 1)
                for j in range(NT):
                    if t == 0:
                        pe.wait_ge(parted, j + 1)
                    for k, part in enumerate((hi, lo)):
                        ins = pe.matmul(bank(t), m.adj_t[:, j, t * P:(t + 1) * P], part[:, j, :],
                                        start=(j == 0 and k == 0), stop=(j == NT - 1 and k == 1))
                ins.then_inc(mixed, 1)

        @block.vector
        def _(dve):
            for t in range(NT):
                dve.wait_ge(rounded, t + 1)
                dve.tensor_tensor(lo[:, t, :], values(t), hi[:, t, :], ALU.subtract).then_inc(parted, 1)
            for t in range(NT):
                dve.wait_ge(mixed, t + 1)
                finish(dve, t, bank(t)).then_inc(finished, 1)


def block_weights(nc, ctx, name, loads, width):
    w = ctx.enter_context(nc.sbuf_tensor(name + "_w", [P, width], F32))
    cleared = nc.alloc_semaphore(name + "_w_cleared")
    loaded = nc.alloc_semaphore(name + "_w_loaded")
    with ExitStack() as inner:
        block = inner.enter_context(nc.Block())

        @block.vector
        def _(dve):
            dve.memset(w[:], 0.0).then_inc(cleared, 1)

        @block.sync
        def _(sp):
            sp.wait_ge(cleared, 1)
            for row, col, src in loads:
                sp.dma_start(w[row:row + src.shape[0], col:col + src.shape[1]], src).then_inc(loaded, 16)
            sp.wait_ge(loaded, 16 * len(loads))
    return w


def graph_layer(nc, m, d):
    with ExitStack() as ctx:
        for r in range(2):
            src = d["L2_w"][r]
            w = block_weights(nc, ctx, f"gl{r}", [(0, 0, src), (F, F, src)], P)
            with ExitStack() as part:
                zw = part.enter_context(nc.sbuf_tensor(f"gl{r}_zw", [P, NT, B, F], F32))
                project(nc, m, part, f"gl{r}_p", w[:], P, [
                    (0, P, lambda q, t: zw[:, t, 2 * q:2 * q + 2, :].rearrange("p a f -> p (a f)"))])

                def finish(dve, t, ps):
                    h = m.h[:, t, :, :].rearrange("p b f -> p (b f)")
                    x = m.x[:, t, :, :].rearrange("p b f -> p (b f)")
                    if r == 0:
                        return dve.tensor_scalar(h, ps, 0.0, None, ALU.max)
                    return dve.scalar_tensor_tensor(out=x, in0=ps, scalar=0.0, in1=x,
                                                    op0=ALU.max, op1=ALU.add)

                mix(nc, m, part, f"gl{r}_m", lambda t: zw[:, t, :, :].rearrange("p b f -> p (b f)"), finish)


def graph_attention_layer(nc, m, d):
    name = "gat"
    with ExitStack() as ctx:
        def sb(n, shape, dt=F32):
            return ctx.enter_context(nc.sbuf_tensor(f"{name}_{n}", shape, dt))

        def sem(n):
            return nc.alloc_semaphore(f"{name}_{n}")

        width = P + 2
        w = block_weights(nc, ctx, "gat", [(0, 0, d["l1_wt"]), (F, F, d["l1_wt"])], width)
        w_rows = sb("w_rows", [F, 2, F])
        a_cols = sb("a_cols", [F, 2])
        a2_w = sb("a2_w", [P, 2, P])
        wh = sb("wh", [P, NT, B, F])
        e1 = sb("e1", [P, NT, B])
        with ExitStack() as prep:
            loaded = nc.alloc_semaphore("gat_loaded")
            ready = nc.alloc_semaphore("gat_ready")
            cleared = nc.alloc_semaphore("gat_cleared")
            block = prep.enter_context(nc.Block())

            @block.sync
            def _(sp):
                for k in range(2):
                    sp.dma_start(w_rows[:, k, :], d["L1_gnn_W"]).then_inc(loaded, 16)
                sp.dma_start(a_cols[:], d["l1_a"]).then_inc(loaded, 16)

            @block.tensor
            def _(pe):
                pe.wait_ge(loaded, 48)
                rows = w_rows[:].rearrange("o a f -> o (a f)")
                pe.matmul(m.ps_misc[:, 0, 0:P], rows, a_cols[:, 1:2].to_broadcast([F, P]),
                          start=True, stop=True)
                pe.matmul(m.ps_misc[:, 1, 0:1], rows, a_cols[:, 0:1], start=True, stop=True)\
                  .then_inc(ready, 1)

            @block.vector
            def _(dve):
                dve.memset(a2_w[:], 0.0).then_inc(cleared, 1)
                dve.wait_ge(ready, 1)
                dve.wait_ge(cleared, 1)
                for k in range(2):
                    half = slice(k * F, (k + 1) * F)
                    dve.tensor_copy(a2_w[half, k, :], m.ps_misc[half, 0, 0:P])
                    dve.tensor_copy(w[half, P + k:P + k + 1], m.ps_misc[half, 1, 0:1])

        x_t = project(nc, m, ctx, "gat_p", w[:], width, [
            (0, P, lambda q, t: wh[:, t, 2 * q:2 * q + 2, :].rearrange("p a f -> p (a f)")),
            (P, P + 2, lambda q, t: e1[:, t, 2 * q:2 * q + 2])])

        a = attention_pipeline(nc, m, ctx, name)
        e2 = sb("e2", [P, 2, N])
        sums = sb("sums", [P, 2, N])
        z_exp = sb("z_exp", [P, HALF])
        step = sem("step")
        e2_ready = sem("e2_ready")
        e2_copied = sem("e2_copied")
        summed = sem("summed")
        z_exped = sem("z_exped")
        activated = sem("activated")
        out_turned = sem("out_turned")
        added = sem("added")
        block = ctx.enter_context(nc.Block())

        @block.tensor
        def _(pe):
            def spread_e2(u):
                for half in range(2):
                    ins = pe.matmul(m.ps_score[:, u % 2, half * HALF:(half + 1) * HALF],
                                    a2_w[:, u % 2, :], x_t[:, u // 2, half * HALF:(half + 1) * HALF],
                                    start=True, stop=True)
                ins.then_inc(e2_ready, 1)

            def turn_out(u):
                pe.wait_ge(activated, u + 1)
                for c in range(NT // 2):
                    ins = pe.transpose(m.ps_score[:, 0, c * P:(c + 1) * P],
                                       a.z[:, u % 2, c * P:(c + 1) * P], m.ident[:])
                ins.then_inc(out_turned, 1)

            spread_e2(0)
            for u in range(B):
                for t in range(NT):
                    pe_turn(pe, m, a, u, u % 2, t, u == 0)
                    if u and t == 2:
                        turn_out(u - 1)
                    if u + 1 < B and t == 4:
                        pe.wait_ge(e2_copied, u + 1)
                        if u:
                            pe.wait_ge(added, u)
                        spread_e2(u + 1)
                pe_inverse_rows(pe, m, a, u, u % 2)
                pe_values(pe, m, a, u, u % 2, lambda j: wh[:, j, u, :])
            turn_out(B - 1)

        @block.scalar
        def _(act):
            def copy_e2(u):
                act.wait_ge(e2_ready, u + 1)
                act.copy(e2[:, u % 2, :], m.ps_score[:, u % 2, :]).then_inc(e2_copied, 1)

            def add_e1(u, t):
                if t == 0:
                    act.wait_ge(e2_copied, u + 1)
                if u or t >= 2:
                    act.wait_ge(a.masked_ready, u * NT + t - 1)
                act.activation(sums[:, t % 2, :], e2[:, u % 2, :], ACT.Identity,
                               bias=e1[:, t, u:u + 1]).then_inc(summed, 1)

            def exp_z(u):
                act.wait_ge(a.z_normed, u + 1)
                act.activation(z_exp[:], a.z[:, u % 2, :], ACT.Exp).then_inc(z_exped, 1)

            copy_e2(0)
            add_e1(0, 0)
            add_e1(0, 1)
            for u in range(B):
                for t in range(NT):
                    act_exp(act, m, a, u, u % 2, t, u == 0)
                    if t + 2 < NT:
                        add_e1(u, t + 2)
                    if u and t == 0:
                        act_copy_inverse(act, m, a, u - 1, (u - 1) % 2)
                    if u and t == 1:
                        exp_z(u - 1)
                    if t >= 1:
                        act_copy_turned(act, m, a, u, u % 2, t - 1)
                    if u + 1 < B and t == 6:
                        copy_e2(u + 1)
                        add_e1(u + 1, 0)
                        add_e1(u + 1, 1)
                act_copy_turned(act, m, a, u, u % 2, NT - 1)
            act_copy_inverse(act, m, a, B - 1, 1)
            exp_z(B - 1)

        @block.vector
        def _(dve):
            link = Chain(dve, step)

            def mask_tile(u, t):
                dve.wait_ge(summed, u * NT + t + 1)
                s = sums[:, t % 2, :]
                dve.scalar_tensor_tensor(out=s, in0=s, scalar=0.2, in1=s, op0=ALU.mult,
                                         op1=ALU.max).then_inc(a.scores_ready, 1)
                dve_mask(dve, m, a, u, u % 2, t, s, m.mask[:, t, :], u == 0)

            def elu(u):
                dve.wait_ge(z_exped, u + 1)
                link(dve.tensor_scalar(z_exp[:], z_exp[:], 1.0, -1.0, ALU.min, ALU.add))
                dve.tensor_tensor(a.z[:, u % 2, :], a.z[:, u % 2, :], z_exp[:], ALU.max).then_inc(activated, 1)

            def add(u):
                dve.wait_ge(out_turned, u + 1)
                src = m.ps_score[:, 0, 0:HALF].rearrange("p (c a f) -> p c a f", c=4, a=2)
                x = m.x[:, :, u, :].rearrange("p (a c) f -> p c a f", a=2)
                link(dve.tensor_tensor(x[:, :, 0, :], x[:, :, 0, :], src[:, :, 0, :], ALU.add))
                dve.tensor_tensor(x[:, :, 1, :], x[:, :, 1, :], src[:, :, 1, :], ALU.add).then_inc(added, 1)

            for u in range(B):
                for t in range(NT):
                    mask_tile(u, t)
                    if u and t == 1:
                        dve_normalise(dve, m, a, u - 1, (u - 1) % 2)
                    if u and t == 2:
                        elu(u - 1)
                    if u and t == 4:
                        add(u - 1)
                    if t >= 2:
                        dve_copy_turned(dve, m, a, u, u % 2, t - 2)
                dve_copy_turned(dve, m, a, u, u % 2, NT - 2)
                dve_copy_turned(dve, m, a, u, u % 2, NT - 1)
                dve_inverse(dve, m, a, u, u % 2)
            dve_normalise(dve, m, a, B - 1, 1)
            elu(B - 1)
            add(B - 1)


def hypergraph_layer(nc, m, d):
    name = "hyp"
    EN = F
    with ExitStack() as ctx:
        def sb(n, shape, dt=F32):
            return ctx.enter_context(nc.sbuf_tensor(f"{name}_{n}", shape, dt))

        width = 2 * P + 2
        w = block_weights(nc, ctx, name, [
            (0, 0, d["L0_gnn_W"]), (F, F, d["L0_gnn_W"]),
            (0, P, d["L0_gnn_W_ind"]), (F, P + F, d["L0_gnn_W_ind"])], width)
        an_w = sb("an_w", [P, 2, P])
        vecs = sb("vecs", [F, 4])
        fc_w = sb("fc_w", [P, 2, P])
        fc_b = sb("fc_b", [P, 1])
        av = sb("av", [P, 1])
        ones = sb("ones", [P, P])
        members = sb("members", [P, N])
        edge_mask = sb("edge_mask", [P, N])
        node_mask = sb("node_mask", [P, NT, EN])
        linked = sb("linked", [P, NT])
        rank = sb("rank", [P, N])
        slots = sb("slots", [P, 1])
        slots_int = sb("slots_int", [P, 1], mybir.dt.int32)
        edge_rows = sb("edge_rows", [P, B, F])
        picks = sb("picks", [P, B * F + 18], F32R)
        best = sb("best", [P, NT, B])
        h1 = sb("h1", [P, NT, B, F])
        gate = sb("gate", [P, NT, B])
        coef_sum = sb("coef_sum", [P, NT, B])
        minus_one = sb("minus_one", [P, 1])
        neighbours = sb("neighbours", [P, NT, B, F])

        with ExitStack() as part:
            def psb(n, shape, dt=F32):
                return part.enter_context(nc.sbuf_tensor(f"{name}_{n}", shape, dt))

            def sem(n):
                return nc.alloc_semaphore(f"{name}_{n}")

            w_t = psb("w_t", [F, 2, F])
            member_rows = psb("member_rows", [P, NT, EN])
            member_cols = psb("member_cols", [P, N])
            counts = psb("counts", [P, NT])
            total = psb("total", [P, N])
            upper = psb("upper", [F, 2, EN])
            loaded, cleared, folded, step = sem("loaded"), sem("cleared"), sem("folded"), sem("stepa")
            counted, filled, ranked, triangle = sem("counted"), sem("filled"), sem("ranked"), sem("triangle")
            block = part.enter_context(nc.Block())

            @block.sync
            def _(sp):
                for k in range(2):
                    sp.dma_start(w_t[:, k, :], d["l0_wt"]).then_inc(loaded, 16)
                    sp.dma_start(member_cols[k * F:(k + 1) * F, :], d["h_t"]).then_inc(loaded, 16)
                sp.dma_start(vecs[:, 0:3], d["l0_vecs"]).then_inc(loaded, 16)
                sp.dma_start(member_rows[:], d["h_rows"]).then_inc(loaded, 16)
                sp.dma_start(fc_b[:], d["L0_gnn_fcb"].rearrange("(f a) -> f a", a=1)).then_inc(loaded, 16)
                sp.dma_start(av[:], d["L0_gnn_av"].rearrange("(f a) -> f a", a=1)).then_inc(loaded, 16)
                sp.wait_ge(cleared, 1)
                for k in range(2):
                    sp.dma_start(fc_w[k * F:(k + 1) * F, k, :], d["L0_gnn_fcW"]).then_inc(loaded, 16)

            @block.gpsimd
            def _(pool):
                pool.memset(upper[:], 1.0).then_inc(triangle, 1)
                pool.wait_ge(triangle, 1)
                pool.affine_select(out=upper[:], in_=upper[:], compare_op=ALU.is_gt, fill=0.0, base=0,
                                   pattern=[[0, 2], [1, EN]], channel_multiplier=-1).then_inc(triangle, 1)

            @block.tensor
            def _(pe):
                pe.wait_ge(loaded, 160)
                rows = w_t[:].rearrange("o a f -> o (a f)")
                pe.matmul(m.ps_misc[:, 0, 0:P], rows, vecs[:, 0:1].to_broadcast([F, P]),
                          start=True, stop=True)
                pe.matmul(m.ps_misc[:, 1, 0:1], rows, vecs[:, 1:2], start=True, stop=True)\
                  .then_inc(folded, 1)
                pe.wait_ge(filled, 1)
                for half in range(2):
                    cols = slice(half * HALF, (half + 1) * HALF)
                    ins = pe.matmul(m.ps_score[:, 0, cols], ones[0:EN, :], members[0:EN, cols],
                                    start=True, stop=True)
                ins.then_inc(counted, 1)
                pe.wait_ge(filled, 2)
                pe.wait_ge(triangle, 2)
                for half in range(2):
                    cols = slice(half * HALF, (half + 1) * HALF)
                    ins = pe.matmul(m.ps_score[:, 1, cols], upper[:].rearrange("p a e -> p (a e)"),
                                    rank[0:EN, cols], start=True, stop=True)
                ins.then_inc(ranked, 1)

            @block.vector
            def _(dve):
                link = Chain(dve, step)
                link(dve.memset(an_w[:], 0.0))
                link(dve.memset(ones[:], 1.0))
                link(dve.memset(fc_w[:], 0.0))
                dve.nop().then_inc(cleared, 1)
                dve.wait_ge(loaded, 160)
                dve.wait_ge(folded, 1)
                for k in range(2):
                    half = slice(k * F, (k + 1) * F)
                    dve.tensor_copy(an_w[half, k, :], m.ps_misc[half, 0, 0:P])
                    link(dve.tensor_copy(w[half, 2 * P + k:2 * P + k + 1], m.ps_misc[half, 1, 0:1]))
                link(dve.tensor_scalar(members[:], member_cols[:], 0.0, None, ALU.is_gt))
                dve.nop().then_inc(filled, 1)
                link(dve.tensor_scalar(edge_mask[:], member_cols[:], 0.0, NEG, ALU.is_le, ALU.mult))
                link(dve.tensor_scalar(node_mask[:], member_rows[:], 0.0, NEG, ALU.is_le, ALU.mult))
                link(dve.tensor_reduce(counts[:], node_mask[:], AX, ALU.max))
                link(dve.tensor_scalar(linked[:], counts[:], 0.0, None, ALU.is_equal))
                dve.wait_ge(counted, 1)
                link(dve.tensor_scalar(total[:], m.ps_score[:, 0, :], 0.0, None, ALU.is_equal))
                link(dve.tensor_tensor(rank[:], members[:], total[:], ALU.max))
                dve.nop().then_inc(filled, 1)
                link(dve.scalar_tensor_tensor(out=total[:], in0=total[:], scalar=float(EN),
                                              in1=m.ps_score[:, 0, :], op0=ALU.mult, op1=ALU.add))
                link(dve.tensor_reduce(slots[:], total[:], AX, ALU.max))
                link(dve.tensor_copy(slots_int[:], slots[:]))
                dve.wait_ge(ranked, 1)
                link(dve.scalar_tensor_tensor(out=rank[:], in0=m.ps_score[:, 1, :], scalar=1.0,
                                              in1=rank[:], op0=ALU.add, op1=ALU.mult))
                dve.tensor_scalar(rank[:], rank[:], -1.0, None, ALU.add)

        with ExitStack() as part:
            x_t = project(nc, m, part, name + "_p", w[:], width, [
                (0, P, lambda q, t: h1[:, t, 2 * q:2 * q + 2, :].rearrange("p a f -> p (a f)")),
                (P, 2 * P, lambda q, t: neighbours[:, t, 2 * q:2 * q + 2, :].rearrange("p a f -> p (a f)")),
                (2 * P, width, lambda q, t: gate[:, t, 2 * q:2 * q + 2])])

            def psb(n, shape, dt=F32):
                return part.enter_context(nc.sbuf_tensor(f"{name}_{n}", shape, dt))

            def sem(n):
                return nc.alloc_semaphore(f"{name}_{n}")

            score = psb("score", [P, 2, N])
            masked = psb("masked", [P, 2, N])
            weights = psb("weights", [P, 2, N])
            weights_t = psb("weights_t", [P, NT, P])
            neg_max, row_sum = psb("neg_max", [P, B]), psb("row_sum", [P, B])
            step, spread, copied, masked_ready, exp_ready = (
                sem("stepb"), sem("spread"), sem("copied"), sem("masked_ready"), sem("exp_ready"))
            turned = [sem("turned0"), sem("turned1")]
            turned_out = [sem("turned_out0"), sem("turned_out1")]
            summed, scaled = sem("summed"), sem("scaled")
            block = part.enter_context(nc.Block())

            @block.tensor
            def _(pe):
                def spread_scores(b):
                    if b >= 2:
                        pe.wait_ge(copied, b - 1)
                    for half in range(2):
                        cols = slice(half * HALF, (half + 1) * HALF)
                        ins = pe.matmul(m.ps_score[:, b % 2, cols], an_w[:, b % 2, :],
                                        x_t[:, b // 2, cols], start=True, stop=True)
                    ins.then_inc(spread, 1)

                spread_scores(0)
                spread_scores(1)
                for b in range(B):
                    pe.wait_ge(exp_ready, b + 1)
                    for half in range(2):
                        if b:
                            pe.wait_ge(turned_out[half], b)
                        for k in range(4):
                            t = half * 4 + k
                            ins = pe.transpose(m.ps_turn[:, half, k * P:(k + 1) * P],
                                               weights[:, b % 2, t * P:(t + 1) * P], m.ident[:])
                        ins.then_inc(turned[half], 1)
                    if b + 2 < B:
                        spread_scores(b + 2)
                    for half in range(2):
                        pe.wait_ge(turned_out[half], b + 1)
                    if b >= 2:
                        pe.wait_ge(scaled, b - 1)
                    for t in range(NT):
                        ins = pe.matmul(m.ps_misc[:, b % 2, 0:F], weights_t[:, t, :], h1[:, t, b, :],
                                        start=(t == 0), stop=(t == NT - 1))
                    ins.then_inc(summed, 1)

            @block.scalar
            def _(act):
                def copy_scores(b):
                    act.wait_ge(spread, b + 1)
                    if b >= 2:
                        act.wait_ge(masked_ready, b - 1)
                    act.copy(score[:, b % 2, :], m.ps_score[:, b % 2, :]).then_inc(copied, 1)

                copy_scores(0)
                copy_scores(1)
                for b in range(B):
                    act.wait_ge(masked_ready, b + 1)
                    if b >= 2:
                        act.wait_ge(turned[1], b - 1)
                    act.activation(weights[:, b % 2, :], masked[:, b % 2, :], ACT.Exp, scale=-1.0,
                                   bias=neg_max[:, b:b + 1], accum_out=row_sum[:, b:b + 1])\
                       .then_inc(exp_ready, 1)
                    if b + 2 < B:
                        copy_scores(b + 2)
                    act.wait_ge(turned[0], b + 1)
                    if b:
                        act.wait_ge(summed, b)
                    act.copy(weights_t[:, 0:4, :].rearrange("p k e -> p (k e)"), m.ps_turn[:, 0, :])\
                       .then_inc(turned_out[0], 1)

            @block.vector
            def _(dve):
                link = Chain(dve, step)

                def mask(b):
                    dve.wait_ge(copied, b + 1)
                    s = score[:, b % 2, :]
                    link(dve.scalar_tensor_tensor(out=s, in0=s, scalar=0.2, in1=s, op0=ALU.mult,
                                                  op1=ALU.max))
                    if b >= 2:
                        dve.wait_ge(exp_ready, b - 1)
                    dve.tensor_tensor_reduce(masked[:, b % 2, :], s, edge_mask[:], -1.0, HUGE, ALU.add,
                                             ALU.min, neg_max[:, b:b + 1]).then_inc(masked_ready, 1)

                mask(0)
                for b in range(B):
                    if b + 1 < B:
                        mask(b + 1)
                    dve.wait_ge(turned[1], b + 1)
                    if b:
                        dve.wait_ge(summed, b)
                    dve.tensor_copy(weights_t[:, 4:8, :].rearrange("p k e -> p (k e)"),
                                    m.ps_turn[:, 1, :]).then_inc(turned_out[1], 1)
                    dve.wait_ge(exp_ready, b + 1)
                    link(dve.reciprocal(row_sum[:, b:b + 1], row_sum[:, b:b + 1]))
                    dve.wait_ge(summed, b + 1)
                    dve.tensor_scalar(edge_rows[:, b, :], m.ps_misc[:, b % 2, 0:F],
                                      row_sum[:, b:b + 1], None, ALU.mult).then_inc(scaled, 1)

        with ExitStack() as part:
            def psb(n, shape, dt=F32):
                return part.enter_context(nc.sbuf_tensor(f"{name}_{n}", shape, dt))

            def sem(n):
                return nc.alloc_semaphore(f"{name}_{n}")

            elus = psb("elus", [P, B, F])
            elus_t = psb("elus_t", [F, B, P])
            rows_t = psb("rows_t", [F, B, P])
            hidden = psb("hidden", [P, B, P])
            pick_hi = psb("pick_hi", [P, B * F + 18], F32R)
            pick_all = psb("pick_all", [P, B * F + 18])
            table = psb("table", [P, NT, B, EN])
            step, exped, elued, turned, copied = (
                sem("stepc"), sem("exped"), sem("elued"), sem("turned_c"), sem("copied_c"))
            hidden_ready, tanh_ready, scored, collected, rounded = (
                sem("hidden_ready"), sem("tanh_ready"), sem("scored"), sem("collected"), sem("rounded_c"))
            block = part.enter_context(nc.Block())
            flat = edge_rows[:].rearrange("p b f -> p (b f)")

            @block.scalar
            def _(act):
                act.activation(elus[:], edge_rows[:], ACT.Exp).then_inc(exped, 1)
                for half in range(2):
                    act.wait_ge(hidden_ready, half + 1)
                    act.activation(hidden[:, 4 * half:4 * half + 4, :],
                                   m.ps_misc[:, half, :].rearrange("p (b e) -> p b e", b=4),
                                   ACT.Tanh, bias=fc_b[:, 0:1]).then_inc(tanh_ready, 1)
                act.wait_ge(collected, 1)
                act.copy(pick_hi[:], pick_all[:]).then_inc(rounded, 1)
                act.copy(picks[0:F, :], pick_all[0:F, :])

            @block.tensor
            def _(pe):
                for b in range(B):
                    pe.transpose(m.ps_score[0:F, b // 4, (b % 4) * P:(b % 4 + 1) * P],
                                 edge_rows[:, b, :], m.ident[:])
                pe.wait_ge(elued, 1)
                for b in range(B):
                    ins = pe.transpose(m.ps_score[0:F, b // 4, HALF + (b % 4) * P:HALF + (b % 4 + 1) * P],
                                       elus[:, b, :], m.ident[:])
                ins.then_inc(turned, 1)
                pe.wait_ge(copied, 2)
                for half in range(2):
                    pe.matmul(m.ps_misc[:, half, :], fc_w[0:F, 0, :],
                              elus_t[:, 4 * half:4 * half + 4, :].rearrange("p b e -> p (b e)"),
                              start=True, stop=True).then_inc(hidden_ready, 1)
                pe.wait_ge(tanh_ready, 2)
                for b in range(B):
                    pe.matmul(m.ps_turn[:, 0, b:b + 1], hidden[:, b, :], av[:], start=True, stop=True)
                    pe.matmul(m.ps_turn[:, 0, B + b:B + b + 1], rows_t[:, b, :], vecs[:, 2:3],
                              start=True, stop=True)
                pe.matmul(m.ps_turn[:, 1, :].rearrange("p (b e) -> p b e", b=B), av[:].to_broadcast([P, P]), hidden[:, :, 0:EN],
                          start=True, stop=True).then_inc(scored, 1)

            @block.vector
            def _(dve):
                link = Chain(dve, step)
                dve.wait_ge(exped, 1)
                link(dve.tensor_scalar(elus[:], elus[:], 1.0, -1.0, ALU.min, ALU.add))
                dve.tensor_tensor(elus[:], elus[:], edge_rows[:], ALU.max).then_inc(elued, 1)
                dve.wait_ge(turned, 1)
                dve.tensor_copy(rows_t[:].rearrange("p (a b) e -> p a (b e)", a=2),
                                m.ps_score[0:F, :, 0:HALF]).then_inc(copied, 1)
                dve.tensor_copy(elus_t[:].rearrange("p (a b) e -> p a (b e)", a=2),
                                m.ps_score[0:F, :, HALF:N]).then_inc(copied, 1)
                dve.wait_ge(scored, 1)
                link(dve.tensor_copy(pick_all[:, 0:B * F], flat))
                link(dve.tensor_copy(pick_all[:, B * F:B * F + 16], m.ps_turn[:, 0, 0:16]))
                link(dve.memset(pick_all[:, B * F + 16:], 1.0))
                dve.nop().then_inc(collected, 1)
                dve.wait_ge(rounded, 1)
                dve.tensor_tensor(picks[F:P, :], pick_all[F:P, :], pick_hi[F:P, :], ALU.subtract)
                edge_scores = m.ps_turn[:, 1, :].rearrange("p (b e) -> p b e", b=B)
                for t in range(NT):
                    ins = dve.tensor_tensor(table[:, t, :, :], edge_scores,
                                            node_mask[:, t, :].unsqueeze(1).to_broadcast([P, B, EN]),
                                            ALU.add)
                link(ins)
                dve.tensor_reduce(best[:], table[:], AX, ALU.max)

        with ExitStack() as part:
            def psb(n, shape, dt=F32):
                return part.enter_context(nc.sbuf_tensor(f"{name}_{n}", shape, dt))

            def sem(n):
                return nc.alloc_semaphore(f"{name}_{n}")

            pick = psb("pick", [P, N], F32R)
            beta = psb("beta", [P, NT, B])
            coef = psb("coef", [P, NT, B])
            diff = psb("diff", [P, 2, B * F])
            blend = psb("blend", [P, 2, B * F])
            blend_exp = psb("blend_exp", [P, 2, B * F])
            share = psb("share", [P, 2, B * F])
            step, picked, small_ready, rows_ready, rows_taken = (
                sem("stepd"), sem("picked"), sem("small_ready"), sem("rows_ready"), sem("rows_taken"))
            maxed = sem("maxed")
            exp_asked, exp_ready, blend_ready, blend_exped, share_ready, share_added = (
                sem("exp_asked"), sem("exp_ready_d"), sem("blend_ready"), sem("blend_exped"),
                sem("share_ready"), sem("share_added"))
            small = m.ps_misc[:, 0, 0:NT * 18].rearrange("p (t c) -> p t c", t=NT)
            block = part.enter_context(nc.Block())

            def slot_count(eng):
                return eng.value_load(slots_int[0:1, 0:1], min_val=1, max_val=EN)

            @block.tensor
            def _(pe):
                with pe.Fori(0, slot_count(pe)) as k:
                    pe.wait_ge(picked, k + 1)
                    for t in range(NT):
                        ins = pe.matmul(m.ps_misc[:, 0, t * 18:(t + 1) * 18], pick[:, t * P:(t + 1) * P],
                                        picks[:, B * F:], start=True, stop=True)
                    ins.then_inc(small_ready, 1)
                    for t in range(NT):
                        pe.wait_ge(rows_taken, k * NT + 1 + max(t - 3, 0))
                        pe.matmul(m.ps_score[:, t % 4 // 2, (t % 2) * HALF:(t % 2 + 1) * HALF],
                                  pick[:, t * P:(t + 1) * P], picks[:, 0:B * F],
                                  start=True, stop=True).then_inc(rows_ready, 1)

            @block.scalar
            def _(act):
                with act.Fori(0, slot_count(act)) as k:
                    act.wait_ge(exp_asked, 2 * k + 1)
                    act.activation(coef[:], coef[:], ACT.Exp).then_inc(exp_ready, 1)
                    act.wait_ge(exp_asked, 2 * k + 2)
                    act.activation(beta[:], beta[:], ACT.Exp, scale=-1.0).then_inc(exp_ready, 1)
                    for t in range(NT):
                        act.wait_ge(blend_ready, k * NT + t + 1)
                        act.activation(blend_exp[:, t % 2, :], blend[:, t % 2, :], ACT.Exp,
                                       bias=minus_one[:, 0:1]).then_inc(blend_exped, 1)

            @block.gpsimd
            def _(pool):
                rows = m.h[:].rearrange("p t b f -> p t (b f)")
                pool.wait_ge(step, 2)
                pool.nop().then_inc(share_added, 1)
                with pool.Fori(0, slot_count(pool)) as k:
                    for t in range(NT):
                        pool.wait_ge(share_ready, k * NT + t + 1)
                        pool.tensor_tensor(rows[:, t, :], rows[:, t, :], share[:, t % 2, :], ALU.add)\
                            .then_inc(share_added, 1)

            @block.vector
            def _(dve):
                dve.memset(minus_one[:], -1.0).then_inc(step, 1)
                dve.memset(m.h[:], 0.0).then_inc(step, 1)
                dve.memset(coef_sum[:], 0.0).then_inc(step, 1)
                dve.wait_ge(step, 3)
                dve.nop().then_inc(rows_taken, 1)
                steps = 6 + 2 * NT

                with dve.Fori(0, slot_count(dve)) as k:
                    link = Chain(dve, step, 3 + k * steps)
                    dve.tensor_scalar(pick[:], rank[:], 0.0, None, ALU.is_equal).then_inc(picked, 1)
                    dve.wait_ge(picked, k + 1)
                    link(dve.tensor_scalar(rank[:], rank[:], -1.0, None, ALU.add))
                    dve.wait_ge(small_ready, k + 1)
                    link(dve.tensor_tensor(coef[:], small[:, :, 0:B], best[:], ALU.subtract))
                    dve.scalar_tensor_tensor(out=coef[:], in0=coef[:], scalar=0.0,
                                             in1=linked[:].unsqueeze(2).to_broadcast([P, NT, B]),
                                             op0=ALU.min, op1=ALU.mult).then_inc(exp_asked, 1)
                    dve.tensor_tensor(beta[:], small[:, :, B:2 * B], gate[:], ALU.add).then_inc(exp_asked, 1)
                    dve.wait_ge(exp_ready, 2 * k + 1)
                    link(dve.tensor_tensor(coef[:], coef[:], small[:, :, 16:17].to_broadcast([P, NT, B]),
                                           ALU.mult))
                    link(dve.tensor_tensor(coef_sum[:], coef_sum[:], coef[:], ALU.add))
                    dve.wait_ge(exp_ready, 2 * k + 2)
                    link(dve.tensor_scalar(beta[:], beta[:], 1.0, None, ALU.add))
                    link(dve.reciprocal(beta[:], beta[:]))

                    def along(v, t):
                        return v[:, t, :].unsqueeze(2).to_broadcast([P, B, F])

                    def by_batch(v):
                        return v.rearrange("p (b f) -> p b f", b=B)

                    def blend_rows(t):
                        dve.wait_ge(rows_ready, k * NT + t + 1)
                        row = m.ps_score[:, t % 4 // 2, (t % 2) * HALF:(t % 2 + 1) * HALF]
                        d2 = diff[:, t % 2, :]
                        link(dve.tensor_tensor(d2, h1[:, t, :, :].rearrange("p b f -> p (b f)"), row,
                                               ALU.subtract))
                        link(dve.tensor_tensor(by_batch(d2), by_batch(d2), along(beta, t), ALU.mult))
                        dve.scalar_tensor_tensor(out=blend[:, t % 2, :], in0=row, scalar=1.0, in1=d2,
                                                 op0=ALU.add, op1=ALU.add).then_inc(blend_ready, 1)
                        dve.wait_ge(blend_ready, k * NT + t + 1)
                        dve.nop().then_inc(rows_taken, 1)

                    def add_share(t):
                        dve.wait_ge(blend_exped, k * NT + t + 1)
                        s = share[:, t % 2, :]
                        dve.wait_ge(share_added, k * NT + 1 + max(t - 1, 0))
                        dve.scalar_tensor_tensor(out=s, in0=blend_exp[:, t % 2, :], scalar=1.0,
                                                 in1=blend[:, t % 2, :], op0=ALU.min,
                                                 op1=ALU.max).then_inc(maxed, 1)
                        dve.wait_ge(maxed, k * NT + t + 1)
                        dve.tensor_tensor(by_batch(s), by_batch(s), along(coef, t), ALU.mult)\
                           .then_inc(share_ready, 1)

                    blend_rows(0)
                    for t in range(NT):
                        if t + 1 < NT:
                            blend_rows(t + 1)
                        add_share(t)

        with ExitStack() as part:
            def divide(dve, t, ps):
                return dve.tensor_scalar(neighbours[:, t, :, :].rearrange("p b f -> p (b f)"), ps,
                                         m.deg_inv[:, t:t + 1], None, ALU.mult)

            mix(nc, m, part, name + "_m", lambda t: neighbours[:, t, :, :].rearrange("p b f -> p (b f)"),
                divide)
        mix_pair(nc, m, name, neighbours, coef_sum, fc_w, fc_b, av)


def mix_pair(nc, m, name, neighbours, coef_sum, fc_w, fc_b, av):
    with ExitStack() as ctx:
        def sb(n, shape, dt=F32):
            return ctx.enter_context(nc.sbuf_tensor(f"{name}_{n}", shape, dt))

        def sem(n):
            return nc.alloc_semaphore(f"{name}_{n}")

        turned = sb("pair_t", [P, 2, 2, N])
        tanhs = sb("tanhs", [P, 2, 2, N])
        apart = sb("apart", [P, 2, N])
        first = sb("first", [P, NT, B])
        step, ready, turned_out, turned_in = sem("stepe"), sem("pair_ready"), sem("pair_out"), sem("pair_in")
        hid, tanhed, parted, scored, exped = (
            sem("pair_hid"), sem("pair_tanh"), sem("pair_apart"), sem("pair_scored"), sem("pair_exp"))
        sources = (neighbours, m.h)
        block = ctx.enter_context(nc.Block())

        @block.tensor
        def _(pe):
            pe.wait_ge(ready, 1)
            scores = m.ps_misc[:, 0, 0:NT * B].rearrange("p (t b) -> p t b", b=B)

            def score(b):
                pe.wait_ge(parted, b + 1)
                for t in range(NT):
                    ins = pe.matmul(scores[:, t, b:b + 1], apart[:, b % 2, t * P:(t + 1) * P], av[:],
                                    start=True, stop=True)
                ins.then_inc(scored, 1)

            for b in range(B):
                q = b // 2
                for s in range(2):
                    u = 2 * b + s
                    if b % 2 == 0:
                        for half in range(2):
                            i = 2 * (2 * q + s) + half
                            if i:
                                pe.wait_ge(turned_in, i)
                            for k in range(4):
                                t = half * 4 + k
                                ins = pe.transpose(m.ps_turn[:, 0, k * P:(k + 1) * P],
                                                   sources[s][:, t, 2 * q:2 * q + 2, :]
                                                   .rearrange("p a f -> p (a f)"), m.ident[:])
                            ins.then_inc(turned_out, 1)
                        pe.wait_ge(turned_in, 4 * q + 2 * s + 2)
                    if u >= 2:
                        pe.wait_ge(tanhed, u - 1)
                    for half in range(2):
                        cols = slice(half * HALF, (half + 1) * HALF)
                        ins = pe.matmul(m.ps_score[:, s, cols], fc_w[:, b % 2, :],
                                        turned[:, q % 2, s, cols], start=True, stop=True)
                    ins.then_inc(hid, 1)
                if b:
                    score(b - 1)
            score(B - 1)

        @block.scalar
        def _(act):
            for b in range(B):
                for s in range(2):
                    act.wait_ge(hid, 2 * b + s + 1)
                    if b >= 2:
                        act.wait_ge(parted, b - 1)
                    act.activation(tanhs[:, b % 2, s, :], m.ps_score[:, s, :], ACT.Tanh,
                                   bias=fc_b[:, 0:1]).then_inc(tanhed, 1)
            act.wait_ge(step, 4)
            act.activation(first[:], first[:], ACT.Exp, scale=-1.0).then_inc(exped, 1)

        @block.vector
        def _(dve):
            link = Chain(dve, step)
            link(dve.reciprocal(coef_sum[:], coef_sum[:]))
            h = m.h[:]
            link(dve.tensor_tensor(h, h, coef_sum[:].unsqueeze(3).to_broadcast([P, NT, B, F]), ALU.mult))
            link(dve.tensor_scalar(h, h, -1.0, None, ALU.add))
            dve.nop().then_inc(ready, 1)
            for b in range(B):
                if b % 2 == 0:
                    for i in range(4):
                        s, half = i // 2, i % 2
                        dve.wait_ge(turned_out, 2 * b + i + 1)
                        if b >= 4:
                            dve.wait_ge(hid, 2 * b - 4)
                        dve.tensor_copy(turned[:, b // 2 % 2, s, half * HALF:(half + 1) * HALF],
                                        m.ps_turn[:, 0, :]).then_inc(turned_in, 1)
                dve.wait_ge(tanhed, 2 * b + 2)
                if b >= 2:
                    dve.wait_ge(scored, b - 1)
                dve.tensor_tensor(apart[:, b % 2, :], tanhs[:, b % 2, 0, :], tanhs[:, b % 2, 1, :],
                                  ALU.subtract).then_inc(parted, 1)
            dve.wait_ge(scored, B)
            link(dve.tensor_copy(first[:].rearrange("p t b -> p (t b)"), m.ps_misc[:, 0, 0:NT * B]))
            link(dve.tensor_tensor(neighbours[:], neighbours[:], h, ALU.subtract))
            dve.wait_ge(exped, 1)
            link(dve.tensor_scalar(first[:], first[:], 1.0, None, ALU.add))
            link(dve.reciprocal(first[:], first[:]))
            link(dve.tensor_tensor(neighbours[:], neighbours[:],
                                   first[:].unsqueeze(3).to_broadcast([P, NT, B, F]), ALU.mult))
            link(dve.tensor_tensor(neighbours[:], neighbours[:], h, ALU.add))
            dve.tensor_tensor(m.x[:], m.x[:], neighbours[:], ALU.add)


def load(nc, m, d):
    with ExitStack() as ctx:
        adj = ctx.enter_context(nc.sbuf_tensor("adj_rows", [P, NT, N], F32))
        adj_cols = ctx.enter_context(nc.sbuf_tensor("adj_cols", [P, 2, N], F32))
        x_loaded = nc.alloc_semaphore("x_loaded")
        adj_loaded = [nc.alloc_semaphore(f"adj_loaded{t}") for t in range(NT)]
        cols_loaded = [nc.alloc_semaphore(f"cols_loaded{i}") for i in range(2)]
        cols_copied = nc.alloc_semaphore("cols_copied")
        zeroed = nc.alloc_semaphore("zeroed")
        summed = nc.alloc_semaphore("summed")
        block = ctx.enter_context(nc.Block())

        @block.sync
        def _(sp):
            sp.dma_start(m.x[:], d["x"]).then_inc(x_loaded, 16)
            for t in range(NT):
                sp.dma_start(adj[:, t, :], d["adj"][t * P:(t + 1) * P, :]).then_inc(adj_loaded[t], 16)
            sp.wait_ge(x_loaded, 16)

        @block.scalar
        def _(act):
            for t in range(NT):
                if t >= 2:
                    act.wait_ge(cols_copied, t - 1)
                act.dma_start(adj_cols[:, t % 2, :], d["adj_t"][t * P:(t + 1) * P, :])\
                   .then_inc(cols_loaded[t % 2], 16)
                act.wait_ge(cols_loaded[t % 2], 16 * (t // 2 + 1))
                act.copy(m.adj_t[:, t, :], adj_cols[:, t % 2, :]).then_inc(cols_copied, 1)

        @block.gpsimd
        def _(pool):
            pool.memset(m.ident[:], 0.0).then_inc(zeroed, 1)
            pool.wait_ge(zeroed, 1)
            pool.affine_select(out=m.ident[:], in_=m.ident[:], compare_op=ALU.not_equal, fill=1.0,
                               base=0, pattern=[[-1, P]], channel_multiplier=1)

        @block.vector
        def _(dve):
            for t in range(NT):
                dve.wait_ge(adj_loaded[t], 16)
                dve.tensor_scalar(m.mask[:, t, :], adj[:, t, :], 0.0, NEG, ALU.is_le, ALU.mult)
                dve.tensor_reduce(m.deg_inv[:, t:t + 1], adj[:, t, :], AX, ALU.add).then_inc(summed, 1)
            dve.wait_ge(summed, NT)
            dve.tensor_scalar(m.deg_inv[:], m.deg_inv[:], 1.0, None, ALU.max).then_inc(summed, 1)
            dve.wait_ge(summed, NT + 1)
            dve.reciprocal(m.deg_inv[:], m.deg_inv[:])


def store(nc, m, d):
    with ExitStack() as ctx:
        stored = nc.alloc_semaphore("stored")
        block = ctx.enter_context(nc.Block())

        @block.sync
        def _(sp):
            sp.dma_start(d["out"], m.x[:]).then_inc(stored, 16)
            sp.wait_ge(stored, 16)


def four_layers(nc, d, stages=None):
    with ExitStack() as ctx:
        m = Mem()

        def sb(n, shape, dt=F32):
            return ctx.enter_context(nc.sbuf_tensor(n, shape, dt))

        m.x = sb("x_sb", [P, NT, B, F])
        m.h = sb("h_sb", [P, NT, B, F])
        m.mask = sb("adj_mask", [P, NT, N], BF16)
        m.deg_inv = sb("deg_inv", [P, NT])
        m.ident = sb("ident", [P, P])
        m.ps_score = ctx.enter_context(nc.psum_tensor("ps_score", [P, 2, N], F32))
        m.ps_turn = ctx.enter_context(nc.psum_tensor("ps_turn", [P, 2, HALF], F32))
        m.ps_misc = ctx.enter_context(nc.psum_tensor("ps_misc", [P, 2, HALF], F32))
        with ExitStack() as graph:
            m.adj_t = graph.enter_context(nc.sbuf_tensor("adj_t_sb", [P, NT, N], F32R))
            with fresh_semaphores(nc):
                load(nc, m, d)
            for k, layer in enumerate((hypergraph_layer, graph_attention_layer, graph_layer)):
                if stages is None or k in stages:
                    with fresh_semaphores(nc):
                        layer_norm(nc, m, f"ln{k}")
                        layer(nc, m, d)
        if stages is None or 3 in stages:
            with ExitStack() as last:
                m.h2t = last.enter_context(nc.sbuf_tensor("h2t_sb", [P, B, HALF], F32))
                with fresh_semaphores(nc):
                    layer_norm(nc, m, "ln3")
                    hidden_attention(nc, m, d)
                with fresh_semaphores(nc):
                    out_attention(nc, m, d)
        store(nc, m, d)


_SHAPES = {
    "x": (P, NT, B, F), "adj": (N, N), "adj_t": (N, N), "wh_t": (HEADS, HID, F),
    "L3_gnn_Wh": (HEADS, F, HID), "L3_gnn_W_out": (HEADS * HID, F), "bh_t": (HID, HEADS),
    "L3_gnn_b_out": (F,), "L2_w": (2, F, F), "L1_gnn_W": (F, F), "l1_wt": (F, F),
    "l1_a": (F, 2), "h_rows": (P, NT, F), "h_t": (F, N), "L0_gnn_W": (F, F),
    "l0_wt": (F, F), "L0_gnn_W_ind": (F, F), "l0_vecs": (F, 3),
    "L0_gnn_fcW": (F, 2 * F), "L0_gnn_fcb": (2 * F,), "L0_gnn_av": (2 * F,),
}


def lay_out(inputs, np):
    v = {k: np.asarray(a) for k, a in inputs.items()}
    v["x"] = v["x"].reshape(B, NT, P, F).transpose(2, 1, 0, 3)
    v["adj_t"] = v["adj"].T
    v["wh_t"] = v["L3_gnn_Wh"].transpose(0, 2, 1)
    v["L2_w"] = v["L2_gnn_net_params"].reshape(2, F, F)
    v["l1_wt"] = v["L1_gnn_W"].T
    v["l1_a"] = v["L1_gnn_a"].reshape(2, F).T
    v["l0_wt"] = v["L0_gnn_W"].T
    v["bh_t"] = v["L3_gnn_bh"].T
    v["h_rows"] = v["L0_gnn_H"].reshape(NT, P, F).transpose(1, 0, 2)
    v["l0_vecs"] = np.stack([v["L0_gnn_a_node"], v["L0_gnn_a_gn"], v["L0_gnn_a_ge"]], axis=1)
    v["h_t"] = v["L0_gnn_H"].T
    return {k: np.ascontiguousarray(v[k]) for k in _SHAPES}


def kernel(**inputs):
    import numpy as np
    import concourse.bacc as bacc
    from concourse.bass_utils import run_bass_kernel_spmd

    arrays = {f"in_{k}": a for k, a in lay_out(inputs, np).items()}
    nc = bacc.Bacc("TRN2", target_bir_lowering=False, num_devices=1)
    d = {k: nc.dram_tensor(f"in_{k}", shape, F32, kind="ExternalInput").ap()
         for k, shape in _SHAPES.items()}
    d["out"] = nc.dram_tensor("out_x", (P, NT, B, F), F32, kind="ExternalOutput").ap()
    four_layers(nc, d)
    result = run_bass_kernel_spmd(nc, [arrays], core_ids=[0])
    out = np.asarray(result.results[0]["out_x"])
    return np.ascontiguousarray(out.transpose(2, 1, 0, 3)).reshape(B, N, F)
```

```python
from contextlib import ExitStack, contextmanager

import concourse.bass as bass
from concourse import mybir

ALU = mybir.AluOpType
ACT = mybir.ActivationFunctionType
F32 = mybir.dt.float32
F32R = mybir.dt.float32r
BF16 = mybir.dt.bfloat16
AX = mybir.AxisListType.X

P = 128
B, N, F = 8, 1024, 64
NT = N // P
HALF = N // 2
QUARTER = N // 4
HEADS, HID = 8, 128
NEG = -2.0 ** 53
HUGE = 3.0e38
EPS = 1.0e-5


class Chain:

    def __init__(self, eng, sem, base=0):
        self.eng, self.sem, self.base, self.n = eng, sem, base, 0

    def __call__(self, ins):
        self.n += 1
        ins.then_inc(self.sem, 1)
        self.eng.wait_ge(self.sem, self.base + self.n)


@contextmanager
def fresh_semaphores(nc):
    before = nc.snapshot_sems()
    yield
    nc.clear_and_free_semaphores(nc.allocated_since(before))
    nc.all_engine_barrier()


class Mem:
    pass


def layer_norm(nc, m, name):
    with ExitStack() as ctx:
        rows = B * NT
        mean = ctx.enter_context(nc.sbuf_tensor(name + "_mean", [P, rows], F32))
        var = ctx.enter_context(nc.sbuf_tensor(name + "_var", [P, rows], F32))
        sq = ctx.enter_context(nc.sbuf_tensor(name + "_sq", [P, rows, F], F32))
        step = nc.alloc_semaphore(name + "_step")
        centred = nc.alloc_semaphore(name + "_centred")
        squared = nc.alloc_semaphore(name + "_squared")
        var_ready = nc.alloc_semaphore(name + "_var_ready")
        std_ready = nc.alloc_semaphore(name + "_std_ready")
        x = m.x[:].rearrange("p t b f -> p (t b) f")
        h = m.h[:].rearrange("p t b f -> p (t b) f")
        parts = 4
        rp = rows // parts
        block = ctx.enter_context(nc.Block())

        @block.vector
        def _(dve):
            link = Chain(dve, step)
            for q in range(parts):
                r = slice(q * rp, (q + 1) * rp)
                link(dve.tensor_reduce(mean[:, r], x[:, r, :], AX, ALU.add))
                link(dve.tensor_scalar(mean[:, r], mean[:, r], 1.0 / F, None, ALU.mult))
                dve.tensor_tensor(h[:, r, :], x[:, r, :],
                                  mean[:, r].unsqueeze(2).to_broadcast([P, rp, F]),
                                  ALU.subtract).then_inc(centred, 1)
            for q in range(parts):
                r = slice(q * rp, (q + 1) * rp)
                dve.wait_ge(squared, q + 1)
                ins = dve.tensor_reduce(var[:, r], sq[:, r, :], AX, ALU.add)
                link(ins)
            dve.tensor_scalar(var[:], var[:], 1.0 / F, EPS, ALU.mult, ALU.add).then_inc(var_ready, 1)
            dve.wait_ge(std_ready, 1)
            link(dve.reciprocal(var[:], var[:]))
            dve.wait_ge(centred, parts)
            dve.scalar_tensor_tensor(out=h, in0=h, scalar=0.0,
                                     in1=var[:].unsqueeze(2).to_broadcast([P, rows, F]),
                                     op0=ALU.max, op1=ALU.mult)

        @block.scalar
        def _(act):
            for q in range(parts):
                r = slice(q * rp, (q + 1) * rp)
                act.wait_ge(centred, q + 1)
                act.activation(sq[:, r, :], h[:, r, :], ACT.Square).then_inc(squared, 1)
            act.wait_ge(var_ready, 1)
            act.activation(var[:], var[:], ACT.Sqrt).then_inc(std_ready, 1)


def attention_pipeline(nc, m, ctx, name):
    a = Mem()

    def sb(n, shape, dt=F32):
        return ctx.enter_context(nc.sbuf_tensor(f"{name}_{n}", shape, dt))

    def sem(n):
        return nc.alloc_semaphore(f"{name}_{n}")

    a.masked = sb("masked", [P, 2, N])
    a.weights = sb("weights", [P, 3, N])
    a.weights_t = sb("weights_t", [P, NT, N])
    a.neg_max = sb("neg_max", [P, 2, NT])
    a.row_sum = sb("row_sum", [P, 2, NT])
    a.row_inv = sb("row_inv", [P, 2, NT])
    a.inv_cols = sb("inv_cols", [P, HALF])
    a.z = sb("z", [P, 2, HALF])
    a.scores_ready = sem("scores_ready")
    a.tile_free = sem("tile_free")
    a.masked_ready = sem("masked_ready")
    a.exp_ready = sem("exp_ready")
    a.turned = [sem("turned0"), sem("turned1")]
    a.copied = [sem("copied0"), sem("copied1")]
    a.inv_ready = sem("inv_ready")
    a.inv_turned = sem("inv_turned")
    a.inv_copied = sem("inv_copied")
    a.z_ready = sem("z_ready")
    a.z_normed = sem("z_normed")
    return a



def pe_turn(pe, m, a, g, t, first):
    pe.wait_ge(a.exp_ready, g * NT + t + 1)
    for half in range(2):
        if not (first and t == 0):
            pe.wait_ge(a.copied[half], g * NT + t)
        for k in range(4):
            j = half * 4 + k
            ins = pe.transpose(m.ps_turn[:, half, k * P:(k + 1) * P],
                               a.weights[:, t % 3, j * P:(j + 1) * P], m.ident[:])
        ins.then_inc(a.turned[half], 1)


def pe_inverse_rows(pe, m, a, g, par):
    pe.wait_ge(a.inv_ready, g + 1)
    for t in range(NT):
        side, col = t // 2 % 2, t // 4 * QUARTER + t % 2 * P
        ins = pe.matmul(m.ps_misc[side * F:(side + 1) * F, 1, col:col + P],
                        a.row_inv[:, par, t:t + 1].to_broadcast([P, F]), m.ident[:],
                        start=True, stop=True)
    ins.then_inc(a.inv_turned, 1)


def pe_values(pe, m, a, g, half, js, values):
    if js[0] == 0:
        for copied in a.copied:
            pe.wait_ge(copied, g * NT + 4 * half + 4)
    for j in js:
        for side in range(2):
            i = half * HALF + side * QUARTER
            ins = pe.matmul(m.ps_misc[side * F:(side + 1) * F, 0, half * QUARTER:(half + 1) * QUARTER],
                            values(j), a.weights_t[:, j, i:i + QUARTER],
                            start=(j == 0), stop=(j == NT - 1))
    if half == 1 and js[-1] == NT - 1:
        ins.then_inc(a.z_ready, 1)


def z_rows(v, side):
    return v.rearrange("p (h s r) f -> p s h r f", h=2, s=2)[:, side, :, :, :]


def turned_rows(ps, side):
    return ps.rearrange("p (h r s f) -> p s h r f", h=2, r=2, s=2)[:, side, :, :, :]


def dve_mask(dve, m, a, g, par, t, scores, mask, first, alone=False):
    dve.wait_ge(a.scores_ready, g * NT + t + 1)
    if not (first and t < 2):
        dve.wait_ge(a.exp_ready, g * NT + t - 1)
    if alone:
        dve.nop().then_inc(a.tile_free, 1)
    dve.tensor_tensor_reduce(a.masked[:, t % 2, :], scores, mask, -1.0, HUGE, ALU.add, ALU.min,
                             a.neg_max[:, par, t:t + 1]).then_inc(a.masked_ready, 1)


def dve_copy_turned(dve, m, a, g, t):
    dve.wait_ge(a.turned[1], g * NT + t + 1)
    dve.tensor_copy(a.weights_t[:, 4:8, t * P:(t + 1) * P],
                    m.ps_turn[:, 1, :].rearrange("p (k i) -> p k i", k=4)).then_inc(a.copied[1], 1)


def dve_inverse(dve, m, a, g, par):
    dve.wait_ge(a.exp_ready, g * NT + NT)
    dve.reciprocal(a.row_inv[:, par, :], a.row_sum[:, par, :]).then_inc(a.inv_ready, 1)


def dve_normalise(dve, m, a, g, par):
    dve.wait_ge(a.z_ready, g + 1)
    dve.wait_ge(a.inv_copied, g + 1)
    dve.tensor_tensor(a.z[:, par, :], m.ps_misc[:, 0, :], a.inv_cols[:], ALU.mult)\
       .then_inc(a.z_normed, 1)


def act_exp(act, m, a, g, par, t, first):
    act.wait_ge(a.masked_ready, g * NT + t + 1)
    if not (first and t < 3):
        act.wait_ge(a.turned[1], g * NT + t - 2)
    act.activation(a.weights[:, t % 3, :], a.masked[:, t % 2, :], ACT.Exp, scale=-1.0,
                   bias=a.neg_max[:, par, t:t + 1],
                   accum_out=a.row_sum[:, par, t:t + 1]).then_inc(a.exp_ready, 1)


def act_copy_turned(act, m, a, g, t):
    act.wait_ge(a.turned[0], g * NT + t + 1)
    act.copy(a.weights_t[:, 0:4, t * P:(t + 1) * P],
             m.ps_turn[:, 0, :].rearrange("p (k i) -> p k i", k=4)).then_inc(a.copied[0], 1)


def act_copy_inverse(act, m, a, g, par):
    act.wait_ge(a.inv_turned, g + 1)
    act.copy(a.inv_cols[:], m.ps_misc[:, 1, :]).then_inc(a.inv_copied, 1)


def split(nc, ctx, name, shape):
    return (ctx.enter_context(nc.sbuf_tensor(name + "_hi", shape, F32R)),
            ctx.enter_context(nc.sbuf_tensor(name + "_lo", shape, F32R)))


def hidden_attention(nc, m, d):
    name = "hid"
    UNITS = 2 * HEADS

    with ExitStack() as ctx:
        a = attention_pipeline(nc, m, ctx, name)

        def sb(n, shape, dt=F32):
            return ctx.enter_context(nc.sbuf_tensor(f"{name}_{n}", shape, dt))

        def sem(n):
            return nc.alloc_semaphore(f"{name}_{n}")

        wh_t = sb("wh_t", [HID, HEADS, 2, F])
        gram = split(nc, ctx, name + "_gram", [P, HEADS, P])
        wz = sb("wz", [P, 2, HEADS, HID])
        wo = sb("wo", [HID, HEADS, F])
        bias = sb("bias", [HID, HEADS])
        x2 = sb("x2", [P, 2, NT, 2, F])
        xs = sb("xs", [P, 2, N], F32R)
        mask = sb("mask", [P, 2, NT, N], BF16)
        y = [split(nc, ctx, f"{name}_y{i}", [P, N]) for i in range(2)]
        ones = sb("ones", [P, P], F32R)
        zero_row = sb("zero_row", [P, NT])
        scratch = sb("scratch", [P, N], F32R)
        hidden = sb("hidden", [P, N])

        loaded = sem("loaded")
        cleared = sem("cleared")
        gram_ready = sem("gram_ready")
        gram_hi = sem("gram_hi")
        gram_split = sem("gram_split")
        staged = sem("staged")
        x_turned = sem("x_turned")
        x_hi_ready = sem("x_hi_ready")
        x_split = sem("x_split")
        sums_ready = sem("sums_ready")
        zeros_ready = sem("zeros_ready")
        mask_ready = sem("mask_ready")
        step = sem("step")
        y_ready = sem("y_ready")
        y_hi = sem("y_hi")
        y_split = sem("y_split")
        hidden_ready = sem("hidden_ready")
        hidden_biased = sem("hidden_biased")
        hidden_done = sem("hidden_done")
        out_ready = sem("out_ready")
        out_added = sem("out_added")

        block = ctx.enter_context(nc.Block())

        @block.sync
        def _(sp):
            for k in range(2):
                sp.dma_start(wh_t[:, :, k, :], d["wh_t"].rearrange("h d f -> d h f")).then_inc(loaded, 16)
            sp.wait_ge(cleared, 1)
            for k in range(2):
                sp.dma_start(wz[k * F:(k + 1) * F, k, :, :],
                             d["L3_gnn_Wh"].rearrange("h f d -> f h d")).then_inc(loaded, 16)
            sp.dma_start(wo[:], d["L3_gnn_W_out"].rearrange("(h d) f -> d h f", d=HID)).then_inc(loaded, 16)
            sp.dma_start(bias[:], d["bh_t"]).then_inc(loaded, 16)

        @block.tensor
        def _(pe):
            pe.wait_ge(loaded, 96)
            for h in range(HEADS):
                if h > 1:
                    pe.wait_ge(gram_split, h - 1)
                w2 = wh_t[:, h, :, :].rearrange("p a f -> p (a f)")
                pe.matmul(m.ps_misc[:, h % 2, 0:P], w2, w2, start=True, stop=True).then_inc(gram_ready, 1)
            pe.wait_ge(gram_split, HEADS)

            def turn_next(n, side, part):
                pe.wait_ge(staged, n + 1)
                for k in range(4):
                    t = 4 * part + k
                    ins = pe.transpose(m.ps_misc[:, 1, k * P:(k + 1) * P],
                                       x2[:, side, t, :, :].rearrange("p a f -> p (a f)"),
                                       m.ident[:])
                ins.then_inc(x_turned, 1)

            def sum_next(n, side, half):
                if half == 0:
                    pe.wait_ge(x_split, 4 * n + 4)
                pe.matmul(m.ps_misc[:, 1, :], ones[:],
                          xs[:, side, half * HALF:(half + 1) * HALF],
                          start=True, stop=True).then_inc(sums_ready, 1)

            def project(g, v):
                for half in range(2):
                    for k in range(2):
                        ins = pe.matmul(m.ps_misc[:, half, :], gram[k][:, v % HEADS, :],
                                        xs[:, v // HEADS % 2, half * HALF:(half + 1) * HALF],
                                        start=(k == 0), stop=(k == 1))
                ins.then_inc(y_ready, 1)

            def score(g, v, t):
                if t == 0:
                    pe.wait_ge(y_split, g + 1)
                if not (v == 0 and t < 2):
                    pe.wait_ge(a.masked_ready, g * NT + t - 1)
                for half in range(2):
                    for k in range(2):
                        ins = pe.matmul(m.ps_score[:, t % 2, half * HALF:(half + 1) * HALF],
                                        xs[:, v // HEADS, t * P:(t + 1) * P],
                                        y[v % 2][k][:, half * HALF:(half + 1) * HALF],
                                        start=(k == 0), stop=(k == 1))
                ins.then_inc(a.scores_ready, 1)

            def head_out(g, v):
                pe.wait_ge(a.z_normed, g + 1)
                for k in range(4):
                    half, side = k // 2, k % 2
                    i = half * HALF + side * QUARTER
                    ins = pe.matmul(m.ps_misc[:, half, i % HALF:i % HALF + QUARTER],
                                    wz[:, side, v % HEADS, :],
                                    a.z[:, v % 2, half * QUARTER:(half + 1) * QUARTER],
                                    start=True, stop=True)
                ins.then_inc(hidden_ready, 1)

            def project_out(g, v):
                pe.wait_ge(hidden_done, g + 1)
                for half in range(2):
                    ins = pe.matmul(m.ps_misc[half * F:(half + 1) * F, 1, :], wo[:, v % HEADS, :],
                                    hidden[:, half * HALF:(half + 1) * HALF],
                                    start=True, stop=True)
                ins.then_inc(out_ready, 1)

            def rows(v):
                return lambda j: x2[:, v // HEADS, j, 0, :]

            for part in range(2):
                if part:
                    pe.wait_ge(x_split, 2)
                turn_next(0, 0, part)
            for half in range(2):
                if half:
                    pe.wait_ge(zeros_ready, 1)
                sum_next(0, 0, half)
            pe.wait_ge(zeros_ready, 2)

            with pe.Fori(0, B // 2) as bb:
                base = bb * UNITS
                project(base, 0)
                score(base, 0, 0)
                score(base, 0, 1)
                for v in range(UNITS):
                    g, u = base + v, v % HEADS
                    n = bb * 2 + v // HEADS + 1
                    side = (v // HEADS + 1) % 2
                    if u in (1, 2):
                        turn_next(n, side, u - 1)
                    if u in (3, 4):
                        sum_next(n, side, u - 3)
                    for t in range(NT):
                        if t + 2 < NT:
                            score(g, v, t + 2)
                        if v and t < 4:
                            pe_values(pe, m, a, g - 1, 1, range(2 * t, 2 * t + 2), rows(v - 1))
                        pe_turn(pe, m, a, g, t, v == 0)
                        if t == 2:
                            if u in (1, 2):
                                pe.wait_ge(x_split, 4 * n + 2 * u)
                            if u in (3, 4):
                                pe.wait_ge(zeros_ready, 2 * n + u - 2)
                            if v >= 2:
                                project_out(g - 2, v - 2)
                        if v and t == 3:
                            if v >= 2:
                                pe.wait_ge(out_added, g - 1)
                            pe_inverse_rows(pe, m, a, g - 1, (v - 1) % 2)
                        if t == 5 and v + 1 < UNITS:
                            if v:
                                pe.wait_ge(a.z_normed, g)
                            project(g + 1, v + 1)
                    if v:
                        if v + 1 < UNITS:
                            pe.wait_ge(y_split, g + 2)
                        head_out(g - 1, v - 1)
                    if v + 1 < UNITS:
                        score(g + 1, v + 1, 0)
                        score(g + 1, v + 1, 1)
                    if v:
                        pe.wait_ge(hidden_biased, g)
                    pe_values(pe, m, a, g, 0, range(NT), rows(v))
                g = base + UNITS - 1
                pe_values(pe, m, a, g, 1, range(NT), rows(UNITS - 1))
                project_out(g - 1, UNITS - 2)
                pe.wait_ge(out_added, g)
                pe_inverse_rows(pe, m, a, g, 1)
                head_out(g, UNITS - 1)
                project_out(g, UNITS - 1)
                pe.wait_ge(out_added, g + 1)

        @block.vector
        def _(dve):
            dve.memset(wz[:], 0.0).then_inc(cleared, 1)
            dve.memset(hidden[:, 0:P], 1.0).then_inc(step, 1)
            dve.wait_ge(step, 1)
            dve.tensor_copy(ones[:], hidden[:, 0:P]).then_inc(step, 1)
            for h in range(HEADS):
                dve.wait_ge(gram_hi, h + 1)
                dve.tensor_tensor(gram[1][:, h, :], m.ps_misc[:, h % 2, 0:P], gram[0][:, h, :],
                                  ALU.subtract).then_inc(gram_split, 1)
            setup_steps = 2
            per_batch = 4

            def stage_next(n, side, b):
                link = Chain(dve, step, setup_steps + per_batch * n)
                link(dve.tensor_copy(x2[:, side, :, 0, :], m.h[:, :, b, :]))
                link(dve.tensor_copy(x2[:, side, :, 1, :], x2[:, side, :, 0, :]))
                dve.nop().then_inc(staged, 1)
                link(dve.tensor_reduce(zero_row[:], x2[:, side, :, 0, :], AX, ALU.max))
                link(dve.tensor_scalar(zero_row[:], zero_row[:], 0.0, NEG, ALU.is_equal, ALU.mult))

            def split_next(n, side, part):
                dve.wait_ge(x_hi_ready, 2 * n + part + 1)
                cols = slice(part * HALF, (part + 1) * HALF)
                dve.tensor_tensor(xs[F:P, side, cols], m.ps_misc[F:P, 1, :], scratch[F:P, cols],
                                  ALU.subtract).then_inc(x_split, 1)

            def find_zeros(n, half):
                dve.wait_ge(sums_ready, 2 * n + half + 1)
                dve.tensor_scalar(scratch[:, half * HALF:(half + 1) * HALF], m.ps_misc[:, 1, :], 0.0,
                                  NEG, ALU.is_equal, ALU.mult).then_inc(zeros_ready, 1)

            def mask_next(n, side, tiles):
                if tiles[0] == 0:
                    dve.wait_ge(zeros_ready, 2 * n + 2)
                for t in tiles:
                    ins = dve.scalar_tensor_tensor(out=mask[:, side, t, :], in0=scratch[:],
                                                   scalar=zero_row[:, t:t + 1], in1=m.mask[:, t, :],
                                                   op0=ALU.min, op1=ALU.min)
                if tiles[-1] == NT - 1:
                    ins.then_inc(mask_ready, 1)

            def split_y(g, v):
                dve.wait_ge(y_hi, g + 1)
                dve.tensor_tensor(y[v % 2][1][:], m.ps_misc[:].rearrange("p a n -> p (a n)"),
                                  y[v % 2][0][:], ALU.subtract).then_inc(y_split, 1)

            def leaky(g):
                dve.wait_ge(hidden_biased, g + 1)
                dve.scalar_tensor_tensor(out=hidden[:], in0=hidden[:], scalar=0.01, in1=hidden[:],
                                         op0=ALU.mult, op1=ALU.max).then_inc(hidden_done, 1)

            def add_out(b, g, u):
                dve.wait_ge(out_ready, g + 1)
                out, share = m.h[:, :, b, :], m.ps_misc[:, 1, :].rearrange("p (t f) -> p t f", f=F)
                if u == 0:
                    dve.nop().then_inc(a.tile_free, 1)
                    dve.tensor_copy(out, share).then_inc(out_added, 1)
                else:
                    dve.wait_ge(out_added, g)
                    dve.tensor_tensor(out, out, share, ALU.add).then_inc(out_added, 1)

            stage_next(0, 0, 0)
            split_next(0, 0, 0)
            split_next(0, 0, 1)
            find_zeros(0, 0)
            find_zeros(0, 1)
            mask_next(0, 0, range(NT))
            with dve.Fori(0, B // 2) as bb:
                base = bb * UNITS

                def ready_mask(v):
                    if v % HEADS == 0:
                        dve.wait_ge(mask_ready, bb * 2 + v // HEADS + 1)

                def masked(g, v, t):
                    if t == 0:
                        ready_mask(v)
                    dve_mask(dve, m, a, g, v % 2, t, m.ps_score[:, t % 2, :],
                             mask[:, v // HEADS, t, :], v == 0, True)

                split_y(base, 0)
                masked(base, 0, 0)
                masked(base, 0, 1)
                for v in range(UNITS):
                    g, u = base + v, v % HEADS
                    n = bb * 2 + v // HEADS + 1
                    side = (v // HEADS + 1) % 2
                    for t in range(NT):
                        if t + 2 < NT:
                            masked(g, v, t + 2)
                        if v and t == 4:
                            dve_normalise(dve, m, a, g - 1, (v - 1) % 2)
                        dve_copy_turned(dve, m, a, g, t)
                        if t == 0 and u in (1, 2):
                            split_next(n, side, u - 1)
                        if t == 0 and u in (3, 4):
                            find_zeros(n, u - 3)
                        if v >= 2 and t == 1:
                            leaky(g - 2)
                        if v >= 2 and t == 2:
                            add_out(bb * 2 + (v - 2) // HEADS, g - 2, (v - 2) % HEADS)
                        if t in (0, 3, 5) and u >= 5:
                            k = 3 * (u - 5) + (0, 3, 5).index(t)
                            if k < NT:
                                mask_next(n, side, (k,))
                        if u == 0 and t == 5:
                            stage_next(n, side, n % B)
                        if t == 6 and v + 1 < UNITS:
                            split_y(g + 1, v + 1)
                    dve_inverse(dve, m, a, g, v % 2)
                    if v + 1 < UNITS:
                        masked(g + 1, v + 1, 0)
                        masked(g + 1, v + 1, 1)
                g = base + UNITS - 1
                leaky(g - 1)
                add_out(bb * 2 + 1, g - 1, HEADS - 2)
                dve_normalise(dve, m, a, g, 1)
                leaky(g)
                add_out(bb * 2 + 1, g, HEADS - 1)

        @block.scalar
        def _(act):
            for h in range(HEADS):
                act.wait_ge(gram_ready, h + 1)
                act.copy(gram[0][:, h, :], m.ps_misc[:, h % 2, 0:P]).then_inc(gram_hi, 1)

            def round_next(n, side, part):
                act.wait_ge(x_turned, 2 * n + part + 1)
                cols = slice(part * HALF, (part + 1) * HALF)
                act.copy(scratch[:, cols], m.ps_misc[:, 1, :]).then_inc(x_hi_ready, 1)
                act.copy(xs[0:F, side, cols], m.ps_misc[0:F, 1, :]).then_inc(x_split, 1)

            def round_y(g, v):
                act.wait_ge(y_ready, g + 1)
                act.copy(y[v % 2][0][:], m.ps_misc[:].rearrange("p a n -> p (a n)")).then_inc(y_hi, 1)

            def add_bias(g, v):
                act.wait_ge(hidden_ready, g + 1)
                act.activation(hidden[:], m.ps_misc[:].rearrange("p a n -> p (a n)"), ACT.Identity,
                               bias=bias[:, v % HEADS:v % HEADS + 1]).then_inc(hidden_biased, 1)

            round_next(0, 0, 0)
            round_next(0, 0, 1)
            with act.Fori(0, B // 2) as bb:
                base = bb * UNITS
                round_y(base, 0)
                for v in range(UNITS):
                    g, u = base + v, v % HEADS
                    n = bb * 2 + v // HEADS + 1
                    side = (v // HEADS + 1) % 2
                    for t in range(NT):
                        act_exp(act, m, a, g, v % 2, t, v == 0)
                        if t >= 1:
                            act_copy_turned(act, m, a, g, t - 1)
                        if t == 0 and u in (1, 2):
                            round_next(n, side, u - 1)
                        if v and t == 4:
                            act_copy_inverse(act, m, a, g - 1, (v - 1) % 2)
                        if t == 6 and v + 1 < UNITS:
                            round_y(g + 1, v + 1)
                    act_copy_turned(act, m, a, g, NT - 1)
                    if v:
                        add_bias(g - 1, v - 1)
                g = base + UNITS - 1
                act_copy_inverse(act, m, a, g, 1)
                add_bias(g, UNITS - 1)


def out_attention(nc, m, d):
    name = "out"
    with ExitStack() as ctx:
        a = attention_pipeline(nc, m, ctx, name)

        def sb(n, shape, dt=F32):
            return ctx.enter_context(nc.sbuf_tensor(f"{name}_{n}", shape, dt))

        def sem(n):
            return nc.alloc_semaphore(f"{name}_{n}")

        x2 = sb("x2", [P, 2, NT, 2, F])
        x_hi = sb("x_hi", [P, 2, N], F32R)
        x_lo = sb("x_lo", [P, 2, N], F32R)
        xs = sb("xs", [P, 2, N], F32R)
        squares = sb("squares", [P, N], F32R)
        row_squares = sb("row_squares", [P, NT, F])
        ones = sb("ones", [P, P], F32R)
        ones_f = sb("ones_f", [P, P])
        zero_row = sb("zero_row", [P, 2, NT])
        zero_col = sb("zero_col", [P, 2, N])
        mask = sb("mask", [P, 2, N])
        bias = sb("bias", [P, 1])

        loaded = sem("loaded")
        step = sem("step")
        rows_ready = sem("rows_ready")
        rows_copied = sem("rows_copied")
        x_turned = sem("x_turned")
        x_hi_ready = sem("x_hi_ready")
        x_lo_ready = sem("x_lo_ready")
        xs_ready = sem("xs_ready")
        squared = sem("squared")
        sums_ready = sem("sums_ready")
        zeros_ready = sem("zeros_ready")
        activated = sem("activated")
        out_turned = sem("out_turned")
        added = sem("added")
        block = ctx.enter_context(nc.Block())

        @block.sync
        def _(sp):
            for k in range(2):
                sp.dma_start(bias[k * F:(k + 1) * F, :],
                             d["L3_gnn_b_out"].rearrange("(f a) -> f a", a=1)).then_inc(loaded, 16)

        @block.tensor
        def _(pe):
            def rows(u):
                for c in range(NT // 2):
                    for k in range(2):
                        ins = pe.matmul(m.ps_misc[k * F:(k + 1) * F, 0, c * P:(c + 1) * P],
                                        m.h[:, 2 * c + k, u, :], m.ident[:], start=True, stop=True)
                ins.then_inc(rows_ready, 1)

            def turn_rows(u):
                pe.wait_ge(rows_copied, 2 * u + 2)
                for t in range(NT):
                    ins = pe.transpose(m.ps_misc[:, t // 4, (t % 4) * P:(t % 4 + 1) * P],
                                       x2[:, u % 2, t, :, :].rearrange("p a f -> p (a f)"), m.ident[:])
                ins.then_inc(x_turned, 1)

            def sum_squares(u):
                pe.wait_ge(squared, u + 1)
                pe.wait_ge(x_lo_ready, u + 1)
                for half in range(2):
                    ins = pe.matmul(m.ps_misc[:, half, :], ones[:],
                                    squares[:, half * HALF:(half + 1) * HALF], start=True, stop=True)
                ins.then_inc(sums_ready, 1)

            def score(u, t):
                if t == 0:
                    pe.wait_ge(xs_ready, 2 * u + 2)
                if not (u == 0 and t < 2):
                    pe.wait_ge(a.masked_ready, u * NT + t - 1)
                for half in range(2):
                    for k, part in enumerate((x_hi, x_lo)):
                        ins = pe.matmul(m.ps_score[:, t % 2, half * HALF:(half + 1) * HALF],
                                        xs[:, u % 2, t * P:(t + 1) * P],
                                        part[:, u % 2, half * HALF:(half + 1) * HALF],
                                        start=(k == 0), stop=(k == 1))
                ins.then_inc(a.scores_ready, 1)

            def turn_out(u):
                pe.wait_ge(activated, u + 1)
                for c in range(NT // 2):
                    ins = pe.transpose(m.ps_misc[:, 1, c * P:(c + 1) * P],
                                       a.z[:, u % 2, c * P:(c + 1) * P], m.ident[:])
                ins.then_inc(out_turned, 1)

            def values(u):
                return lambda j: x2[:, u % 2, j, 0, :]

            pe.wait_ge(step, 2)
            rows(0)
            turn_rows(0)
            sum_squares(0)
            score(0, 0)
            score(0, 1)
            for u in range(B):
                for t in range(NT):
                    if t + 2 < NT:
                        score(u, t + 2)
                    if u and t < 4:
                        pe_values(pe, m, a, u - 1, 1, range(2 * t, 2 * t + 2), values(u - 1))
                    pe_turn(pe, m, a, u, t, u == 0)
                    if u and t == 3:
                        pe_inverse_rows(pe, m, a, u - 1, (u - 1) % 2)
                    if u + 1 < B and t == 4:
                        if u:
                            pe.wait_ge(a.z_normed, u)
                        else:
                            pe.wait_ge(zeros_ready, 1)
                        rows(u + 1)
                    if u and t == 5:
                        turn_out(u - 1)
                    if u + 1 < B and t == 6:
                        if u:
                            pe.wait_ge(added, u)
                        turn_rows(u + 1)
                    if u + 1 < B and t == 7:
                        sum_squares(u + 1)
                if u + 1 < B:
                    score(u + 1, 0)
                    score(u + 1, 1)
                    pe.wait_ge(zeros_ready, u + 2)
                pe_values(pe, m, a, u, 0, range(NT), values(u))
            pe_values(pe, m, a, B - 1, 1, range(NT), values(B - 1))
            pe.wait_ge(added, B - 1)
            pe_inverse_rows(pe, m, a, B - 1, 1)
            turn_out(B - 1)

        @block.vector
        def _(dve):
            link = Chain(dve, step)
            link(dve.memset(ones_f[:], 1.0))
            link(dve.tensor_copy(ones[:], ones_f[:]))
            dve.wait_ge(loaded, 32)

            def copy_rows(u):
                dve.wait_ge(rows_copied, 2 * u + 1)
                dve.tensor_copy(x2[:, u % 2, :, 1, :], x2[:, u % 2, :, 0, :]).then_inc(rows_copied, 1)
                link(dve.tensor_tensor(row_squares[:], x2[:, u % 2, :, 0, :], x2[:, u % 2, :, 0, :], ALU.mult))
                link(dve.tensor_reduce(zero_row[:, u % 2, :], row_squares[:], AX, ALU.max))
                link(dve.tensor_scalar(zero_row[:, u % 2, :], zero_row[:, u % 2, :], 0.0, NEG,
                                       ALU.is_equal, ALU.mult))

            def split_x(u):
                dve.wait_ge(x_hi_ready, u + 1)
                dve.tensor_tensor(x_lo[:, u % 2, :], m.ps_misc[:].rearrange("p a n -> p (a n)"),
                                  x_hi[:, u % 2, :], ALU.subtract).then_inc(x_lo_ready, 1)
                dve.wait_ge(x_lo_ready, u + 1)
                dve.tensor_copy(xs[F:P, u % 2, :], x_lo[F:P, u % 2, :]).then_inc(xs_ready, 1)

            def find_zeros(u):
                dve.wait_ge(sums_ready, u + 1)
                dve.tensor_scalar(zero_col[:, u % 2, :], m.ps_misc[:].rearrange("p a n -> p (a n)"),
                                  0.0, NEG, ALU.is_equal, ALU.mult).then_inc(zeros_ready, 1)

            def mask_tile(u, t):
                if t == 0:
                    dve.wait_ge(zeros_ready, u + 1)
                link(dve.scalar_tensor_tensor(out=mask[:, t % 2, :], in0=zero_col[:, u % 2, :],
                                              scalar=zero_row[:, u % 2, t:t + 1], in1=m.mask[:, t, :],
                                              op0=ALU.min, op1=ALU.min))
                dve_mask(dve, m, a, u, u % 2, t, m.ps_score[:, t % 2, :], mask[:, t % 2, :], u == 0)

            def activate(u):
                dve_normalise(dve, m, a, u, u % 2)
                dve.wait_ge(a.z_normed, u + 1)
                z = a.z[:, u % 2, :]
                link(dve.tensor_scalar(z, z, bias[:, 0:1], None, ALU.add))
                dve.scalar_tensor_tensor(out=z, in0=z, scalar=0.01, in1=z, op0=ALU.mult,
                                         op1=ALU.max).then_inc(activated, 1)

            def add(u):
                dve.wait_ge(out_turned, u + 1)
                for side in range(2):
                    x = z_rows(m.x[:, :, u, :], side)
                    ins = dve.tensor_tensor(x, x, turned_rows(m.ps_misc[:, 1, :], side), ALU.add)
                ins.then_inc(added, 1)

            copy_rows(0)
            split_x(0)
            find_zeros(0)
            mask_tile(0, 0)
            mask_tile(0, 1)
            for u in range(B):
                for t in range(NT):
                    if t + 2 < NT:
                        mask_tile(u, t + 2)
                    if u and t == 4:
                        activate(u - 1)
                    dve_copy_turned(dve, m, a, u, t)
                    if u + 1 < B and t == 5:
                        copy_rows(u + 1)
                    if u and t == 6:
                        add(u - 1)
                    if u + 1 < B and t == 6:
                        split_x(u + 1)
                dve_inverse(dve, m, a, u, u % 2)
                if u + 1 < B:
                    find_zeros(u + 1)
                    mask_tile(u + 1, 0)
                    mask_tile(u + 1, 1)
            activate(B - 1)
            add(B - 1)

        @block.scalar
        def _(act):
            def copy_rows(u):
                act.wait_ge(rows_ready, u + 1)
                dst = x2[:, u % 2, :, 0, :].rearrange("p (a c) f -> p a c f", a=2)
                src = m.ps_misc[:, 0, :].rearrange("p (c a f) -> p a c f", c=4, a=2)
                act.copy(dst, src).then_inc(rows_copied, 1)

            def split_x(u):
                act.wait_ge(x_turned, u + 1)
                ps = m.ps_misc[:].rearrange("p a n -> p (a n)")
                act.copy(x_hi[:, u % 2, :], ps).then_inc(x_hi_ready, 1)
                act.wait_ge(x_hi_ready, u + 1)
                act.copy(xs[0:F, u % 2, :], x_hi[0:F, u % 2, :]).then_inc(xs_ready, 1)
                act.activation(squares[:], x_hi[:, u % 2, :], ACT.Square).then_inc(squared, 1)

            copy_rows(0)
            split_x(0)
            for u in range(B):
                for t in range(NT):
                    act_exp(act, m, a, u, u % 2, t, u == 0)
                    if t >= 1:
                        act_copy_turned(act, m, a, u, t - 1)
                    if u and t == 4:
                        act_copy_inverse(act, m, a, u - 1, (u - 1) % 2)
                    if u + 1 < B and t == 5:
                        copy_rows(u + 1)
                    if u + 1 < B and t == 7:
                        split_x(u + 1)
                act_copy_turned(act, m, a, u, NT - 1)
            act_copy_inverse(act, m, a, B - 1, 1)


def project(nc, m, ctx, name, weight, width, dests):
    turned = ctx.enter_context(nc.sbuf_tensor(name + "_turned", [P, B // 2, N], F32))
    ready = nc.alloc_semaphore(name + "_ready")
    copied = nc.alloc_semaphore(name + "_copied")
    done = nc.alloc_semaphore(name + "_done")
    taken = [nc.alloc_semaphore(f"{name}_taken{i}") for i in range(2)]
    with ExitStack() as inner:
        block = inner.enter_context(nc.Block())
        pairs = [(q, t) for q in range(B // 2) for t in range(NT)]

        @block.tensor
        def _(pe):
            for q in range(B // 2):
                if q >= 2:
                    pe.wait_ge(copied, q - 1)
                for t in range(NT):
                    ins = pe.transpose(m.ps_score[:, q % 2, t * P:(t + 1) * P],
                                       m.h[:, t, 2 * q:2 * q + 2, :].rearrange("p a f -> p (a f)"),
                                       m.ident[:])
                ins.then_inc(ready, 1)
            for i, (q, t) in enumerate(pairs):
                if t == 0:
                    pe.wait_ge(copied, q + 1)
                if i >= 4:
                    pe.wait_ge(taken[i % 2], (i - 4) // 2 + 1)
                bank = m.ps_misc[:, i % 4 // 2, 0:width] if i % 2 else m.ps_turn[:, i % 4 // 2, 0:width]
                pe.matmul(bank, turned[:, q, t * P:(t + 1) * P], weight, start=True,
                          stop=True).then_inc(done, 1)

        def take(eng, copy, parity):
            for q in range(parity, B // 2, 2):
                eng.wait_ge(ready, q + 1)
                if q >= 1:
                    eng.wait_ge(copied, q)
                copy(turned[:, q, :], m.ps_score[:, q % 2, :]).then_inc(copied, 1)
            for i, (q, t) in enumerate(pairs):
                if i % 2 != parity:
                    continue
                eng.wait_ge(done, i + 1)
                bank = m.ps_misc if i % 2 else m.ps_turn
                for lo, hi, place in dests:
                    ins = copy(place(q, t), bank[:, i % 4 // 2, lo:hi])
                ins.then_inc(taken[parity], 1)

        @block.vector
        def _(dve):
            take(dve, dve.tensor_copy, 0)

        @block.scalar
        def _(act):
            take(act, act.copy, 1)
    return turned


def mix(nc, m, ctx, name, values, finish, act_finish=None):
    hi, lo = split(nc, ctx, name + "_v", [P, NT, B * F])
    rounded = nc.alloc_semaphore(name + "_rounded")
    parted = nc.alloc_semaphore(name + "_parted")
    mixed = nc.alloc_semaphore(name + "_mixed")
    finished = nc.alloc_semaphore(name + "_finished")
    with ExitStack() as inner:
        block = inner.enter_context(nc.Block())

        def bank(t):
            return m.ps_misc[:, t % 2, :]

        @block.scalar
        def _(act):
            for t in range(NT):
                act.copy(hi[:, t, :], values(t)).then_inc(rounded, 1)

        @block.tensor
        def _(pe):
            for t in range(NT):
                if t >= 2:
                    pe.wait_ge(finished, t - 1)
                for j in range(NT):
                    if t == 0:
                        pe.wait_ge(parted, j + 1)
                    for k, part in enumerate((hi, lo)):
                        ins = pe.matmul(bank(t), m.adj_t[:, j, t * P:(t + 1) * P], part[:, j, :],
                                        start=(j == 0 and k == 0), stop=(j == NT - 1 and k == 1))
                ins.then_inc(mixed, 1)

        @block.vector
        def _(dve):
            for t in range(NT):
                dve.wait_ge(rounded, t + 1)
                dve.tensor_tensor(lo[:, t, :], values(t), hi[:, t, :], ALU.subtract).then_inc(parted, 1)
            for t in range(NT):
                dve.wait_ge(mixed, t + 1)
                finish(dve, t, bank(t)).then_inc(finished, 1)


def block_weights(nc, ctx, name, loads, width):
    w = ctx.enter_context(nc.sbuf_tensor(name + "_w", [P, width], F32))
    cleared = nc.alloc_semaphore(name + "_w_cleared")
    loaded = nc.alloc_semaphore(name + "_w_loaded")
    with ExitStack() as inner:
        block = inner.enter_context(nc.Block())

        @block.vector
        def _(dve):
            dve.memset(w[:], 0.0).then_inc(cleared, 1)

        @block.sync
        def _(sp):
            sp.wait_ge(cleared, 1)
            for row, col, src in loads:
                sp.dma_start(w[row:row + src.shape[0], col:col + src.shape[1]], src).then_inc(loaded, 16)
            sp.wait_ge(loaded, 16 * len(loads))
    return w


def graph_layer(nc, m, d):
    with ExitStack() as ctx:
        for r in range(2):
            src = d["L2_w"][r]
            w = block_weights(nc, ctx, f"gl{r}", [(0, 0, src), (F, F, src)], P)
            with ExitStack() as part:
                zw = part.enter_context(nc.sbuf_tensor(f"gl{r}_zw", [P, NT, B, F], F32))
                project(nc, m, part, f"gl{r}_p", w[:], P, [
                    (0, P, lambda q, t: zw[:, t, 2 * q:2 * q + 2, :].rearrange("p a f -> p (a f)"))])

                def finish(dve, t, ps):
                    h = m.h[:, t, :, :].rearrange("p b f -> p (b f)")
                    x = m.x[:, t, :, :].rearrange("p b f -> p (b f)")
                    if r == 0:
                        return dve.tensor_scalar(h, ps, 0.0, None, ALU.max)
                    return dve.scalar_tensor_tensor(out=x, in0=ps, scalar=0.0, in1=x,
                                                    op0=ALU.max, op1=ALU.add)

                mix(nc, m, part, f"gl{r}_m", lambda t: zw[:, t, :, :].rearrange("p b f -> p (b f)"), finish)


def graph_attention_layer(nc, m, d):
    name = "gat"
    with ExitStack() as ctx:
        def sb(n, shape, dt=F32):
            return ctx.enter_context(nc.sbuf_tensor(f"{name}_{n}", shape, dt))

        def sem(n):
            return nc.alloc_semaphore(f"{name}_{n}")

        width = P + 2
        w = block_weights(nc, ctx, "gat", [(0, 0, d["l1_wt"]), (F, F, d["l1_wt"])], width)
        w_rows = sb("w_rows", [F, 2, F])
        a_cols = sb("a_cols", [F, 2])
        a2_w = sb("a2_w", [P, 2, P])
        wh = sb("wh", [P, NT, B, F])
        e1 = sb("e1", [P, NT, B])
        with ExitStack() as prep:
            loaded = nc.alloc_semaphore("gat_loaded")
            ready = nc.alloc_semaphore("gat_ready")
            cleared = nc.alloc_semaphore("gat_cleared")
            block = prep.enter_context(nc.Block())

            @block.sync
            def _(sp):
                for k in range(2):
                    sp.dma_start(w_rows[:, k, :], d["L1_gnn_W"]).then_inc(loaded, 16)
                sp.dma_start(a_cols[:], d["l1_a"]).then_inc(loaded, 16)

            @block.tensor
            def _(pe):
                pe.wait_ge(loaded, 48)
                rows = w_rows[:].rearrange("o a f -> o (a f)")
                pe.matmul(m.ps_misc[:, 0, 0:P], rows, a_cols[:, 1:2].to_broadcast([F, P]),
                          start=True, stop=True)
                pe.matmul(m.ps_misc[:, 1, 0:1], rows, a_cols[:, 0:1], start=True, stop=True)\
                  .then_inc(ready, 1)

            @block.vector
            def _(dve):
                dve.memset(a2_w[:], 0.0).then_inc(cleared, 1)
                dve.wait_ge(ready, 1)
                dve.wait_ge(cleared, 1)
                for k in range(2):
                    half = slice(k * F, (k + 1) * F)
                    dve.tensor_copy(a2_w[half, k, :], m.ps_misc[half, 0, 0:P])
                    dve.tensor_copy(w[half, P + k:P + k + 1], m.ps_misc[half, 1, 0:1])

        x_t = project(nc, m, ctx, "gat_p", w[:], width, [
            (0, P, lambda q, t: wh[:, t, 2 * q:2 * q + 2, :].rearrange("p a f -> p (a f)")),
            (P, P + 2, lambda q, t: e1[:, t, 2 * q:2 * q + 2])])

        a = attention_pipeline(nc, m, ctx, name)
        e2 = sb("e2", [P, 2, N])
        sums = sb("sums", [P, 2, N])
        z_exp = sb("z_exp", [P, HALF])
        step = sem("step")
        e2_ready = sem("e2_ready")
        e2_copied = sem("e2_copied")
        summed = sem("summed")
        z_exped = sem("z_exped")
        activated = sem("activated")
        out_turned = sem("out_turned")
        added = sem("added")
        block = ctx.enter_context(nc.Block())

        @block.tensor
        def _(pe):
            def spread_e2(u):
                for half in range(2):
                    ins = pe.matmul(m.ps_score[:, u % 2, half * HALF:(half + 1) * HALF],
                                    a2_w[:, u % 2, :], x_t[:, u // 2, half * HALF:(half + 1) * HALF],
                                    start=True, stop=True)
                ins.then_inc(e2_ready, 1)

            def turn_out(u):
                pe.wait_ge(activated, u + 1)
                for c in range(NT // 2):
                    ins = pe.transpose(m.ps_misc[:, 1, c * P:(c + 1) * P],
                                       a.z[:, u % 2, c * P:(c + 1) * P], m.ident[:])
                ins.then_inc(out_turned, 1)

            def values(u):
                return lambda j: wh[:, j, u, :]

            spread_e2(0)
            for u in range(B):
                for t in range(NT):
                    if u and t < 4:
                        pe_values(pe, m, a, u - 1, 1, range(2 * t, 2 * t + 2), values(u - 1))
                    pe_turn(pe, m, a, u, t, u == 0)
                    if u and t == 3:
                        if u >= 2:
                            pe.wait_ge(added, u - 1)
                        pe_inverse_rows(pe, m, a, u - 1, (u - 1) % 2)
                    if u + 1 < B and t == 4:
                        pe.wait_ge(e2_copied, u + 1)
                        spread_e2(u + 1)
                    if u and t == 6:
                        turn_out(u - 1)
                if u:
                    pe.wait_ge(a.z_normed, u)
                pe_values(pe, m, a, u, 0, range(NT), values(u))
            pe_values(pe, m, a, B - 1, 1, range(NT), values(B - 1))
            pe.wait_ge(added, B - 1)
            pe_inverse_rows(pe, m, a, B - 1, 1)
            turn_out(B - 1)

        @block.scalar
        def _(act):
            def copy_e2(u):
                act.wait_ge(e2_ready, u + 1)
                act.copy(e2[:, u % 2, :], m.ps_score[:, u % 2, :]).then_inc(e2_copied, 1)

            def add_e1(u, t):
                if t == 0:
                    act.wait_ge(e2_copied, u + 1)
                if u or t >= 2:
                    act.wait_ge(a.masked_ready, u * NT + t - 1)
                act.activation(sums[:, t % 2, :], e2[:, u % 2, :], ACT.Identity,
                               bias=e1[:, t, u:u + 1]).then_inc(summed, 1)

            def exp_z(u):
                act.wait_ge(a.z_normed, u + 1)
                act.activation(z_exp[:], a.z[:, u % 2, :], ACT.Exp).then_inc(z_exped, 1)

            copy_e2(0)
            add_e1(0, 0)
            add_e1(0, 1)
            for u in range(B):
                for t in range(NT):
                    act_exp(act, m, a, u, u % 2, t, u == 0)
                    if t + 2 < NT:
                        add_e1(u, t + 2)
                    if t >= 1:
                        act_copy_turned(act, m, a, u, t - 1)
                    if u and t == 4:
                        act_copy_inverse(act, m, a, u - 1, (u - 1) % 2)
                    if u and t == 5:
                        exp_z(u - 1)
                    if u + 1 < B and t == 6:
                        copy_e2(u + 1)
                        add_e1(u + 1, 0)
                        add_e1(u + 1, 1)
                act_copy_turned(act, m, a, u, NT - 1)
            act_copy_inverse(act, m, a, B - 1, 1)
            exp_z(B - 1)

        @block.vector
        def _(dve):
            link = Chain(dve, step)

            def mask_tile(u, t):
                dve.wait_ge(summed, u * NT + t + 1)
                s = sums[:, t % 2, :]
                dve.scalar_tensor_tensor(out=s, in0=s, scalar=0.2, in1=s, op0=ALU.mult,
                                         op1=ALU.max).then_inc(a.scores_ready, 1)
                dve_mask(dve, m, a, u, u % 2, t, s, m.mask[:, t, :], u == 0)

            def elu(u):
                dve.wait_ge(z_exped, u + 1)
                link(dve.tensor_scalar(z_exp[:], z_exp[:], 1.0, -1.0, ALU.min, ALU.add))
                dve.tensor_tensor(a.z[:, u % 2, :], a.z[:, u % 2, :], z_exp[:], ALU.max).then_inc(activated, 1)

            def add(u):
                dve.wait_ge(out_turned, u + 1)
                for side in range(2):
                    x = z_rows(m.x[:, :, u, :], side)
                    ins = dve.tensor_tensor(x, x, turned_rows(m.ps_misc[:, 1, :], side), ALU.add)
                ins.then_inc(added, 1)

            mask_tile(0, 0)
            mask_tile(0, 1)
            for u in range(B):
                for t in range(NT):
                    if t + 2 < NT:
                        mask_tile(u, t + 2)
                    if u and t == 4:
                        dve_normalise(dve, m, a, u - 1, (u - 1) % 2)
                    dve_copy_turned(dve, m, a, u, t)
                    if u and t == 5:
                        elu(u - 1)
                    if u and t == 6:
                        add(u - 1)
                dve_inverse(dve, m, a, u, u % 2)
                if u + 1 < B:
                    mask_tile(u + 1, 0)
                    mask_tile(u + 1, 1)
            dve_normalise(dve, m, a, B - 1, 1)
            elu(B - 1)
            add(B - 1)


def hypergraph_layer(nc, m, d):
    name = "hyp"
    EN = F
    with ExitStack() as ctx:
        def sb(n, shape, dt=F32):
            return ctx.enter_context(nc.sbuf_tensor(f"{name}_{n}", shape, dt))

        width = 2 * P + 2
        w = block_weights(nc, ctx, name, [
            (0, 0, d["L0_gnn_W"]), (F, F, d["L0_gnn_W"]),
            (0, P, d["L0_gnn_W_ind"]), (F, P + F, d["L0_gnn_W_ind"])], width)
        an_w = sb("an_w", [P, 2, P])
        vecs = sb("vecs", [F, 4])
        fc_w = sb("fc_w", [P, 2, P])
        fc_b = sb("fc_b", [P, 1])
        av = sb("av", [P, 1])
        ones = sb("ones", [P, P])
        members = sb("members", [P, N])
        edge_mask = sb("edge_mask", [P, N])
        node_mask = sb("node_mask", [P, NT, EN])
        linked = sb("linked", [P, NT])
        rank = sb("rank", [P, N])
        slots = sb("slots", [P, 1])
        slots_int = sb("slots_int", [P, 1], mybir.dt.int32)
        edge_rows = sb("edge_rows", [P, B, F])
        picks = sb("picks", [P, B * F + 18], F32R)
        best = sb("best", [P, NT, B])
        h1 = sb("h1", [P, NT, B, F])
        gate = sb("gate", [P, NT, B])
        coef_sum = sb("coef_sum", [P, NT, B])
        minus_one = sb("minus_one", [P, 1])
        neighbours = sb("neighbours", [P, NT, B, F])

        with ExitStack() as part:
            def psb(n, shape, dt=F32):
                return part.enter_context(nc.sbuf_tensor(f"{name}_{n}", shape, dt))

            def sem(n):
                return nc.alloc_semaphore(f"{name}_{n}")

            w_t = psb("w_t", [F, 2, F])
            member_rows = psb("member_rows", [P, NT, EN])
            member_cols = psb("member_cols", [P, N])
            counts = psb("counts", [P, NT])
            total = psb("total", [P, N])
            upper = psb("upper", [F, 2, EN])
            loaded, cleared, folded, step = sem("loaded"), sem("cleared"), sem("folded"), sem("stepa")
            counted, filled, ranked, triangle = sem("counted"), sem("filled"), sem("ranked"), sem("triangle")
            block = part.enter_context(nc.Block())

            @block.sync
            def _(sp):
                for k in range(2):
                    sp.dma_start(w_t[:, k, :], d["l0_wt"]).then_inc(loaded, 16)
                    sp.dma_start(member_cols[k * F:(k + 1) * F, :], d["h_t"]).then_inc(loaded, 16)
                sp.dma_start(vecs[:, 0:3], d["l0_vecs"]).then_inc(loaded, 16)
                sp.dma_start(member_rows[:], d["h_rows"]).then_inc(loaded, 16)
                sp.dma_start(fc_b[:], d["L0_gnn_fcb"].rearrange("(f a) -> f a", a=1)).then_inc(loaded, 16)
                sp.dma_start(av[:], d["L0_gnn_av"].rearrange("(f a) -> f a", a=1)).then_inc(loaded, 16)
                sp.wait_ge(cleared, 1)
                for k in range(2):
                    sp.dma_start(fc_w[k * F:(k + 1) * F, k, :], d["L0_gnn_fcW"]).then_inc(loaded, 16)

            @block.gpsimd
            def _(pool):
                pool.memset(upper[:], 1.0).then_inc(triangle, 1)
                pool.wait_ge(triangle, 1)
                pool.affine_select(out=upper[:], in_=upper[:], compare_op=ALU.is_gt, fill=0.0, base=0,
                                   pattern=[[0, 2], [1, EN]], channel_multiplier=-1).then_inc(triangle, 1)

            @block.tensor
            def _(pe):
                pe.wait_ge(loaded, 160)
                rows = w_t[:].rearrange("o a f -> o (a f)")
                pe.matmul(m.ps_misc[:, 0, 0:P], rows, vecs[:, 0:1].to_broadcast([F, P]),
                          start=True, stop=True)
                pe.matmul(m.ps_misc[:, 1, 0:1], rows, vecs[:, 1:2], start=True, stop=True)\
                  .then_inc(folded, 1)
                pe.wait_ge(filled, 1)
                for half in range(2):
                    cols = slice(half * HALF, (half + 1) * HALF)
                    ins = pe.matmul(m.ps_score[:, 0, cols], ones[0:EN, :], members[0:EN, cols],
                                    start=True, stop=True)
                ins.then_inc(counted, 1)
                pe.wait_ge(filled, 2)
                pe.wait_ge(triangle, 2)
                for half in range(2):
                    cols = slice(half * HALF, (half + 1) * HALF)
                    ins = pe.matmul(m.ps_score[:, 1, cols], upper[:].rearrange("p a e -> p (a e)"),
                                    rank[0:EN, cols], start=True, stop=True)
                ins.then_inc(ranked, 1)

            @block.vector
            def _(dve):
                link = Chain(dve, step)
                link(dve.memset(an_w[:], 0.0))
                link(dve.memset(ones[:], 1.0))
                link(dve.memset(fc_w[:], 0.0))
                dve.nop().then_inc(cleared, 1)
                dve.wait_ge(loaded, 160)
                dve.wait_ge(folded, 1)
                for k in range(2):
                    half = slice(k * F, (k + 1) * F)
                    dve.tensor_copy(an_w[half, k, :], m.ps_misc[half, 0, 0:P])
                    link(dve.tensor_copy(w[half, 2 * P + k:2 * P + k + 1], m.ps_misc[half, 1, 0:1]))
                link(dve.tensor_scalar(members[:], member_cols[:], 0.0, None, ALU.is_gt))
                dve.nop().then_inc(filled, 1)
                link(dve.tensor_scalar(edge_mask[:], member_cols[:], 0.0, NEG, ALU.is_le, ALU.mult))
                link(dve.tensor_scalar(node_mask[:], member_rows[:], 0.0, NEG, ALU.is_le, ALU.mult))
                link(dve.tensor_reduce(counts[:], node_mask[:], AX, ALU.max))
                link(dve.tensor_scalar(linked[:], counts[:], 0.0, None, ALU.is_equal))
                dve.wait_ge(counted, 1)
                link(dve.tensor_scalar(total[:], m.ps_score[:, 0, :], 0.0, None, ALU.is_equal))
                link(dve.tensor_tensor(rank[:], members[:], total[:], ALU.max))
                dve.nop().then_inc(filled, 1)
                link(dve.scalar_tensor_tensor(out=total[:], in0=total[:], scalar=float(EN),
                                              in1=m.ps_score[:, 0, :], op0=ALU.mult, op1=ALU.add))
                link(dve.tensor_reduce(slots[:], total[:], AX, ALU.max))
                link(dve.tensor_copy(slots_int[:], slots[:]))
                dve.wait_ge(ranked, 1)
                link(dve.scalar_tensor_tensor(out=rank[:], in0=m.ps_score[:, 1, :], scalar=1.0,
                                              in1=rank[:], op0=ALU.add, op1=ALU.mult))
                dve.tensor_scalar(rank[:], rank[:], -1.0, None, ALU.add)

        with ExitStack() as part:
            x_t = project(nc, m, part, name + "_p", w[:], width, [
                (0, P, lambda q, t: h1[:, t, 2 * q:2 * q + 2, :].rearrange("p a f -> p (a f)")),
                (P, 2 * P, lambda q, t: neighbours[:, t, 2 * q:2 * q + 2, :].rearrange("p a f -> p (a f)")),
                (2 * P, width, lambda q, t: gate[:, t, 2 * q:2 * q + 2])])

            def psb(n, shape, dt=F32):
                return part.enter_context(nc.sbuf_tensor(f"{name}_{n}", shape, dt))

            def sem(n):
                return nc.alloc_semaphore(f"{name}_{n}")

            score = psb("score", [P, 2, N])
            masked = psb("masked", [P, 2, N])
            weights = psb("weights", [P, 2, N])
            weights_t = psb("weights_t", [P, NT, P])
            neg_max, row_sum = psb("neg_max", [P, B]), psb("row_sum", [P, B])
            step, spread, copied, masked_ready, exp_ready = (
                sem("stepb"), sem("spread"), sem("copied"), sem("masked_ready"), sem("exp_ready"))
            turned = [sem("turned0"), sem("turned1")]
            turned_out = [sem("turned_out0"), sem("turned_out1")]
            summed, scaled = sem("summed"), sem("scaled")
            block = part.enter_context(nc.Block())

            @block.tensor
            def _(pe):
                def spread_scores(b):
                    if b >= 2:
                        pe.wait_ge(copied, b - 1)
                    for half in range(2):
                        cols = slice(half * HALF, (half + 1) * HALF)
                        ins = pe.matmul(m.ps_score[:, b % 2, cols], an_w[:, b % 2, :],
                                        x_t[:, b // 2, cols], start=True, stop=True)
                    ins.then_inc(spread, 1)

                spread_scores(0)
                spread_scores(1)
                for b in range(B):
                    pe.wait_ge(exp_ready, b + 1)
                    for half in range(2):
                        if b:
                            pe.wait_ge(turned_out[half], b)
                        for k in range(4):
                            t = half * 4 + k
                            ins = pe.transpose(m.ps_turn[:, half, k * P:(k + 1) * P],
                                               weights[:, b % 2, t * P:(t + 1) * P], m.ident[:])
                        ins.then_inc(turned[half], 1)
                    if b + 2 < B:
                        spread_scores(b + 2)
                    for half in range(2):
                        pe.wait_ge(turned_out[half], b + 1)
                    if b >= 2:
                        pe.wait_ge(scaled, b - 1)
                    for t in range(NT):
                        ins = pe.matmul(m.ps_misc[:, b % 2, 0:F], weights_t[:, t, :], h1[:, t, b, :],
                                        start=(t == 0), stop=(t == NT - 1))
                    ins.then_inc(summed, 1)

            @block.scalar
            def _(act):
                def copy_scores(b):
                    act.wait_ge(spread, b + 1)
                    if b >= 2:
                        act.wait_ge(masked_ready, b - 1)
                    act.copy(score[:, b % 2, :], m.ps_score[:, b % 2, :]).then_inc(copied, 1)

                copy_scores(0)
                copy_scores(1)
                for b in range(B):
                    act.wait_ge(masked_ready, b + 1)
                    if b >= 2:
                        act.wait_ge(turned[1], b - 1)
                    act.activation(weights[:, b % 2, :], masked[:, b % 2, :], ACT.Exp, scale=-1.0,
                                   bias=neg_max[:, b:b + 1], accum_out=row_sum[:, b:b + 1])\
                       .then_inc(exp_ready, 1)
                    if b + 2 < B:
                        copy_scores(b + 2)
                    act.wait_ge(turned[0], b + 1)
                    if b:
                        act.wait_ge(summed, b)
                    act.copy(weights_t[:, 0:4, :].rearrange("p k e -> p (k e)"), m.ps_turn[:, 0, :])\
                       .then_inc(turned_out[0], 1)

            @block.vector
            def _(dve):
                link = Chain(dve, step)

                def mask(b):
                    dve.wait_ge(copied, b + 1)
                    s = score[:, b % 2, :]
                    link(dve.scalar_tensor_tensor(out=s, in0=s, scalar=0.2, in1=s, op0=ALU.mult,
                                                  op1=ALU.max))
                    if b >= 2:
                        dve.wait_ge(exp_ready, b - 1)
                    dve.tensor_tensor_reduce(masked[:, b % 2, :], s, edge_mask[:], -1.0, HUGE, ALU.add,
                                             ALU.min, neg_max[:, b:b + 1]).then_inc(masked_ready, 1)

                mask(0)
                for b in range(B):
                    if b + 1 < B:
                        mask(b + 1)
                    dve.wait_ge(turned[1], b + 1)
                    if b:
                        dve.wait_ge(summed, b)
                    dve.tensor_copy(weights_t[:, 4:8, :].rearrange("p k e -> p (k e)"),
                                    m.ps_turn[:, 1, :]).then_inc(turned_out[1], 1)
                    dve.wait_ge(exp_ready, b + 1)
                    link(dve.reciprocal(row_sum[:, b:b + 1], row_sum[:, b:b + 1]))
                    dve.wait_ge(summed, b + 1)
                    dve.tensor_scalar(edge_rows[:, b, :], m.ps_misc[:, b % 2, 0:F],
                                      row_sum[:, b:b + 1], None, ALU.mult).then_inc(scaled, 1)

        with ExitStack() as part:
            def psb(n, shape, dt=F32):
                return part.enter_context(nc.sbuf_tensor(f"{name}_{n}", shape, dt))

            def sem(n):
                return nc.alloc_semaphore(f"{name}_{n}")

            elus = psb("elus", [P, B, F])
            elus_t = psb("elus_t", [F, B, P])
            rows_t = psb("rows_t", [F, B, P])
            hidden = psb("hidden", [P, B, P])
            pick_hi = psb("pick_hi", [P, B * F + 18], F32R)
            pick_all = psb("pick_all", [P, B * F + 18])
            table = psb("table", [P, NT, B, EN])
            step, exped, elued, turned, copied = (
                sem("stepc"), sem("exped"), sem("elued"), sem("turned_c"), sem("copied_c"))
            hidden_ready, tanh_ready, scored, collected, rounded = (
                sem("hidden_ready"), sem("tanh_ready"), sem("scored"), sem("collected"), sem("rounded_c"))
            block = part.enter_context(nc.Block())
            flat = edge_rows[:].rearrange("p b f -> p (b f)")

            @block.scalar
            def _(act):
                act.activation(elus[:], edge_rows[:], ACT.Exp).then_inc(exped, 1)
                for half in range(2):
                    act.wait_ge(hidden_ready, half + 1)
                    act.activation(hidden[:, 4 * half:4 * half + 4, :],
                                   m.ps_misc[:, half, :].rearrange("p (b e) -> p b e", b=4),
                                   ACT.Tanh, bias=fc_b[:, 0:1]).then_inc(tanh_ready, 1)
                act.wait_ge(collected, 1)
                act.copy(pick_hi[:], pick_all[:]).then_inc(rounded, 1)
                act.copy(picks[0:F, :], pick_all[0:F, :])

            @block.tensor
            def _(pe):
                for b in range(B):
                    pe.transpose(m.ps_score[0:F, b // 4, (b % 4) * P:(b % 4 + 1) * P],
                                 edge_rows[:, b, :], m.ident[:])
                pe.wait_ge(elued, 1)
                for b in range(B):
                    ins = pe.transpose(m.ps_score[0:F, b // 4, HALF + (b % 4) * P:HALF + (b % 4 + 1) * P],
                                       elus[:, b, :], m.ident[:])
                ins.then_inc(turned, 1)
                pe.wait_ge(copied, 2)
                for half in range(2):
                    pe.matmul(m.ps_misc[:, half, :], fc_w[0:F, 0, :],
                              elus_t[:, 4 * half:4 * half + 4, :].rearrange("p b e -> p (b e)"),
                              start=True, stop=True).then_inc(hidden_ready, 1)
                pe.wait_ge(tanh_ready, 2)
                for b in range(B):
                    pe.matmul(m.ps_turn[:, 0, b:b + 1], hidden[:, b, :], av[:], start=True, stop=True)
                    pe.matmul(m.ps_turn[:, 0, B + b:B + b + 1], rows_t[:, b, :], vecs[:, 2:3],
                              start=True, stop=True)
                pe.matmul(m.ps_turn[:, 1, :].rearrange("p (b e) -> p b e", b=B), av[:].to_broadcast([P, P]), hidden[:, :, 0:EN],
                          start=True, stop=True).then_inc(scored, 1)

            @block.vector
            def _(dve):
                link = Chain(dve, step)
                dve.wait_ge(exped, 1)
                link(dve.tensor_scalar(elus[:], elus[:], 1.0, -1.0, ALU.min, ALU.add))
                dve.tensor_tensor(elus[:], elus[:], edge_rows[:], ALU.max).then_inc(elued, 1)
                dve.wait_ge(turned, 1)
                dve.tensor_copy(rows_t[:].rearrange("p (a b) e -> p a (b e)", a=2),
                                m.ps_score[0:F, :, 0:HALF]).then_inc(copied, 1)
                dve.tensor_copy(elus_t[:].rearrange("p (a b) e -> p a (b e)", a=2),
                                m.ps_score[0:F, :, HALF:N]).then_inc(copied, 1)
                dve.wait_ge(scored, 1)
                link(dve.tensor_copy(pick_all[:, 0:B * F], flat))
                link(dve.tensor_copy(pick_all[:, B * F:B * F + 16], m.ps_turn[:, 0, 0:16]))
                link(dve.memset(pick_all[:, B * F + 16:], 1.0))
                dve.nop().then_inc(collected, 1)
                dve.wait_ge(rounded, 1)
                dve.tensor_tensor(picks[F:P, :], pick_all[F:P, :], pick_hi[F:P, :], ALU.subtract)
                edge_scores = m.ps_turn[:, 1, :].rearrange("p (b e) -> p b e", b=B)
                for t in range(NT):
                    ins = dve.tensor_tensor(table[:, t, :, :], edge_scores,
                                            node_mask[:, t, :].unsqueeze(1).to_broadcast([P, B, EN]),
                                            ALU.add)
                link(ins)
                dve.tensor_reduce(best[:], table[:], AX, ALU.max)

        with ExitStack() as part:
            def psb(n, shape, dt=F32):
                return part.enter_context(nc.sbuf_tensor(f"{name}_{n}", shape, dt))

            def sem(n):
                return nc.alloc_semaphore(f"{name}_{n}")

            pick = psb("pick", [P, N], F32R)
            beta = psb("beta", [P, NT, B])
            coef = psb("coef", [P, NT, B])
            diff = psb("diff", [P, 2, B * F])
            blend = psb("blend", [P, 2, B * F])
            blend_exp = psb("blend_exp", [P, 2, B * F])
            share = psb("share", [P, 2, B * F])
            step, picked, small_ready, rows_ready, rows_taken = (
                sem("stepd"), sem("picked"), sem("small_ready"), sem("rows_ready"), sem("rows_taken"))
            maxed = sem("maxed")
            exp_asked, exp_ready, blend_ready, blend_exped, share_ready, share_added = (
                sem("exp_asked"), sem("exp_ready_d"), sem("blend_ready"), sem("blend_exped"),
                sem("share_ready"), sem("share_added"))
            small = m.ps_misc[:, 0, 0:NT * 18].rearrange("p (t c) -> p t c", t=NT)
            block = part.enter_context(nc.Block())

            def slot_count(eng):
                return eng.value_load(slots_int[0:1, 0:1], min_val=1, max_val=EN)

            @block.tensor
            def _(pe):
                with pe.Fori(0, slot_count(pe)) as k:
                    pe.wait_ge(picked, k + 1)
                    for t in range(NT):
                        ins = pe.matmul(m.ps_misc[:, 0, t * 18:(t + 1) * 18], pick[:, t * P:(t + 1) * P],
                                        picks[:, B * F:], start=True, stop=True)
                    ins.then_inc(small_ready, 1)
                    for t in range(NT):
                        pe.wait_ge(rows_taken, k * NT + 1 + max(t - 3, 0))
                        pe.matmul(m.ps_score[:, t % 4 // 2, (t % 2) * HALF:(t % 2 + 1) * HALF],
                                  pick[:, t * P:(t + 1) * P], picks[:, 0:B * F],
                                  start=True, stop=True).then_inc(rows_ready, 1)

            @block.scalar
            def _(act):
                with act.Fori(0, slot_count(act)) as k:
                    act.wait_ge(exp_asked, 2 * k + 1)
                    act.activation(coef[:], coef[:], ACT.Exp).then_inc(exp_ready, 1)
                    act.wait_ge(exp_asked, 2 * k + 2)
                    act.activation(beta[:], beta[:], ACT.Exp, scale=-1.0).then_inc(exp_ready, 1)
                    for t in range(NT):
                        act.wait_ge(blend_ready, k * NT + t + 1)
                        act.activation(blend_exp[:, t % 2, :], blend[:, t % 2, :], ACT.Exp,
                                       bias=minus_one[:, 0:1]).then_inc(blend_exped, 1)

            @block.gpsimd
            def _(pool):
                rows = m.h[:].rearrange("p t b f -> p t (b f)")
                pool.wait_ge(step, 2)
                pool.nop().then_inc(share_added, 1)
                with pool.Fori(0, slot_count(pool)) as k:
                    for t in range(NT):
                        pool.wait_ge(share_ready, k * NT + t + 1)
                        pool.tensor_tensor(rows[:, t, :], rows[:, t, :], share[:, t % 2, :], ALU.add)\
                            .then_inc(share_added, 1)

            @block.vector
            def _(dve):
                dve.memset(minus_one[:], -1.0).then_inc(step, 1)
                dve.memset(m.h[:], 0.0).then_inc(step, 1)
                dve.memset(coef_sum[:], 0.0).then_inc(step, 1)
                dve.wait_ge(step, 3)
                dve.nop().then_inc(rows_taken, 1)
                steps = 6 + 2 * NT

                with dve.Fori(0, slot_count(dve)) as k:
                    link = Chain(dve, step, 3 + k * steps)
                    dve.tensor_scalar(pick[:], rank[:], 0.0, None, ALU.is_equal).then_inc(picked, 1)
                    dve.wait_ge(picked, k + 1)
                    link(dve.tensor_scalar(rank[:], rank[:], -1.0, None, ALU.add))
                    dve.wait_ge(small_ready, k + 1)
                    link(dve.tensor_tensor(coef[:], small[:, :, 0:B], best[:], ALU.subtract))
                    dve.scalar_tensor_tensor(out=coef[:], in0=coef[:], scalar=0.0,
                                             in1=linked[:].unsqueeze(2).to_broadcast([P, NT, B]),
                                             op0=ALU.min, op1=ALU.mult).then_inc(exp_asked, 1)
                    dve.tensor_tensor(beta[:], small[:, :, B:2 * B], gate[:], ALU.add).then_inc(exp_asked, 1)
                    dve.wait_ge(exp_ready, 2 * k + 1)
                    link(dve.tensor_tensor(coef[:], coef[:], small[:, :, 16:17].to_broadcast([P, NT, B]),
                                           ALU.mult))
                    link(dve.tensor_tensor(coef_sum[:], coef_sum[:], coef[:], ALU.add))
                    dve.wait_ge(exp_ready, 2 * k + 2)
                    link(dve.tensor_scalar(beta[:], beta[:], 1.0, None, ALU.add))
                    link(dve.reciprocal(beta[:], beta[:]))

                    def along(v, t):
                        return v[:, t, :].unsqueeze(2).to_broadcast([P, B, F])

                    def by_batch(v):
                        return v.rearrange("p (b f) -> p b f", b=B)

                    def blend_rows(t):
                        dve.wait_ge(rows_ready, k * NT + t + 1)
                        row = m.ps_score[:, t % 4 // 2, (t % 2) * HALF:(t % 2 + 1) * HALF]
                        d2 = diff[:, t % 2, :]
                        link(dve.tensor_tensor(d2, h1[:, t, :, :].rearrange("p b f -> p (b f)"), row,
                                               ALU.subtract))
                        link(dve.tensor_tensor(by_batch(d2), by_batch(d2), along(beta, t), ALU.mult))
                        dve.scalar_tensor_tensor(out=blend[:, t % 2, :], in0=row, scalar=1.0, in1=d2,
                                                 op0=ALU.add, op1=ALU.add).then_inc(blend_ready, 1)
                        dve.wait_ge(blend_ready, k * NT + t + 1)
                        dve.nop().then_inc(rows_taken, 1)

                    def add_share(t):
                        dve.wait_ge(blend_exped, k * NT + t + 1)
                        s = share[:, t % 2, :]
                        dve.wait_ge(share_added, k * NT + 1 + max(t - 1, 0))
                        dve.scalar_tensor_tensor(out=s, in0=blend_exp[:, t % 2, :], scalar=1.0,
                                                 in1=blend[:, t % 2, :], op0=ALU.min,
                                                 op1=ALU.max).then_inc(maxed, 1)
                        dve.wait_ge(maxed, k * NT + t + 1)
                        dve.tensor_tensor(by_batch(s), by_batch(s), along(coef, t), ALU.mult)\
                           .then_inc(share_ready, 1)

                    blend_rows(0)
                    for t in range(NT):
                        if t + 1 < NT:
                            blend_rows(t + 1)
                        add_share(t)

        with ExitStack() as part:
            def divide(dve, t, ps):
                return dve.tensor_scalar(neighbours[:, t, :, :].rearrange("p b f -> p (b f)"), ps,
                                         m.deg_inv[:, t:t + 1], None, ALU.mult)

            mix(nc, m, part, name + "_m", lambda t: neighbours[:, t, :, :].rearrange("p b f -> p (b f)"),
                divide)
        mix_pair(nc, m, name, neighbours, coef_sum, fc_w, fc_b, av)


def mix_pair(nc, m, name, neighbours, coef_sum, fc_w, fc_b, av):
    with ExitStack() as ctx:
        def sb(n, shape, dt=F32):
            return ctx.enter_context(nc.sbuf_tensor(f"{name}_{n}", shape, dt))

        def sem(n):
            return nc.alloc_semaphore(f"{name}_{n}")

        turned = sb("pair_t", [P, 2, 2, N])
        tanhs = sb("tanhs", [P, 2, 2, N])
        apart = sb("apart", [P, 2, N])
        first = sb("first", [P, NT, B])
        step, ready, turned_out, turned_in = sem("stepe"), sem("pair_ready"), sem("pair_out"), sem("pair_in")
        hid, tanhed, parted, scored, exped = (
            sem("pair_hid"), sem("pair_tanh"), sem("pair_apart"), sem("pair_scored"), sem("pair_exp"))
        sources = (neighbours, m.h)
        block = ctx.enter_context(nc.Block())

        @block.tensor
        def _(pe):
            pe.wait_ge(ready, 1)
            scores = m.ps_misc[:, 0, 0:NT * B].rearrange("p (t b) -> p t b", b=B)

            def score(b):
                pe.wait_ge(parted, b + 1)
                for t in range(NT):
                    ins = pe.matmul(scores[:, t, b:b + 1], apart[:, b % 2, t * P:(t + 1) * P], av[:],
                                    start=True, stop=True)
                ins.then_inc(scored, 1)

            for b in range(B):
                q = b // 2
                for s in range(2):
                    u = 2 * b + s
                    if b % 2 == 0:
                        for half in range(2):
                            i = 2 * (2 * q + s) + half
                            if i:
                                pe.wait_ge(turned_in, i)
                            for k in range(4):
                                t = half * 4 + k
                                ins = pe.transpose(m.ps_turn[:, 0, k * P:(k + 1) * P],
                                                   sources[s][:, t, 2 * q:2 * q + 2, :]
                                                   .rearrange("p a f -> p (a f)"), m.ident[:])
                            ins.then_inc(turned_out, 1)
                        pe.wait_ge(turned_in, 4 * q + 2 * s + 2)
                    if u >= 2:
                        pe.wait_ge(tanhed, u - 1)
                    for half in range(2):
                        cols = slice(half * HALF, (half + 1) * HALF)
                        ins = pe.matmul(m.ps_score[:, s, cols], fc_w[:, b % 2, :],
                                        turned[:, q % 2, s, cols], start=True, stop=True)
                    ins.then_inc(hid, 1)
                if b:
                    score(b - 1)
            score(B - 1)

        @block.scalar
        def _(act):
            for b in range(B):
                for s in range(2):
                    act.wait_ge(hid, 2 * b + s + 1)
                    if b >= 2:
                        act.wait_ge(parted, b - 1)
                    act.activation(tanhs[:, b % 2, s, :], m.ps_score[:, s, :], ACT.Tanh,
                                   bias=fc_b[:, 0:1]).then_inc(tanhed, 1)
            act.wait_ge(step, 4)
            act.activation(first[:], first[:], ACT.Exp, scale=-1.0).then_inc(exped, 1)

        @block.vector
        def _(dve):
            link = Chain(dve, step)
            link(dve.reciprocal(coef_sum[:], coef_sum[:]))
            h = m.h[:]
            link(dve.tensor_tensor(h, h, coef_sum[:].unsqueeze(3).to_broadcast([P, NT, B, F]), ALU.mult))
            link(dve.tensor_scalar(h, h, -1.0, None, ALU.add))
            dve.nop().then_inc(ready, 1)
            for b in range(B):
                if b % 2 == 0:
                    for i in range(4):
                        s, half = i // 2, i % 2
                        dve.wait_ge(turned_out, 2 * b + i + 1)
                        if b >= 4:
                            dve.wait_ge(hid, 2 * b - 4)
                        dve.tensor_copy(turned[:, b // 2 % 2, s, half * HALF:(half + 1) * HALF],
                                        m.ps_turn[:, 0, :]).then_inc(turned_in, 1)
                dve.wait_ge(tanhed, 2 * b + 2)
                if b >= 2:
                    dve.wait_ge(scored, b - 1)
                dve.tensor_tensor(apart[:, b % 2, :], tanhs[:, b % 2, 0, :], tanhs[:, b % 2, 1, :],
                                  ALU.subtract).then_inc(parted, 1)
            dve.wait_ge(scored, B)
            link(dve.tensor_copy(first[:].rearrange("p t b -> p (t b)"), m.ps_misc[:, 0, 0:NT * B]))
            link(dve.tensor_tensor(neighbours[:], neighbours[:], h, ALU.subtract))
            dve.wait_ge(exped, 1)
            link(dve.tensor_scalar(first[:], first[:], 1.0, None, ALU.add))
            link(dve.reciprocal(first[:], first[:]))
            link(dve.tensor_tensor(neighbours[:], neighbours[:],
                                   first[:].unsqueeze(3).to_broadcast([P, NT, B, F]), ALU.mult))
            link(dve.tensor_tensor(neighbours[:], neighbours[:], h, ALU.add))
            dve.tensor_tensor(m.x[:], m.x[:], neighbours[:], ALU.add)


def load(nc, m, d):
    with ExitStack() as ctx:
        adj = ctx.enter_context(nc.sbuf_tensor("adj_rows", [P, NT, N], F32))
        adj_cols = ctx.enter_context(nc.sbuf_tensor("adj_cols", [P, 2, N], F32))
        x_loaded = nc.alloc_semaphore("x_loaded")
        adj_loaded = [nc.alloc_semaphore(f"adj_loaded{t}") for t in range(NT)]
        cols_loaded = [nc.alloc_semaphore(f"cols_loaded{i}") for i in range(2)]
        cols_copied = nc.alloc_semaphore("cols_copied")
        zeroed = nc.alloc_semaphore("zeroed")
        summed = nc.alloc_semaphore("summed")
        block = ctx.enter_context(nc.Block())

        @block.sync
        def _(sp):
            sp.dma_start(m.x[:], d["x"]).then_inc(x_loaded, 16)
            for t in range(NT):
                sp.dma_start(adj[:, t, :], d["adj"][t * P:(t + 1) * P, :]).then_inc(adj_loaded[t], 16)
            sp.wait_ge(x_loaded, 16)

        @block.scalar
        def _(act):
            for t in range(NT):
                if t >= 2:
                    act.wait_ge(cols_copied, t - 1)
                act.dma_start(adj_cols[:, t % 2, :], d["adj_t"][t * P:(t + 1) * P, :])\
                   .then_inc(cols_loaded[t % 2], 16)
                act.wait_ge(cols_loaded[t % 2], 16 * (t // 2 + 1))
                act.copy(m.adj_t[:, t, :], adj_cols[:, t % 2, :]).then_inc(cols_copied, 1)

        @block.gpsimd
        def _(pool):
            pool.memset(m.ident[:], 0.0).then_inc(zeroed, 1)
            pool.wait_ge(zeroed, 1)
            pool.affine_select(out=m.ident[:], in_=m.ident[:], compare_op=ALU.not_equal, fill=1.0,
                               base=0, pattern=[[-1, P]], channel_multiplier=1)

        @block.vector
        def _(dve):
            for t in range(NT):
                dve.wait_ge(adj_loaded[t], 16)
                dve.tensor_scalar(m.mask[:, t, :], adj[:, t, :], 0.0, NEG, ALU.is_le, ALU.mult)
                dve.tensor_reduce(m.deg_inv[:, t:t + 1], adj[:, t, :], AX, ALU.add).then_inc(summed, 1)
            dve.wait_ge(summed, NT)
            dve.tensor_scalar(m.deg_inv[:], m.deg_inv[:], 1.0, None, ALU.max).then_inc(summed, 1)
            dve.wait_ge(summed, NT + 1)
            dve.reciprocal(m.deg_inv[:], m.deg_inv[:])


def store(nc, m, d):
    with ExitStack() as ctx:
        stored = nc.alloc_semaphore("stored")
        block = ctx.enter_context(nc.Block())

        @block.sync
        def _(sp):
            sp.dma_start(d["out"], m.x[:]).then_inc(stored, 16)
            sp.wait_ge(stored, 16)


def four_layers(nc, d, stages=None):
    with ExitStack() as ctx:
        m = Mem()

        def sb(n, shape, dt=F32):
            return ctx.enter_context(nc.sbuf_tensor(n, shape, dt))

        m.x = sb("x_sb", [P, NT, B, F])
        m.h = sb("h_sb", [P, NT, B, F])
        m.mask = sb("adj_mask", [P, NT, N], BF16)
        m.deg_inv = sb("deg_inv", [P, NT])
        m.ident = sb("ident", [P, P])
        m.ps_score = ctx.enter_context(nc.psum_tensor("ps_score", [P, 2, N], F32))
        m.ps_turn = ctx.enter_context(nc.psum_tensor("ps_turn", [P, 2, HALF], F32))
        m.ps_misc = ctx.enter_context(nc.psum_tensor("ps_misc", [P, 2, HALF], F32))
        with ExitStack() as graph:
            m.adj_t = graph.enter_context(nc.sbuf_tensor("adj_t_sb", [P, NT, N], F32R))
            with fresh_semaphores(nc):
                load(nc, m, d)
            for k, layer in enumerate((hypergraph_layer, graph_attention_layer, graph_layer)):
                if stages is None or k in stages:
                    with fresh_semaphores(nc):
                        layer_norm(nc, m, f"ln{k}")
                        layer(nc, m, d)
        if stages is None or 3 in stages:
            with fresh_semaphores(nc):
                layer_norm(nc, m, "ln3")
                hidden_attention(nc, m, d)
            with fresh_semaphores(nc):
                out_attention(nc, m, d)
        store(nc, m, d)


_SHAPES = {
    "x": (P, NT, B, F), "adj": (N, N), "adj_t": (N, N), "wh_t": (HEADS, HID, F),
    "L3_gnn_Wh": (HEADS, F, HID), "L3_gnn_W_out": (HEADS * HID, F), "bh_t": (HID, HEADS),
    "L3_gnn_b_out": (F,), "L2_w": (2, F, F), "L1_gnn_W": (F, F), "l1_wt": (F, F),
    "l1_a": (F, 2), "h_rows": (P, NT, F), "h_t": (F, N), "L0_gnn_W": (F, F),
    "l0_wt": (F, F), "L0_gnn_W_ind": (F, F), "l0_vecs": (F, 3),
    "L0_gnn_fcW": (F, 2 * F), "L0_gnn_fcb": (2 * F,), "L0_gnn_av": (2 * F,),
}


def lay_out(inputs, np):
    v = {k: np.asarray(a) for k, a in inputs.items()}
    v["x"] = v["x"].reshape(B, NT, P, F).transpose(2, 1, 0, 3)
    v["adj_t"] = v["adj"].T
    v["wh_t"] = v["L3_gnn_Wh"].transpose(0, 2, 1)
    v["L2_w"] = v["L2_gnn_net_params"].reshape(2, F, F)
    v["l1_wt"] = v["L1_gnn_W"].T
    v["l1_a"] = v["L1_gnn_a"].reshape(2, F).T
    v["l0_wt"] = v["L0_gnn_W"].T
    v["bh_t"] = v["L3_gnn_bh"].T
    v["h_rows"] = v["L0_gnn_H"].reshape(NT, P, F).transpose(1, 0, 2)
    v["l0_vecs"] = np.stack([v["L0_gnn_a_node"], v["L0_gnn_a_gn"], v["L0_gnn_a_ge"]], axis=1)
    v["h_t"] = v["L0_gnn_H"].T
    return {k: np.ascontiguousarray(v[k]) for k in _SHAPES}


def kernel(**inputs):
    import numpy as np
    import concourse.bacc as bacc
    from concourse.bass_utils import run_bass_kernel_spmd

    arrays = {f"in_{k}": a for k, a in lay_out(inputs, np).items()}
    nc = bacc.Bacc("TRN2", target_bir_lowering=False, num_devices=1)
    d = {k: nc.dram_tensor(f"in_{k}", shape, F32, kind="ExternalInput").ap()
         for k, shape in _SHAPES.items()}
    d["out"] = nc.dram_tensor("out_x", (P, NT, B, F), F32, kind="ExternalOutput").ap()
    four_layers(nc, d)
    result = run_bass_kernel_spmd(nc, [arrays], core_ids=[0])
    out = np.asarray(result.results[0]["out_x"])
    return np.ascontiguousarray(out.transpose(2, 1, 0, 3)).reshape(B, N, F)
```

```python
from contextlib import ExitStack, contextmanager

import concourse.bass as bass
from concourse import mybir

ALU = mybir.AluOpType
ACT = mybir.ActivationFunctionType
F32 = mybir.dt.float32
F32R = mybir.dt.float32r
BF16 = mybir.dt.bfloat16
AX = mybir.AxisListType.X

P = 128
B, N, F = 8, 1024, 64
NT = N // P
HALF = N // 2
QUARTER = N // 4
HEADS, HID = 8, 128
NEG = -2.0 ** 53
HUGE = 3.0e38
EPS = 1.0e-5


class Chain:

    def __init__(self, eng, sem, base=0):
        self.eng, self.sem, self.base, self.n = eng, sem, base, 0

    def __call__(self, ins):
        self.n += 1
        ins.then_inc(self.sem, 1)
        self.eng.wait_ge(self.sem, self.base + self.n)


@contextmanager
def fresh_semaphores(nc):
    before = nc.snapshot_sems()
    yield
    nc.clear_and_free_semaphores(nc.allocated_since(before))
    nc.all_engine_barrier()


class Mem:
    pass


def layer_norm(nc, m, name, g):
    with ExitStack() as ctx:
        rows = B * NT
        mean = ctx.enter_context(nc.sbuf_tensor(name + "_mean", [P, rows], F32))
        var = ctx.enter_context(nc.sbuf_tensor(name + "_var", [P, rows], F32))
        sq = ctx.enter_context(nc.sbuf_tensor(name + "_sq", [P, rows, F], F32))
        step = nc.alloc_semaphore(name + "_step")
        centred = nc.alloc_semaphore(name + "_centred")
        squared = nc.alloc_semaphore(name + "_squared")
        var_ready = nc.alloc_semaphore(name + "_var_ready")
        std_ready = nc.alloc_semaphore(name + "_std_ready")
        x = m.x[:].rearrange("p t b f -> p (t b) f")
        h = m.h[:].rearrange("p t b f -> p (t b) f")
        parts = 4
        rp = rows // parts
        cleared = nc.alloc_semaphore(name + "_cleared")
        loaded = nc.alloc_semaphore(name + "_loaded")
        block = ctx.enter_context(nc.Block())

        @block.gpsimd
        def _(pool):
            for w in g.clear:
                pool.memset(w[:], 0.0).then_inc(cleared, 1)

        @block.sync
        def _(sp):
            sp.wait_ge(cleared, len(g.clear))
            for place, src in g.loads:
                sp.dma_start(place, src).then_inc(loaded, 16)
            sp.wait_ge(loaded, 16 * len(g.loads))

        @block.vector
        def _(dve):
            link = Chain(dve, step)
            for q in range(parts):
                r = slice(q * rp, (q + 1) * rp)
                link(dve.tensor_reduce(mean[:, r], x[:, r, :], AX, ALU.add))
                link(dve.tensor_scalar(mean[:, r], mean[:, r], 1.0 / F, None, ALU.mult))
                dve.tensor_tensor(h[:, r, :], x[:, r, :],
                                  mean[:, r].unsqueeze(2).to_broadcast([P, rp, F]),
                                  ALU.subtract).then_inc(centred, 1)
            for q in range(parts):
                r = slice(q * rp, (q + 1) * rp)
                dve.wait_ge(squared, q + 1)
                ins = dve.tensor_reduce(var[:, r], sq[:, r, :], AX, ALU.add)
                link(ins)
            dve.tensor_scalar(var[:], var[:], 1.0 / F, EPS, ALU.mult, ALU.add).then_inc(var_ready, 1)
            dve.wait_ge(std_ready, 1)
            link(dve.reciprocal(var[:], var[:]))
            dve.wait_ge(centred, parts)
            dve.scalar_tensor_tensor(out=h, in0=h, scalar=0.0,
                                     in1=var[:].unsqueeze(2).to_broadcast([P, rows, F]),
                                     op0=ALU.max, op1=ALU.mult)

        @block.scalar
        def _(act):
            for q in range(parts):
                r = slice(q * rp, (q + 1) * rp)
                act.wait_ge(centred, q + 1)
                act.activation(sq[:, r, :], h[:, r, :], ACT.Square).then_inc(squared, 1)
            act.wait_ge(var_ready, 1)
            act.activation(var[:], var[:], ACT.Sqrt).then_inc(std_ready, 1)


def attention_pipeline(nc, m, ctx, name, vector_tiles):
    a = Mem()
    a.vector_tiles = vector_tiles

    def sb(n, shape, dt=F32):
        return ctx.enter_context(nc.sbuf_tensor(f"{name}_{n}", shape, dt))

    def sem(n):
        return nc.alloc_semaphore(f"{name}_{n}")

    a.masked = sb("masked", [P, 2, N])
    a.weights = sb("weights", [P, 3, N])
    a.weights_t = sb("weights_t", [P, NT, N])
    a.neg_max = sb("neg_max", [P, 2, NT])
    a.row_sum = sb("row_sum", [P, 2, NT])
    a.row_inv = sb("row_inv", [P, 2, NT])
    a.inv_cols = sb("inv_cols", [P, HALF])
    a.z = sb("z", [P, 2, HALF])
    a.scores_ready = sem("scores_ready")
    a.tile_free = sem("tile_free")
    a.masked_ready = sem("masked_ready")
    a.exp_ready = sem("exp_ready")
    a.turned = [sem("turned0"), sem("turned1")]
    a.copied = [sem("copied0"), sem("copied1")]
    a.inv_ready = sem("inv_ready")
    a.inv_turned = sem("inv_turned")
    a.inv_copied = sem("inv_copied")
    a.z_ready = sem("z_ready")
    a.z_normed = sem("z_normed")
    return a



def pe_turn(pe, m, a, g, t, first):
    pe.wait_ge(a.exp_ready, g * NT + t + 1)
    for half in range(2):
        if not (first and t == 0):
            pe.wait_ge(a.copied[half], g * NT + t)
        for k in range(4):
            j = half * 4 + k
            ins = pe.transpose(m.ps_turn[:, half, k * P:(k + 1) * P],
                               a.weights[:, t % 3, j * P:(j + 1) * P], m.ident[:])
        ins.then_inc(a.turned[half], 1)


def pe_inverse_rows(pe, m, a, g, par):
    pe.wait_ge(a.inv_ready, g + 1)
    for t in range(NT):
        side, col = t // 2 % 2, t // 4 * QUARTER + t % 2 * P
        ins = pe.matmul(m.ps_misc[side * F:(side + 1) * F, 1, col:col + P],
                        a.row_inv[:, par, t:t + 1].to_broadcast([P, F]), m.ident[:],
                        start=True, stop=True)
    ins.then_inc(a.inv_turned, 1)


def pe_values(pe, m, a, g, half, js, values):
    if js[0] == 0:
        for copied in a.copied:
            pe.wait_ge(copied, g * NT + 4 * half + 4)
    for j in js:
        for side in range(2):
            i = half * HALF + side * QUARTER
            ins = pe.matmul(m.ps_misc[side * F:(side + 1) * F, 0, half * QUARTER:(half + 1) * QUARTER],
                            values(j), a.weights_t[:, j, i:i + QUARTER],
                            start=(j == 0), stop=(j == NT - 1))
    if half == 1 and js[-1] == NT - 1:
        ins.then_inc(a.z_ready, 1)


def z_rows(v, side):
    return v.rearrange("p (h s r) f -> p s h r f", h=2, s=2)[:, side, :, :, :]


def turned_rows(ps, side):
    return ps.rearrange("p (h r s f) -> p s h r f", h=2, r=2, s=2)[:, side, :, :, :]


def dve_mask(dve, m, a, g, par, t, scores, mask, first, alone=False):
    dve.wait_ge(a.scores_ready, g * NT + t + 1)
    if not (first and t < 2):
        dve.wait_ge(a.exp_ready, g * NT + t - 1)
    if alone:
        dve.nop().then_inc(a.tile_free, 1)
    dve.tensor_tensor_reduce(a.masked[:, t % 2, :], scores, mask, -1.0, HUGE, ALU.add, ALU.min,
                             a.neg_max[:, par, t:t + 1]).then_inc(a.masked_ready, 1)


def dve_copy_turned(dve, m, a, g, t):
    if t not in a.vector_tiles:
        return
    dve.wait_ge(a.turned[1], g * NT + t + 1)
    dve.tensor_copy(a.weights_t[:, 4:8, t * P:(t + 1) * P],
                    m.ps_turn[:, 1, :].rearrange("p (k i) -> p k i", k=4)).then_inc(a.copied[1], 1)


def dve_inverse(dve, m, a, g, par):
    dve.wait_ge(a.exp_ready, g * NT + NT)
    dve.reciprocal(a.row_inv[:, par, :], a.row_sum[:, par, :]).then_inc(a.inv_ready, 1)


def dve_normalise(dve, m, a, g, par):
    dve.wait_ge(a.z_ready, g + 1)
    dve.wait_ge(a.inv_copied, g + 1)
    dve.tensor_tensor(a.z[:, par, :], m.ps_misc[:, 0, :], a.inv_cols[:], ALU.mult)\
       .then_inc(a.z_normed, 1)


def act_exp(act, m, a, g, par, t, first):
    act.wait_ge(a.masked_ready, g * NT + t + 1)
    if not (first and t < 3):
        act.wait_ge(a.turned[1], g * NT + t - 2)
    act.activation(a.weights[:, t % 3, :], a.masked[:, t % 2, :], ACT.Exp, scale=-1.0,
                   bias=a.neg_max[:, par, t:t + 1],
                   accum_out=a.row_sum[:, par, t:t + 1]).then_inc(a.exp_ready, 1)


def act_copy_turned(act, m, a, g, t):
    act.wait_ge(a.turned[0], g * NT + t + 1)
    act.copy(a.weights_t[:, 0:4, t * P:(t + 1) * P],
             m.ps_turn[:, 0, :].rearrange("p (k i) -> p k i", k=4)).then_inc(a.copied[0], 1)
    if t not in a.vector_tiles:
        act.wait_ge(a.turned[1], g * NT + t + 1)
        act.copy(a.weights_t[:, 4:8, t * P:(t + 1) * P],
                 m.ps_turn[:, 1, :].rearrange("p (k i) -> p k i", k=4)).then_inc(a.copied[1], 1)


def act_copy_inverse(act, m, a, g, par):
    act.wait_ge(a.inv_turned, g + 1)
    act.copy(a.inv_cols[:], m.ps_misc[:, 1, :]).then_inc(a.inv_copied, 1)


def split(nc, ctx, name, shape):
    return (ctx.enter_context(nc.sbuf_tensor(name + "_hi", shape, F32R)),
            ctx.enter_context(nc.sbuf_tensor(name + "_lo", shape, F32R)))


def hidden_attention(nc, m, w):
    name = "hid"
    UNITS = 2 * HEADS

    with ExitStack() as ctx:
        a = attention_pipeline(nc, m, ctx, name, (0, 1, 3, 5, 7))

        def sb(n, shape, dt=F32):
            return ctx.enter_context(nc.sbuf_tensor(f"{name}_{n}", shape, dt))

        def sem(n):
            return nc.alloc_semaphore(f"{name}_{n}")

        wh_t, wz, wo, bias = w.wh_t, w.wz, w.wo, w.bias
        gram = split(nc, ctx, name + "_gram", [P, HEADS, P])
        x2 = sb("x2", [P, 2, NT, 2, F])
        xs = sb("xs", [P, 2, N], F32R)
        mask = sb("mask", [P, 2, NT, N], BF16)
        y = [split(nc, ctx, f"{name}_y{i}", [P, N]) for i in range(2)]
        ones = sb("ones", [P, P], F32R)
        zero_row = sb("zero_row", [P, NT])
        scratch = sb("scratch", [P, N], F32R)
        hidden = sb("hidden", [P, N])

        gram_ready = sem("gram_ready")
        gram_hi = sem("gram_hi")
        gram_split = sem("gram_split")
        staged = sem("staged")
        x_turned = sem("x_turned")
        x_hi_ready = sem("x_hi_ready")
        x_split = sem("x_split")
        sums_ready = sem("sums_ready")
        zeros_ready = sem("zeros_ready")
        mask_ready = sem("mask_ready")
        step = sem("step")
        y_ready = sem("y_ready")
        y_hi = sem("y_hi")
        y_split = sem("y_split")
        hidden_ready = sem("hidden_ready")
        hidden_biased = sem("hidden_biased")
        hidden_done = sem("hidden_done")
        out_ready = sem("out_ready")
        out_added = sem("out_added")

        block = ctx.enter_context(nc.Block())

        @block.tensor
        def _(pe):
            for h in range(HEADS):
                if h > 1:
                    pe.wait_ge(gram_split, h - 1)
                w2 = wh_t[:, h, :, :].rearrange("p a f -> p (a f)")
                pe.matmul(m.ps_misc[:, h % 2, 0:P], w2, w2, start=True, stop=True).then_inc(gram_ready, 1)
            pe.wait_ge(gram_split, HEADS)

            def turn_next(n, side, part):
                pe.wait_ge(staged, n + 1)
                for k in range(4):
                    t = 4 * part + k
                    ins = pe.transpose(m.ps_misc[:, 1, k * P:(k + 1) * P],
                                       x2[:, side, t, :, :].rearrange("p a f -> p (a f)"),
                                       m.ident[:])
                ins.then_inc(x_turned, 1)

            def sum_next(n, side, half):
                if half == 0:
                    pe.wait_ge(x_split, 4 * n + 4)
                pe.matmul(m.ps_misc[:, 1, :], ones[:],
                          xs[:, side, half * HALF:(half + 1) * HALF],
                          start=True, stop=True).then_inc(sums_ready, 1)

            def project(g, v):
                for half in range(2):
                    for k in range(2):
                        ins = pe.matmul(m.ps_misc[:, half, :], gram[k][:, v % HEADS, :],
                                        xs[:, v // HEADS % 2, half * HALF:(half + 1) * HALF],
                                        start=(k == 0), stop=(k == 1))
                ins.then_inc(y_ready, 1)

            def score(g, v, t):
                if t == 0:
                    pe.wait_ge(y_split, g + 1)
                if not (v == 0 and t < 2):
                    pe.wait_ge(a.masked_ready, g * NT + t - 1)
                for half in range(2):
                    for k in range(2):
                        ins = pe.matmul(m.ps_score[:, t % 2, half * HALF:(half + 1) * HALF],
                                        xs[:, v // HEADS % 2, t * P:(t + 1) * P],
                                        y[v % 2][k][:, half * HALF:(half + 1) * HALF],
                                        start=(k == 0), stop=(k == 1))
                ins.then_inc(a.scores_ready, 1)

            def head_out(g, v):
                pe.wait_ge(a.z_normed, g + 1)
                for k in range(4):
                    half, side = k // 2, k % 2
                    i = half * HALF + side * QUARTER
                    ins = pe.matmul(m.ps_misc[:, half, i % HALF:i % HALF + QUARTER],
                                    wz[:, side, v % HEADS, :],
                                    a.z[:, v % 2, half * QUARTER:(half + 1) * QUARTER],
                                    start=True, stop=True)
                ins.then_inc(hidden_ready, 1)

            def project_out(g, v):
                pe.wait_ge(hidden_done, g + 1)
                for half in range(2):
                    ins = pe.matmul(m.ps_misc[half * F:(half + 1) * F, 1, :], wo[:, v % HEADS, :],
                                    hidden[:, half * HALF:(half + 1) * HALF],
                                    start=True, stop=True)
                ins.then_inc(out_ready, 1)

            def rows(v):
                return lambda j: x2[:, v // HEADS, j, 0, :]

            for part in range(2):
                if part:
                    pe.wait_ge(x_split, 2)
                turn_next(0, 0, part)
            for half in range(2):
                if half:
                    pe.wait_ge(zeros_ready, 1)
                sum_next(0, 0, half)
            pe.wait_ge(zeros_ready, 2)

            project(0, 0)
            score(0, 0, 0)
            score(0, 0, 1)
            with pe.Fori(0, B // 2) as bb:
                base = bb * UNITS
                for v in range(UNITS):
                    g, u = base + v, v % HEADS
                    n = bb * 2 + v // HEADS + 1
                    side = (v // HEADS + 1) % 2
                    if u in (1, 2):
                        turn_next(n, side, u - 1)
                    if u in (3, 4):
                        sum_next(n, side, u - 3)
                    for t in range(NT):
                        if t + 2 < NT:
                            score(g, v, t + 2)
                        if v and t < 4:
                            pe_values(pe, m, a, g - 1, 1, range(2 * t, 2 * t + 2), rows(v - 1))
                        pe_turn(pe, m, a, g, t, v == 0)
                        if t == 2:
                            if u in (1, 2):
                                pe.wait_ge(x_split, 4 * n + 2 * u)
                            if u in (3, 4):
                                pe.wait_ge(zeros_ready, 2 * n + u - 2)
                            if v >= 2:
                                project_out(g - 2, v - 2)
                        if v and t == 3:
                            if v >= 2:
                                pe.wait_ge(out_added, g - 1)
                            pe_inverse_rows(pe, m, a, g - 1, (v - 1) % 2)
                        if t == 5:
                            if v:
                                pe.wait_ge(a.z_normed, g)
                            project(g + 1, v + 1)
                    if v:
                        pe.wait_ge(y_split, g + 2)
                        head_out(g - 1, v - 1)
                    score(g + 1, v + 1, 0)
                    score(g + 1, v + 1, 1)
                    if v:
                        pe.wait_ge(hidden_biased, g)
                    pe_values(pe, m, a, g, 0, range(NT), rows(v))
                g = base + UNITS - 1
                pe_values(pe, m, a, g, 1, range(NT), rows(UNITS - 1))
                project_out(g - 1, UNITS - 2)
                pe.wait_ge(out_added, g)
                pe_inverse_rows(pe, m, a, g, 1)
                head_out(g, UNITS - 1)
                project_out(g, UNITS - 1)
                pe.wait_ge(out_added, g + 1)

        @block.vector
        def _(dve):
            dve.memset(hidden[:, 0:P], 1.0).then_inc(step, 1)
            dve.wait_ge(step, 1)
            dve.tensor_copy(ones[:], hidden[:, 0:P]).then_inc(step, 1)
            for h in range(HEADS):
                dve.wait_ge(gram_hi, h + 1)
                dve.tensor_tensor(gram[1][:, h, :], m.ps_misc[:, h % 2, 0:P], gram[0][:, h, :],
                                  ALU.subtract).then_inc(gram_split, 1)
            setup_steps = 2
            per_batch = 4

            def stage_next(n, side, b):
                link = Chain(dve, step, setup_steps + per_batch * n)
                link(dve.tensor_copy(x2[:, side, :, 0, :], m.h[:, :, b, :]))
                link(dve.tensor_copy(x2[:, side, :, 1, :], x2[:, side, :, 0, :]))
                dve.nop().then_inc(staged, 1)
                link(dve.tensor_reduce(zero_row[:], x2[:, side, :, 0, :], AX, ALU.max))
                link(dve.tensor_scalar(zero_row[:], zero_row[:], 0.0, NEG, ALU.is_equal, ALU.mult))

            def split_next(n, side, part):
                dve.wait_ge(x_hi_ready, 2 * n + part + 1)
                cols = slice(part * HALF, (part + 1) * HALF)
                dve.tensor_tensor(xs[F:P, side, cols], m.ps_misc[F:P, 1, :], scratch[F:P, cols],
                                  ALU.subtract).then_inc(x_split, 1)

            def find_zeros(n, half):
                dve.wait_ge(sums_ready, 2 * n + half + 1)
                dve.tensor_scalar(scratch[:, half * HALF:(half + 1) * HALF], m.ps_misc[:, 1, :], 0.0,
                                  NEG, ALU.is_equal, ALU.mult).then_inc(zeros_ready, 1)

            def mask_next(n, side, tiles):
                if tiles[0] == 0:
                    dve.wait_ge(zeros_ready, 2 * n + 2)
                for t in tiles:
                    ins = dve.scalar_tensor_tensor(out=mask[:, side, t, :], in0=scratch[:],
                                                   scalar=zero_row[:, t:t + 1], in1=m.mask[:, t, :],
                                                   op0=ALU.min, op1=ALU.min)
                if tiles[-1] == NT - 1:
                    ins.then_inc(mask_ready, 1)

            def split_y(g, v):
                dve.wait_ge(y_hi, g + 1)
                dve.tensor_tensor(y[v % 2][1][:], m.ps_misc[:].rearrange("p a n -> p (a n)"),
                                  y[v % 2][0][:], ALU.subtract).then_inc(y_split, 1)

            def leaky(g):
                dve.wait_ge(hidden_biased, g + 1)
                dve.scalar_tensor_tensor(out=hidden[:], in0=hidden[:], scalar=0.01, in1=hidden[:],
                                         op0=ALU.mult, op1=ALU.max).then_inc(hidden_done, 1)

            def add_out(b, g, u):
                dve.wait_ge(out_ready, g + 1)
                out, share = m.h[:, :, b, :], m.ps_misc[:, 1, :].rearrange("p (t f) -> p t f", f=F)
                if u == 0:
                    dve.nop().then_inc(a.tile_free, 1)
                    dve.tensor_copy(out, share).then_inc(out_added, 1)
                else:
                    dve.wait_ge(out_added, g)
                    dve.tensor_tensor(out, out, share, ALU.add).then_inc(out_added, 1)

            stage_next(0, 0, 0)
            split_next(0, 0, 0)
            split_next(0, 0, 1)
            find_zeros(0, 0)
            find_zeros(0, 1)
            mask_next(0, 0, range(NT))

            def masked(bb, g, v, t):
                if t == 0 and v % HEADS == 0:
                    dve.wait_ge(mask_ready, bb * 2 + v // HEADS + 1)
                dve_mask(dve, m, a, g, v % 2, t, m.ps_score[:, t % 2, :],
                         mask[:, v // HEADS % 2, t, :], v == 0, True)

            split_y(0, 0)
            masked(0, 0, 0, 0)
            masked(0, 0, 0, 1)
            with dve.Fori(0, B // 2) as bb:
                base = bb * UNITS
                for v in range(UNITS):
                    g, u = base + v, v % HEADS
                    n = bb * 2 + v // HEADS + 1
                    side = (v // HEADS + 1) % 2
                    for t in range(NT):
                        if t + 2 < NT:
                            masked(bb, g, v, t + 2)
                        if v and t == 4:
                            dve_normalise(dve, m, a, g - 1, (v - 1) % 2)
                        dve_copy_turned(dve, m, a, g, t)
                        if t == 0 and u in (1, 2):
                            split_next(n, side, u - 1)
                        if t == 0 and u in (3, 4):
                            find_zeros(n, u - 3)
                        if v >= 2 and t == 1:
                            leaky(g - 2)
                        if v >= 2 and t == 2:
                            add_out(bb * 2 + (v - 2) // HEADS, g - 2, (v - 2) % HEADS)
                        if t in (0, 3, 5) and u >= 5:
                            k = 3 * (u - 5) + (0, 3, 5).index(t)
                            if k < NT:
                                mask_next(n, side, (k,))
                        if u == 0 and t == 5:
                            stage_next(n, side, n % B)
                        if t == 6:
                            split_y(g + 1, v + 1)
                    dve_inverse(dve, m, a, g, v % 2)
                    masked(bb, g + 1, v + 1, 0)
                    masked(bb, g + 1, v + 1, 1)
                g = base + UNITS - 1
                leaky(g - 1)
                add_out(bb * 2 + 1, g - 1, HEADS - 2)
                dve_normalise(dve, m, a, g, 1)
                leaky(g)
                add_out(bb * 2 + 1, g, HEADS - 1)

        @block.scalar
        def _(act):
            for h in range(HEADS):
                act.wait_ge(gram_ready, h + 1)
                act.copy(gram[0][:, h, :], m.ps_misc[:, h % 2, 0:P]).then_inc(gram_hi, 1)

            def round_next(n, side, part):
                act.wait_ge(x_turned, 2 * n + part + 1)
                cols = slice(part * HALF, (part + 1) * HALF)
                act.copy(scratch[:, cols], m.ps_misc[:, 1, :]).then_inc(x_hi_ready, 1)
                act.copy(xs[0:F, side, cols], m.ps_misc[0:F, 1, :]).then_inc(x_split, 1)

            def round_y(g, v):
                act.wait_ge(y_ready, g + 1)
                act.copy(y[v % 2][0][:], m.ps_misc[:].rearrange("p a n -> p (a n)")).then_inc(y_hi, 1)

            def add_bias(g, v):
                act.wait_ge(hidden_ready, g + 1)
                act.activation(hidden[:], m.ps_misc[:].rearrange("p a n -> p (a n)"), ACT.Identity,
                               bias=bias[:, v % HEADS:v % HEADS + 1]).then_inc(hidden_biased, 1)

            round_next(0, 0, 0)
            round_next(0, 0, 1)
            round_y(0, 0)
            with act.Fori(0, B // 2) as bb:
                base = bb * UNITS
                for v in range(UNITS):
                    g, u = base + v, v % HEADS
                    n = bb * 2 + v // HEADS + 1
                    side = (v // HEADS + 1) % 2
                    for t in range(NT):
                        act_exp(act, m, a, g, v % 2, t, v == 0)
                        if t >= 1:
                            act_copy_turned(act, m, a, g, t - 1)
                        if t == 0 and u in (1, 2):
                            round_next(n, side, u - 1)
                        if v and t == 4:
                            act_copy_inverse(act, m, a, g - 1, (v - 1) % 2)
                        if t == 6:
                            round_y(g + 1, v + 1)
                    act_copy_turned(act, m, a, g, NT - 1)
                    if v:
                        add_bias(g - 1, v - 1)
                g = base + UNITS - 1
                act_copy_inverse(act, m, a, g, 1)
                add_bias(g, UNITS - 1)


def out_attention(nc, m, d):
    name = "out"
    with ExitStack() as ctx:
        a = attention_pipeline(nc, m, ctx, name, ())

        def sb(n, shape, dt=F32):
            return ctx.enter_context(nc.sbuf_tensor(f"{name}_{n}", shape, dt))

        def sem(n):
            return nc.alloc_semaphore(f"{name}_{n}")

        x2 = sb("x2", [P, 3, NT, 2, F])
        x_hi = sb("x_hi", [P, 2, N], F32R)
        x_lo = sb("x_lo", [P, 2, N], F32R)
        xs = sb("xs", [P, 2, N], F32R)
        row_squares = sb("row_squares", [P, NT, F])
        zero_row = sb("zero_row", [P, 2, NT])
        zero_col = sb("zero_col", [P, 2, N])
        mask = sb("mask", [P, 2, N])
        bias = sb("bias", [P, 1])

        loaded = sem("loaded")
        step = sem("step")
        rows_ready = sem("rows_ready")
        rows_copied = sem("rows_copied")
        rows_squared = sem("rows_squared")
        rows_found = sem("rows_found")
        x_turned = sem("x_turned")
        x_hi_ready = sem("x_hi_ready")
        x_lo_ready = sem("x_lo_ready")
        xs_ready = sem("xs_ready")
        zeros_spread = sem("zeros_spread")
        zeros_ready = sem("zeros_ready")
        activated = sem("activated")
        out_turned = sem("out_turned")
        added = sem("added")
        block = ctx.enter_context(nc.Block())

        @block.sync
        def _(sp):
            for k in range(2):
                sp.dma_start(bias[k * F:(k + 1) * F, :],
                             d["L3_gnn_b_out"].rearrange("(f a) -> f a", a=1)).then_inc(loaded, 16)

        @block.tensor
        def _(pe):
            def rows(u):
                for c in range(NT // 2):
                    for k in range(2):
                        ins = pe.matmul(m.ps_misc[k * F:(k + 1) * F, 1, c * P:(c + 1) * P],
                                        m.h[:, 2 * c + k, u, :], m.ident[:], start=True, stop=True)
                ins.then_inc(rows_ready, 1)

            def turn_rows(u, half):
                if half == 0:
                    pe.wait_ge(rows_copied, 2 * u + 2)
                else:
                    pe.wait_ge(x_lo_ready, 2 * u + 1)
                for k in range(4):
                    ins = pe.transpose(m.ps_misc[:, 1, k * P:(k + 1) * P],
                                       x2[:, u % 3, 4 * half + k, :, :].rearrange("p a f -> p (a f)"),
                                       m.ident[:])
                ins.then_inc(x_turned, 1)

            def spread_zeros(u, half):
                if half == 0:
                    pe.wait_ge(rows_found, u + 1)
                else:
                    pe.wait_ge(zeros_ready, 2 * u + 1)
                for k in range(4):
                    t = 4 * half + k
                    ins = pe.matmul(m.ps_misc[:, 1, k * P:(k + 1) * P],
                                    zero_row[:, u % 2, t:t + 1].to_broadcast([P, P]), m.ident[:],
                                    start=True, stop=True)
                ins.then_inc(zeros_spread, 1)

            def score(u, t):
                if t == 0:
                    pe.wait_ge(xs_ready, 4 * u + 4)
                    pe.wait_ge(x_lo_ready, 2 * u + 2)
                if not (u == 0 and t < 2):
                    pe.wait_ge(a.masked_ready, u * NT + t - 1)
                for half in range(2):
                    for k, part in enumerate((x_hi, x_lo)):
                        ins = pe.matmul(m.ps_score[:, t % 2, half * HALF:(half + 1) * HALF],
                                        xs[:, u % 2, t * P:(t + 1) * P],
                                        part[:, u % 2, half * HALF:(half + 1) * HALF],
                                        start=(k == 0), stop=(k == 1))
                ins.then_inc(a.scores_ready, 1)

            def turn_out(u):
                pe.wait_ge(activated, u + 1)
                for c in range(NT // 2):
                    ins = pe.transpose(m.ps_misc[:, 1, c * P:(c + 1) * P],
                                       a.z[:, u % 2, c * P:(c + 1) * P], m.ident[:])
                ins.then_inc(out_turned, 1)

            def values(u):
                return lambda j: x2[:, u % 3, j, 0, :]

            rows(0)
            for half in range(2):
                turn_rows(0, half)
            pe.wait_ge(x_lo_ready, 2)
            for half in range(2):
                spread_zeros(0, half)
            score(0, 0)
            score(0, 1)
            for u in range(B):
                more = u + 1 < B
                for t in range(NT):
                    if t + 2 < NT:
                        score(u, t + 2)
                    if u and t < 4:
                        pe_values(pe, m, a, u - 1, 1, range(2 * t, 2 * t + 2), values(u - 1))
                    pe_turn(pe, m, a, u, t, u == 0)
                    if more and t == 0:
                        if u >= 2:
                            pe.wait_ge(added, u - 1)
                        else:
                            pe.wait_ge(zeros_ready, 2 * u + 2)
                        rows(u + 1)
                    if more and t in (1, 2):
                        turn_rows(u + 1, t - 1)
                    if u and t == 3:
                        if more:
                            pe.wait_ge(x_lo_ready, 2 * u + 4)
                        else:
                            pe.wait_ge(added, u - 1)
                        pe_inverse_rows(pe, m, a, u - 1, (u - 1) % 2)
                    if more and t == 4:
                        if u:
                            pe.wait_ge(a.inv_copied, u)
                        else:
                            pe.wait_ge(x_lo_ready, 4)
                        spread_zeros(u + 1, 0)
                    if more and t == 5:
                        spread_zeros(u + 1, 1)
                    if u and t == 6:
                        if more:
                            pe.wait_ge(zeros_ready, 2 * u + 4)
                        turn_out(u - 1)
                if more:
                    score(u + 1, 0)
                    score(u + 1, 1)
                if u:
                    pe.wait_ge(a.z_normed, u)
                pe_values(pe, m, a, u, 0, range(NT), values(u))
            pe_values(pe, m, a, B - 1, 1, range(NT), values(B - 1))
            pe.wait_ge(added, B - 1)
            pe_inverse_rows(pe, m, a, B - 1, 1)
            turn_out(B - 1)

        @block.vector
        def _(dve):
            link = Chain(dve, step)
            dve.wait_ge(loaded, 32)

            def copy_rows(u):
                dve.wait_ge(rows_copied, 2 * u + 1)
                dve.tensor_copy(x2[:, u % 3, :, 1, :], x2[:, u % 3, :, 0, :]).then_inc(rows_copied, 1)

            def find_zero_rows(u):
                dve.wait_ge(rows_squared, u + 1)
                link(dve.tensor_reduce(zero_row[:, u % 2, :], row_squares[:], AX, ALU.max))
                link(dve.tensor_scalar(zero_row[:, u % 2, :], zero_row[:, u % 2, :], 0.0, NEG,
                                       ALU.is_equal, ALU.mult))
                dve.nop().then_inc(rows_found, 1)

            def split_x(u, half):
                cols = slice(half * HALF, (half + 1) * HALF)
                dve.wait_ge(x_hi_ready, 2 * u + half + 1)
                dve.tensor_tensor(x_lo[:, u % 2, cols], m.ps_misc[:, 1, :], x_hi[:, u % 2, cols],
                                  ALU.subtract).then_inc(x_lo_ready, 1)
                dve.wait_ge(x_lo_ready, 2 * u + half + 1)
                dve.tensor_copy(xs[F:P, u % 2, cols], x_lo[F:P, u % 2, cols]).then_inc(xs_ready, 1)

            def mask_tile(u, t):
                if t == 0:
                    dve.wait_ge(zeros_ready, 2 * u + 2)
                link(dve.scalar_tensor_tensor(out=mask[:, t % 2, :], in0=zero_col[:, u % 2, :],
                                              scalar=zero_row[:, u % 2, t:t + 1], in1=m.mask[:, t, :],
                                              op0=ALU.min, op1=ALU.min))
                dve_mask(dve, m, a, u, u % 2, t, m.ps_score[:, t % 2, :], mask[:, t % 2, :], u == 0)

            def activate(u):
                dve_normalise(dve, m, a, u, u % 2)
                dve.wait_ge(a.z_normed, u + 1)
                z = a.z[:, u % 2, :]
                link(dve.tensor_scalar(z, z, bias[:, 0:1], None, ALU.add))
                dve.scalar_tensor_tensor(out=z, in0=z, scalar=0.01, in1=z, op0=ALU.mult,
                                         op1=ALU.max).then_inc(activated, 1)

            def add(u):
                dve.wait_ge(out_turned, u + 1)
                for side in range(2):
                    x = z_rows(m.x[:, :, u, :], side)
                    ins = dve.tensor_tensor(x, x, turned_rows(m.ps_misc[:, 1, :], side), ALU.add)
                ins.then_inc(added, 1)

            copy_rows(0)
            for half in range(2):
                split_x(0, half)
            find_zero_rows(0)
            mask_tile(0, 0)
            mask_tile(0, 1)
            for u in range(B):
                more = u + 1 < B
                for t in range(NT):
                    if more and t == 1:
                        copy_rows(u + 1)
                    if more and t in (2, 3):
                        split_x(u + 1, t - 2)
                    if t + 2 < NT:
                        mask_tile(u, t + 2)
                    if u and t == 4:
                        activate(u - 1)
                    if more and t == 3:
                        find_zero_rows(u + 1)
                    if u and t == 7:
                        add(u - 1)
                dve_inverse(dve, m, a, u, u % 2)
                if more:
                    mask_tile(u + 1, 0)
                    mask_tile(u + 1, 1)
            activate(B - 1)
            add(B - 1)

        @block.scalar
        def _(act):
            def copy_rows(u):
                act.wait_ge(rows_ready, u + 1)
                dst = x2[:, u % 3, :, 0, :].rearrange("p (a c) f -> p c a f", a=2)
                src = m.ps_misc[:, 1, :].rearrange("p (c a f) -> p c a f", c=4, a=2)
                act.copy(dst, src).then_inc(rows_copied, 1)

            def split_x(u, half):
                cols = slice(half * HALF, (half + 1) * HALF)
                act.wait_ge(x_turned, 2 * u + half + 1)
                act.copy(x_hi[:, u % 2, cols], m.ps_misc[:, 1, :]).then_inc(x_hi_ready, 1)
                act.wait_ge(x_hi_ready, 2 * u + half + 1)
                act.copy(xs[0:F, u % 2, cols], x_hi[0:F, u % 2, cols]).then_inc(xs_ready, 1)

            def square(u):
                act.wait_ge(rows_copied, 2 * u + 1)
                if u:
                    act.wait_ge(rows_found, u)
                act.activation(row_squares[:], x2[:, u % 3, :, 0, :], ACT.Square).then_inc(rows_squared, 1)

            def copy_zeros(u, half):
                act.wait_ge(zeros_spread, 2 * u + half + 1)
                act.copy(zero_col[:, u % 2, half * HALF:(half + 1) * HALF], m.ps_misc[:, 1, :])\
                   .then_inc(zeros_ready, 1)

            copy_rows(0)
            square(0)
            for half in range(2):
                split_x(0, half)
            for half in range(2):
                copy_zeros(0, half)
            for u in range(B):
                more = u + 1 < B
                for t in range(NT):
                    act_exp(act, m, a, u, u % 2, t, u == 0)
                    if t >= 1:
                        act_copy_turned(act, m, a, u, t - 1)
                    if more and t == 1:
                        copy_rows(u + 1)
                        square(u + 1)
                    if more and t in (2, 3):
                        split_x(u + 1, t - 2)
                    if u and t == 4:
                        act_copy_inverse(act, m, a, u - 1, (u - 1) % 2)
                    if more and t in (5, 6):
                        copy_zeros(u + 1, t - 5)
                act_copy_turned(act, m, a, u, NT - 1)
            act_copy_inverse(act, m, a, B - 1, 1)


def project(nc, m, ctx, name, weight, width, dests):
    turned = ctx.enter_context(nc.sbuf_tensor(name + "_turned", [P, B // 2, N], F32))
    ready = nc.alloc_semaphore(name + "_ready")
    copied = nc.alloc_semaphore(name + "_copied")
    done = nc.alloc_semaphore(name + "_done")
    taken = [nc.alloc_semaphore(f"{name}_taken{i}") for i in range(2)]
    with ExitStack() as inner:
        block = inner.enter_context(nc.Block())
        pairs = [(q, t) for q in range(B // 2) for t in range(NT)]

        @block.tensor
        def _(pe):
            for q in range(B // 2):
                if q >= 2:
                    pe.wait_ge(copied, q - 1)
                for t in range(NT):
                    ins = pe.transpose(m.ps_score[:, q % 2, t * P:(t + 1) * P],
                                       m.h[:, t, 2 * q:2 * q + 2, :].rearrange("p a f -> p (a f)"),
                                       m.ident[:])
                ins.then_inc(ready, 1)
            for i, (q, t) in enumerate(pairs):
                if t == 0:
                    pe.wait_ge(copied, q + 1)
                if i >= 4:
                    pe.wait_ge(taken[i % 2], (i - 4) // 2 + 1)
                bank = m.ps_misc[:, i % 4 // 2, 0:width] if i % 2 else m.ps_turn[:, i % 4 // 2, 0:width]
                pe.matmul(bank, turned[:, q, t * P:(t + 1) * P], weight, start=True,
                          stop=True).then_inc(done, 1)

        def take(eng, copy, parity):
            for q in range(parity, B // 2, 2):
                eng.wait_ge(ready, q + 1)
                if q >= 1:
                    eng.wait_ge(copied, q)
                copy(turned[:, q, :], m.ps_score[:, q % 2, :]).then_inc(copied, 1)
            for i, (q, t) in enumerate(pairs):
                if i % 2 != parity:
                    continue
                eng.wait_ge(done, i + 1)
                bank = m.ps_misc if i % 2 else m.ps_turn
                for lo, hi, place in dests:
                    ins = copy(place(q, t), bank[:, i % 4 // 2, lo:hi])
                ins.then_inc(taken[parity], 1)

        @block.vector
        def _(dve):
            take(dve, dve.tensor_copy, 0)

        @block.scalar
        def _(act):
            take(act, act.copy, 1)
    return turned


def mix(nc, m, ctx, name, values, finish, act_finish=None):
    hi, lo = split(nc, ctx, name + "_v", [P, NT, B * F])
    rounded = nc.alloc_semaphore(name + "_rounded")
    parted = nc.alloc_semaphore(name + "_parted")
    mixed = nc.alloc_semaphore(name + "_mixed")
    finished = nc.alloc_semaphore(name + "_finished")
    with ExitStack() as inner:
        block = inner.enter_context(nc.Block())

        def bank(t):
            return m.ps_misc[:, t % 2, :]

        @block.scalar
        def _(act):
            for t in range(NT):
                act.copy(hi[:, t, :], values(t)).then_inc(rounded, 1)

        @block.tensor
        def _(pe):
            for t in range(NT):
                if t >= 2:
                    pe.wait_ge(finished, t - 1)
                for j in range(NT):
                    if t == 0:
                        pe.wait_ge(parted, j + 1)
                    for k, part in enumerate((hi, lo)):
                        ins = pe.matmul(bank(t), m.adj_t[:, j, t * P:(t + 1) * P], part[:, j, :],
                                        start=(j == 0 and k == 0), stop=(j == NT - 1 and k == 1))
                ins.then_inc(mixed, 1)

        @block.vector
        def _(dve):
            for t in range(NT):
                dve.wait_ge(rounded, t + 1)
                dve.tensor_tensor(lo[:, t, :], values(t), hi[:, t, :], ALU.subtract).then_inc(parted, 1)
            for t in range(NT):
                dve.wait_ge(mixed, t + 1)
                finish(dve, t, bank(t)).then_inc(finished, 1)


class Weights:

    def __init__(self, nc, ctx, name):
        self.nc, self.ctx, self.name, self.clear, self.loads = nc, ctx, name, [], []

    def buffer(self, n, shape):
        return self.ctx.enter_context(self.nc.sbuf_tensor(f"{self.name}_{n}", shape, F32))

    def load(self, place, src):
        self.loads.append((place, src))

    def blocks(self, n, width, parts):
        w = self.buffer(n, [P, width])
        self.clear.append(w)
        for row, col, src in parts:
            self.load(w[row:row + src.shape[0], col:col + src.shape[1]], src)
        return w


def hypergraph_weights(nc, ctx, d):
    g = Weights(nc, ctx, "hyp")
    g.w = g.blocks("w", 2 * P + 2, [
        (0, 0, d["L0_gnn_W"]), (F, F, d["L0_gnn_W"]),
        (0, P, d["L0_gnn_W_ind"]), (F, P + F, d["L0_gnn_W_ind"])])
    g.fc_w = g.blocks("fc_w", 2 * P, [(0, 0, d["L0_gnn_fcW"]), (F, P, d["L0_gnn_fcW"])])
    g.w_t = g.buffer("w_t", [F, 2, F])
    g.vecs = g.buffer("vecs", [F, 4])
    g.fc_b, g.av = g.buffer("fc_b", [P, 1]), g.buffer("av", [P, 1])
    g.member_rows = g.buffer("member_rows", [P, NT, F])
    g.member_cols = g.buffer("member_cols", [P, N])
    for k in range(2):
        g.load(g.w_t[:, k, :], d["l0_wt"])
        g.load(g.member_cols[k * F:(k + 1) * F, :], d["h_t"])
    g.load(g.vecs[:, 0:3], d["l0_vecs"])
    g.load(g.member_rows[:], d["h_rows"])
    g.load(g.fc_b[:], d["L0_gnn_fcb"].rearrange("(f a) -> f a", a=1))
    g.load(g.av[:], d["L0_gnn_av"].rearrange("(f a) -> f a", a=1))
    return g


def graph_attention_weights(nc, ctx, d):
    g = Weights(nc, ctx, "gat")
    g.w = g.blocks("w", P + 2, [(0, 0, d["l1_wt"]), (F, F, d["l1_wt"])])
    g.w_rows = g.buffer("w_rows", [F, 2, F])
    g.a_cols = g.buffer("a_cols", [F, 2])
    for k in range(2):
        g.load(g.w_rows[:, k, :], d["L1_gnn_W"])
    g.load(g.a_cols[:], d["l1_a"])
    return g


def graph_weights(nc, ctx, d):
    g = Weights(nc, ctx, "gl")
    g.w = [g.blocks(f"w{r}", P, [(0, 0, d["L2_w"][r]), (F, F, d["L2_w"][r])]) for r in range(2)]
    return g


def last_weights(nc, ctx, d):
    g = Weights(nc, ctx, "hid")
    g.wh_t = g.buffer("wh_t", [HID, HEADS, 2, F])
    g.wz = g.buffer("wz", [P, 2, HEADS, HID])
    g.wo = g.buffer("wo", [HID, HEADS, F])
    g.bias = g.buffer("bias", [HID, HEADS])
    g.clear.append(g.wz)
    for k in range(2):
        g.load(g.wh_t[:, :, k, :], d["wh_t"].rearrange("h d f -> d h f"))
        g.load(g.wz[k * F:(k + 1) * F, k, :, :], d["L3_gnn_Wh"].rearrange("h f d -> f h d"))
    g.load(g.wo[:], d["L3_gnn_W_out"].rearrange("(h d) f -> d h f", d=HID))
    g.load(g.bias[:], d["bh_t"])
    return g


def graph_layer(nc, m, g):
    with ExitStack() as ctx:
        for r in range(2):
            with ExitStack() as part:
                zw = part.enter_context(nc.sbuf_tensor(f"gl{r}_zw", [P, NT, B, F], F32))
                project(nc, m, part, f"gl{r}_p", g.w[r][:], P, [
                    (0, P, lambda q, t: zw[:, t, 2 * q:2 * q + 2, :].rearrange("p a f -> p (a f)"))])

                def finish(dve, t, ps):
                    h = m.h[:, t, :, :].rearrange("p b f -> p (b f)")
                    x = m.x[:, t, :, :].rearrange("p b f -> p (b f)")
                    if r == 0:
                        return dve.tensor_scalar(h, ps, 0.0, None, ALU.max)
                    return dve.scalar_tensor_tensor(out=x, in0=ps, scalar=0.0, in1=x,
                                                    op0=ALU.max, op1=ALU.add)

                mix(nc, m, part, f"gl{r}_m", lambda t: zw[:, t, :, :].rearrange("p b f -> p (b f)"), finish)


def graph_attention_layer(nc, m, g):
    name = "gat"
    with ExitStack() as ctx:
        def sb(n, shape, dt=F32):
            return ctx.enter_context(nc.sbuf_tensor(f"{name}_{n}", shape, dt))

        def sem(n):
            return nc.alloc_semaphore(f"{name}_{n}")

        w, w_rows, a_cols, width = g.w, g.w_rows, g.a_cols, P + 2
        a2_w = sb("a2_w", [P, 2, P])
        wh = sb("wh", [P, NT, B, F])
        e1 = sb("e1", [P, NT, B])
        with ExitStack() as prep:
            ready = nc.alloc_semaphore("gat_ready")
            cleared = nc.alloc_semaphore("gat_cleared")
            block = prep.enter_context(nc.Block())

            @block.tensor
            def _(pe):
                rows = w_rows[:].rearrange("o a f -> o (a f)")
                pe.matmul(m.ps_misc[:, 0, 0:P], rows, a_cols[:, 1:2].to_broadcast([F, P]),
                          start=True, stop=True)
                pe.matmul(m.ps_misc[:, 1, 0:1], rows, a_cols[:, 0:1], start=True, stop=True)\
                  .then_inc(ready, 1)

            @block.vector
            def _(dve):
                dve.memset(a2_w[:], 0.0).then_inc(cleared, 1)
                dve.wait_ge(ready, 1)
                dve.wait_ge(cleared, 1)
                for k in range(2):
                    half = slice(k * F, (k + 1) * F)
                    dve.tensor_copy(a2_w[half, k, :], m.ps_misc[half, 0, 0:P])
                    dve.tensor_copy(w[half, P + k:P + k + 1], m.ps_misc[half, 1, 0:1])

        x_t = project(nc, m, ctx, "gat_p", w[:], width, [
            (0, P, lambda q, t: wh[:, t, 2 * q:2 * q + 2, :].rearrange("p a f -> p (a f)")),
            (P, P + 2, lambda q, t: e1[:, t, 2 * q:2 * q + 2])])

        a = attention_pipeline(nc, m, ctx, name, range(0, NT, 2))
        e2 = sb("e2", [P, 2, N])
        sums = sb("sums", [P, 2, N])
        z_exp = sb("z_exp", [P, HALF])
        step = sem("step")
        e2_ready = sem("e2_ready")
        e2_copied = sem("e2_copied")
        summed = sem("summed")
        z_exped = sem("z_exped")
        activated = sem("activated")
        out_turned = sem("out_turned")
        added = sem("added")
        block = ctx.enter_context(nc.Block())

        @block.tensor
        def _(pe):
            def spread_e2(u):
                for half in range(2):
                    ins = pe.matmul(m.ps_score[:, u % 2, half * HALF:(half + 1) * HALF],
                                    a2_w[:, u % 2, :], x_t[:, u // 2, half * HALF:(half + 1) * HALF],
                                    start=True, stop=True)
                ins.then_inc(e2_ready, 1)

            def turn_out(u):
                pe.wait_ge(activated, u + 1)
                for c in range(NT // 2):
                    ins = pe.transpose(m.ps_misc[:, 1, c * P:(c + 1) * P],
                                       a.z[:, u % 2, c * P:(c + 1) * P], m.ident[:])
                ins.then_inc(out_turned, 1)

            def values(u):
                return lambda j: wh[:, j, u, :]

            spread_e2(0)
            for u in range(B):
                for t in range(NT):
                    if u and t < 4:
                        pe_values(pe, m, a, u - 1, 1, range(2 * t, 2 * t + 2), values(u - 1))
                    pe_turn(pe, m, a, u, t, u == 0)
                    if u and t == 3:
                        if u >= 2:
                            pe.wait_ge(added, u - 1)
                        pe_inverse_rows(pe, m, a, u - 1, (u - 1) % 2)
                    if u + 1 < B and t == 4:
                        pe.wait_ge(e2_copied, u + 1)
                        spread_e2(u + 1)
                    if u and t == 6:
                        turn_out(u - 1)
                if u:
                    pe.wait_ge(a.z_normed, u)
                pe_values(pe, m, a, u, 0, range(NT), values(u))
            pe_values(pe, m, a, B - 1, 1, range(NT), values(B - 1))
            pe.wait_ge(added, B - 1)
            pe_inverse_rows(pe, m, a, B - 1, 1)
            turn_out(B - 1)

        @block.scalar
        def _(act):
            def copy_e2(u):
                act.wait_ge(e2_ready, u + 1)
                act.copy(e2[:, u % 2, :], m.ps_score[:, u % 2, :]).then_inc(e2_copied, 1)

            def add_e1(u, t):
                if t == 0:
                    act.wait_ge(e2_copied, u + 1)
                if u or t >= 2:
                    act.wait_ge(a.masked_ready, u * NT + t - 1)
                act.activation(sums[:, t % 2, :], e2[:, u % 2, :], ACT.Identity,
                               bias=e1[:, t, u:u + 1]).then_inc(summed, 1)

            def exp_z(u):
                act.wait_ge(a.z_normed, u + 1)
                act.activation(z_exp[:], a.z[:, u % 2, :], ACT.Exp).then_inc(z_exped, 1)

            copy_e2(0)
            add_e1(0, 0)
            add_e1(0, 1)
            for u in range(B):
                for t in range(NT):
                    act_exp(act, m, a, u, u % 2, t, u == 0)
                    if t + 2 < NT:
                        add_e1(u, t + 2)
                    if t >= 1:
                        act_copy_turned(act, m, a, u, t - 1)
                    if u and t == 4:
                        act_copy_inverse(act, m, a, u - 1, (u - 1) % 2)
                    if u and t == 5:
                        exp_z(u - 1)
                    if u + 1 < B and t == 6:
                        copy_e2(u + 1)
                        add_e1(u + 1, 0)
                        add_e1(u + 1, 1)
                act_copy_turned(act, m, a, u, NT - 1)
            act_copy_inverse(act, m, a, B - 1, 1)
            exp_z(B - 1)

        @block.vector
        def _(dve):
            link = Chain(dve, step)

            def mask_tile(u, t):
                dve.wait_ge(summed, u * NT + t + 1)
                s = sums[:, t % 2, :]
                dve.scalar_tensor_tensor(out=s, in0=s, scalar=0.2, in1=s, op0=ALU.mult,
                                         op1=ALU.max).then_inc(a.scores_ready, 1)
                dve_mask(dve, m, a, u, u % 2, t, s, m.mask[:, t, :], u == 0)

            def elu(u):
                dve.wait_ge(z_exped, u + 1)
                link(dve.tensor_scalar(z_exp[:], z_exp[:], 1.0, -1.0, ALU.min, ALU.add))
                dve.tensor_tensor(a.z[:, u % 2, :], a.z[:, u % 2, :], z_exp[:], ALU.max).then_inc(activated, 1)

            def add(u):
                dve.wait_ge(out_turned, u + 1)
                for side in range(2):
                    x = z_rows(m.x[:, :, u, :], side)
                    ins = dve.tensor_tensor(x, x, turned_rows(m.ps_misc[:, 1, :], side), ALU.add)
                ins.then_inc(added, 1)

            mask_tile(0, 0)
            mask_tile(0, 1)
            for u in range(B):
                for t in range(NT):
                    if t + 2 < NT:
                        mask_tile(u, t + 2)
                    if u and t == 4:
                        dve_normalise(dve, m, a, u - 1, (u - 1) % 2)
                    dve_copy_turned(dve, m, a, u, t)
                    if u and t == 5:
                        elu(u - 1)
                    if u and t == 6:
                        add(u - 1)
                dve_inverse(dve, m, a, u, u % 2)
                if u + 1 < B:
                    mask_tile(u + 1, 0)
                    mask_tile(u + 1, 1)
            dve_normalise(dve, m, a, B - 1, 1)
            elu(B - 1)
            add(B - 1)


def hypergraph_layer(nc, m, g):
    name = "hyp"
    EN = F
    with ExitStack() as ctx:
        def sb(n, shape, dt=F32):
            return ctx.enter_context(nc.sbuf_tensor(f"{name}_{n}", shape, dt))

        w, width, w_t, vecs, fc_b, av = g.w, 2 * P + 2, g.w_t, g.vecs, g.fc_b, g.av
        member_rows, member_cols = g.member_rows, g.member_cols
        fc_w = g.fc_w[:].rearrange("p (k f) -> p k f", k=2)
        an_w = sb("an_w", [P, 2, P])
        ones = sb("ones", [P, P])
        members = sb("members", [P, N])
        edge_mask = sb("edge_mask", [P, N])
        node_mask = sb("node_mask", [P, NT, EN])
        linked = sb("linked", [P, NT])
        rank = sb("rank", [P, N])
        slots = sb("slots", [P, 1])
        slots_int = sb("slots_int", [P, 1], mybir.dt.int32)
        edge_rows = sb("edge_rows", [P, B, F])
        picks = sb("picks", [P, B * F + 18], F32R)
        best = sb("best", [P, NT, B])
        h1 = sb("h1", [P, NT, B, F])
        gate = sb("gate", [P, NT, B])
        coef_sum = sb("coef_sum", [P, NT, B])
        minus_one = sb("minus_one", [P, 1])
        neighbours = sb("neighbours", [P, NT, B, F])

        with ExitStack() as part:
            def psb(n, shape, dt=F32):
                return part.enter_context(nc.sbuf_tensor(f"{name}_{n}", shape, dt))

            def sem(n):
                return nc.alloc_semaphore(f"{name}_{n}")

            counts = psb("counts", [P, NT])
            total = psb("total", [P, N])
            upper = psb("upper", [F, 2, EN])
            folded, step = sem("folded"), sem("stepa")
            counted, filled, ranked, triangle = sem("counted"), sem("filled"), sem("ranked"), sem("triangle")
            block = part.enter_context(nc.Block())

            @block.gpsimd
            def _(pool):
                pool.memset(upper[:], 1.0).then_inc(triangle, 1)
                pool.wait_ge(triangle, 1)
                pool.affine_select(out=upper[:], in_=upper[:], compare_op=ALU.is_gt, fill=0.0, base=0,
                                   pattern=[[0, 2], [1, EN]], channel_multiplier=-1).then_inc(triangle, 1)

            @block.tensor
            def _(pe):
                rows = w_t[:].rearrange("o a f -> o (a f)")
                pe.matmul(m.ps_misc[:, 0, 0:P], rows, vecs[:, 0:1].to_broadcast([F, P]),
                          start=True, stop=True)
                pe.matmul(m.ps_misc[:, 1, 0:1], rows, vecs[:, 1:2], start=True, stop=True)\
                  .then_inc(folded, 1)
                pe.wait_ge(filled, 1)
                for half in range(2):
                    cols = slice(half * HALF, (half + 1) * HALF)
                    ins = pe.matmul(m.ps_score[:, 0, cols], ones[0:EN, :], members[0:EN, cols],
                                    start=True, stop=True)
                ins.then_inc(counted, 1)
                pe.wait_ge(filled, 2)
                pe.wait_ge(triangle, 2)
                for half in range(2):
                    cols = slice(half * HALF, (half + 1) * HALF)
                    ins = pe.matmul(m.ps_score[:, 1, cols], upper[:].rearrange("p a e -> p (a e)"),
                                    rank[0:EN, cols], start=True, stop=True)
                ins.then_inc(ranked, 1)

            @block.vector
            def _(dve):
                link = Chain(dve, step)
                link(dve.memset(an_w[:], 0.0))
                link(dve.memset(ones[:], 1.0))
                dve.wait_ge(folded, 1)
                for k in range(2):
                    half = slice(k * F, (k + 1) * F)
                    dve.tensor_copy(an_w[half, k, :], m.ps_misc[half, 0, 0:P])
                    link(dve.tensor_copy(w[half, 2 * P + k:2 * P + k + 1], m.ps_misc[half, 1, 0:1]))
                link(dve.tensor_scalar(members[:], member_cols[:], 0.0, None, ALU.is_gt))
                dve.nop().then_inc(filled, 1)
                link(dve.tensor_scalar(edge_mask[:], member_cols[:], 0.0, NEG, ALU.is_le, ALU.mult))
                link(dve.tensor_scalar(node_mask[:], member_rows[:], 0.0, NEG, ALU.is_le, ALU.mult))
                link(dve.tensor_reduce(counts[:], node_mask[:], AX, ALU.max))
                link(dve.tensor_scalar(linked[:], counts[:], 0.0, None, ALU.is_equal))
                dve.wait_ge(counted, 1)
                link(dve.tensor_scalar(total[:], m.ps_score[:, 0, :], 0.0, None, ALU.is_equal))
                link(dve.tensor_tensor(rank[:], members[:], total[:], ALU.max))
                dve.nop().then_inc(filled, 1)
                link(dve.scalar_tensor_tensor(out=total[:], in0=total[:], scalar=float(EN),
                                              in1=m.ps_score[:, 0, :], op0=ALU.mult, op1=ALU.add))
                link(dve.tensor_reduce(slots[:], total[:], AX, ALU.max))
                link(dve.tensor_copy(slots_int[:], slots[:]))
                dve.wait_ge(ranked, 1)
                link(dve.scalar_tensor_tensor(out=rank[:], in0=m.ps_score[:, 1, :], scalar=1.0,
                                              in1=rank[:], op0=ALU.add, op1=ALU.mult))
                dve.tensor_scalar(rank[:], rank[:], -1.0, None, ALU.add)

        with ExitStack() as part:
            x_t = project(nc, m, part, name + "_p", w[:], width, [
                (0, P, lambda q, t: h1[:, t, 2 * q:2 * q + 2, :].rearrange("p a f -> p (a f)")),
                (P, 2 * P, lambda q, t: neighbours[:, t, 2 * q:2 * q + 2, :].rearrange("p a f -> p (a f)")),
                (2 * P, width, lambda q, t: gate[:, t, 2 * q:2 * q + 2])])

            def psb(n, shape, dt=F32):
                return part.enter_context(nc.sbuf_tensor(f"{name}_{n}", shape, dt))

            def sem(n):
                return nc.alloc_semaphore(f"{name}_{n}")

            score = psb("score", [P, 2, N])
            masked = psb("masked", [P, 2, N])
            weights = psb("weights", [P, 2, N])
            weights_t = psb("weights_t", [P, 2, NT, P])
            neg_max, row_sum = psb("neg_max", [P, B]), psb("row_sum", [P, B])
            step, spread, copied, masked_ready, exp_ready = (
                sem("stepb"), sem("spread"), sem("copied"), sem("masked_ready"), sem("exp_ready"))
            turned = [sem("turned0"), sem("turned1")]
            turned_out = [sem("turned_out0"), sem("turned_out1")]
            summed, scaled = sem("summed"), sem("scaled")
            block = part.enter_context(nc.Block())

            @block.tensor
            def _(pe):
                def spread_scores(b):
                    if b >= 2:
                        pe.wait_ge(copied, b - 1)
                    for half in range(2):
                        cols = slice(half * HALF, (half + 1) * HALF)
                        ins = pe.matmul(m.ps_score[:, b % 2, cols], an_w[:, b % 2, :],
                                        x_t[:, b // 2, cols], start=True, stop=True)
                    ins.then_inc(spread, 1)

                def turn_weights(b):
                    pe.wait_ge(exp_ready, b + 1)
                    for half in range(2):
                        if b:
                            pe.wait_ge(turned_out[half], b)
                        for k in range(4):
                            t = half * 4 + k
                            ins = pe.transpose(m.ps_turn[:, half, k * P:(k + 1) * P],
                                               weights[:, b % 2, t * P:(t + 1) * P], m.ident[:])
                        ins.then_inc(turned[half], 1)

                spread_scores(0)
                spread_scores(1)
                turn_weights(0)
                for b in range(B):
                    if b + 2 < B:
                        spread_scores(b + 2)
                    if b + 1 < B:
                        turn_weights(b + 1)
                    for half in range(2):
                        pe.wait_ge(turned_out[half], b + 1)
                    if b >= 2:
                        pe.wait_ge(scaled, b - 1)
                    for t in range(NT):
                        ins = pe.matmul(m.ps_misc[:, b % 2, 0:F], weights_t[:, b % 2, t, :],
                                        h1[:, t, b, :], start=(t == 0), stop=(t == NT - 1))
                    ins.then_inc(summed, 1)

            @block.scalar
            def _(act):
                def copy_scores(b):
                    act.wait_ge(spread, b + 1)
                    if b >= 2:
                        act.wait_ge(masked_ready, b - 1)
                    act.copy(score[:, b % 2, :], m.ps_score[:, b % 2, :]).then_inc(copied, 1)

                def copy_turned(b):
                    act.wait_ge(turned[0], b + 1)
                    if b >= 2:
                        act.wait_ge(summed, b - 1)
                    act.copy(weights_t[:, b % 2, 0:4, :].rearrange("p k e -> p (k e)"),
                             m.ps_turn[:, 0, :]).then_inc(turned_out[0], 1)

                def exp_scores(b):
                    act.wait_ge(masked_ready, b + 1)
                    if b >= 2:
                        act.wait_ge(turned[1], b - 1)
                    act.activation(weights[:, b % 2, :], masked[:, b % 2, :], ACT.Exp, scale=-1.0,
                                   bias=neg_max[:, b:b + 1], accum_out=row_sum[:, b:b + 1])\
                       .then_inc(exp_ready, 1)

                copy_scores(0)
                copy_scores(1)
                exp_scores(0)
                for b in range(B):
                    if b + 1 < B:
                        exp_scores(b + 1)
                    copy_turned(b)
                    if b + 2 < B:
                        copy_scores(b + 2)

            @block.vector
            def _(dve):
                link = Chain(dve, step)

                def mask(b):
                    dve.wait_ge(copied, b + 1)
                    s = score[:, b % 2, :]
                    link(dve.scalar_tensor_tensor(out=s, in0=s, scalar=0.2, in1=s, op0=ALU.mult,
                                                  op1=ALU.max))
                    if b >= 2:
                        dve.wait_ge(exp_ready, b - 1)
                    dve.tensor_tensor_reduce(masked[:, b % 2, :], s, edge_mask[:], -1.0, HUGE, ALU.add,
                                             ALU.min, neg_max[:, b:b + 1]).then_inc(masked_ready, 1)

                def scale(b):
                    dve.wait_ge(summed, b + 1)
                    dve.tensor_scalar(edge_rows[:, b, :], m.ps_misc[:, b % 2, 0:F],
                                      row_sum[:, b:b + 1], None, ALU.mult).then_inc(scaled, 1)

                mask(0)
                mask(1)
                for b in range(B):
                    dve.wait_ge(turned[1], b + 1)
                    if b >= 2:
                        dve.wait_ge(summed, b - 1)
                    dve.tensor_copy(weights_t[:, b % 2, 4:8, :].rearrange("p k e -> p (k e)"),
                                    m.ps_turn[:, 1, :]).then_inc(turned_out[1], 1)
                    if b + 2 < B:
                        mask(b + 2)
                    dve.wait_ge(exp_ready, b + 1)
                    link(dve.reciprocal(row_sum[:, b:b + 1], row_sum[:, b:b + 1]))
                    if b:
                        scale(b - 1)
                scale(B - 1)

        with ExitStack() as part:
            def psb(n, shape, dt=F32):
                return part.enter_context(nc.sbuf_tensor(f"{name}_{n}", shape, dt))

            def sem(n):
                return nc.alloc_semaphore(f"{name}_{n}")

            elus = psb("elus", [P, B, F])
            elus_t = psb("elus_t", [F, B, P])
            rows_t = psb("rows_t", [F, B, P])
            hidden = psb("hidden", [P, B, P])
            pick_hi = psb("pick_hi", [P, B * F + 18], F32R)
            pick_all = psb("pick_all", [P, B * F + 18])
            table = psb("table", [P, NT, B, EN])
            step, exped, elued, turned, copied = (
                sem("stepc"), sem("exped"), sem("elued"), sem("turned_c"), sem("copied_c"))
            hidden_ready, tanh_ready, scored, collected, rounded = (
                sem("hidden_ready"), sem("tanh_ready"), sem("scored"), sem("collected"), sem("rounded_c"))
            block = part.enter_context(nc.Block())
            flat = edge_rows[:].rearrange("p b f -> p (b f)")

            @block.scalar
            def _(act):
                act.activation(elus[:], edge_rows[:], ACT.Exp).then_inc(exped, 1)
                for half in range(2):
                    act.wait_ge(hidden_ready, half + 1)
                    act.activation(hidden[:, 4 * half:4 * half + 4, :],
                                   m.ps_misc[:, half, :].rearrange("p (b e) -> p b e", b=4),
                                   ACT.Tanh, bias=fc_b[:, 0:1]).then_inc(tanh_ready, 1)
                act.wait_ge(collected, 1)
                act.copy(pick_hi[:], pick_all[:]).then_inc(rounded, 1)
                act.copy(picks[0:F, :], pick_all[0:F, :])

            @block.tensor
            def _(pe):
                for b in range(B):
                    pe.transpose(m.ps_score[0:F, b // 4, (b % 4) * P:(b % 4 + 1) * P],
                                 edge_rows[:, b, :], m.ident[:])
                pe.wait_ge(elued, 1)
                for b in range(B):
                    ins = pe.transpose(m.ps_score[0:F, b // 4, HALF + (b % 4) * P:HALF + (b % 4 + 1) * P],
                                       elus[:, b, :], m.ident[:])
                ins.then_inc(turned, 1)
                pe.wait_ge(copied, 2)
                for half in range(2):
                    pe.matmul(m.ps_misc[:, half, :], fc_w[0:F, 0, :],
                              elus_t[:, 4 * half:4 * half + 4, :].rearrange("p b e -> p (b e)"),
                              start=True, stop=True).then_inc(hidden_ready, 1)
                pe.wait_ge(tanh_ready, 2)
                for b in range(B):
                    pe.matmul(m.ps_turn[:, 0, b:b + 1], hidden[:, b, :], av[:], start=True, stop=True)
                    pe.matmul(m.ps_turn[:, 0, B + b:B + b + 1], rows_t[:, b, :], vecs[:, 2:3],
                              start=True, stop=True)
                pe.matmul(m.ps_turn[:, 1, :].rearrange("p (b e) -> p b e", b=B), av[:].to_broadcast([P, P]), hidden[:, :, 0:EN],
                          start=True, stop=True).then_inc(scored, 1)

            @block.vector
            def _(dve):
                link = Chain(dve, step)
                dve.wait_ge(exped, 1)
                link(dve.tensor_scalar(elus[:], elus[:], 1.0, -1.0, ALU.min, ALU.add))
                dve.tensor_tensor(elus[:], elus[:], edge_rows[:], ALU.max).then_inc(elued, 1)
                dve.wait_ge(turned, 1)
                dve.tensor_copy(rows_t[:].rearrange("p (a b) e -> p a (b e)", a=2),
                                m.ps_score[0:F, :, 0:HALF]).then_inc(copied, 1)
                dve.tensor_copy(elus_t[:].rearrange("p (a b) e -> p a (b e)", a=2),
                                m.ps_score[0:F, :, HALF:N]).then_inc(copied, 1)
                dve.wait_ge(scored, 1)
                link(dve.tensor_copy(pick_all[:, 0:B * F], flat))
                link(dve.tensor_copy(pick_all[:, B * F:B * F + 16], m.ps_turn[:, 0, 0:16]))
                link(dve.memset(pick_all[:, B * F + 16:], 1.0))
                dve.nop().then_inc(collected, 1)
                dve.wait_ge(rounded, 1)
                dve.tensor_tensor(picks[F:P, :], pick_all[F:P, :], pick_hi[F:P, :], ALU.subtract)
                edge_scores = m.ps_turn[:, 1, :].rearrange("p (b e) -> p b e", b=B)
                for t in range(NT):
                    ins = dve.tensor_tensor(table[:, t, :, :], edge_scores,
                                            node_mask[:, t, :].unsqueeze(1).to_broadcast([P, B, EN]),
                                            ALU.add)
                link(ins)
                dve.tensor_reduce(best[:], table[:], AX, ALU.max)

        with ExitStack() as part:
            def psb(n, shape, dt=F32):
                return part.enter_context(nc.sbuf_tensor(f"{name}_{n}", shape, dt))

            def sem(n):
                return nc.alloc_semaphore(f"{name}_{n}")

            pick = psb("pick", [P, N], F32R)
            beta = psb("beta", [P, NT, B])
            coef = psb("coef", [P, NT, B])
            diff = psb("diff", [P, 2, B * F])
            blend = psb("blend", [P, 2, B * F])
            blend_exp = psb("blend_exp", [P, 2, B * F])
            share = psb("share", [P, 4, B * F])
            pool_coef = psb("pool_coef", [P, NT, B])
            picks_neg = psb("picks_neg", [P, B * F], F32R)
            step, picked, small_ready, rows_ready, rows_taken = (
                sem("stepd"), sem("picked"), sem("small_ready"), sem("rows_ready"), sem("rows_taken"))
            sums_zeroed = sem("sums_zeroed")
            coef_ready, coef_seen, coef_taken, scaled = (
                sem("coef_ready"), sem("coef_seen"), sem("coef_taken"), sem("scaled_d"))
            exp_asked, exp_ready, blend_ready, blend_exped, share_ready, share_added = (
                sem("exp_asked"), sem("exp_ready_d"), sem("blend_ready"), sem("blend_exped"),
                sem("share_ready"), sem("share_added"))
            small = m.ps_misc[:, 0, 0:NT * 18].rearrange("p (t c) -> p t c", t=NT)
            block = part.enter_context(nc.Block())

            def along(v, t):
                return v[:, t, :].unsqueeze(2).to_broadcast([P, B, F])

            def by_batch(v):
                return v.rearrange("p (b f) -> p b f", b=B)

            def row_banks(t):
                if t % 3 == 2:
                    return m.ps_turn[:, 0, :], m.ps_turn[:, 1, :]
                return m.ps_score[:, t % 3, 0:HALF], m.ps_score[:, t % 3, HALF:N]

            def slot_count(eng):
                return eng.value_load(slots_int[0:1, 0:1], min_val=1, max_val=EN)

            @block.tensor
            def _(pe):
                with pe.Fori(0, slot_count(pe)) as k:
                    pe.wait_ge(picked, k + 1)
                    for t in range(NT):
                        ins = pe.matmul(m.ps_misc[:, 0, t * 18:(t + 1) * 18], pick[:, t * P:(t + 1) * P],
                                        picks[:, B * F:], start=True, stop=True)
                    ins.then_inc(small_ready, 1)
                    for t in range(NT):
                        pe.wait_ge(rows_taken, k * NT + max(t + 1, 3))
                        row, away = row_banks(t)
                        pe.matmul(row, pick[:, t * P:(t + 1) * P], picks[:, 0:B * F],
                                  start=True, stop=True)
                        pe.matmul(away, m.ident[:], h1[:, t, :, :].rearrange("p b f -> p (b f)"),
                                  start=True, stop=False)
                        pe.matmul(away, pick[:, t * P:(t + 1) * P], picks_neg[:],
                                  start=False, stop=True).then_inc(rows_ready, 1)

            @block.scalar
            def _(act):
                with act.Fori(0, slot_count(act)) as k:
                    act.wait_ge(exp_asked, 2 * k + 1)
                    act.activation(coef[:], coef[:], ACT.Exp).then_inc(exp_ready, 1)
                    act.wait_ge(exp_asked, 2 * k + 2)
                    act.activation(beta[:], beta[:], ACT.Exp, scale=-1.0).then_inc(exp_ready, 1)
                    for t in range(NT):
                        act.wait_ge(blend_ready, k * NT + t + 1)
                        act.activation(blend_exp[:, t % 2, :], blend[:, t % 2, :], ACT.Exp,
                                       bias=minus_one[:, 0:1]).then_inc(blend_exped, 1)

            @block.gpsimd
            def _(pool):
                rows = m.h[:].rearrange("p t b f -> p t (b f)")
                pool.memset(m.h[:], 0.0).then_inc(sums_zeroed, 1)
                pool.wait_ge(sums_zeroed, 1)
                pool.nop().then_inc(share_added, 4)
                with pool.Fori(0, slot_count(pool)) as k:
                    pool.wait_ge(coef_ready, k + 1)
                    pool.nop().then_inc(coef_seen, 1)
                    pool.tensor_copy(pool_coef[:], coef[:]).then_inc(coef_taken, 1)
                    pool.wait_ge(coef_taken, k + 2)
                    for t in range(NT):
                        pool.wait_ge(share_ready, k * NT + t + 1)
                        s = share[:, t % 4, :]
                        pool.tensor_tensor(by_batch(s), by_batch(s), along(pool_coef, t), ALU.mult)\
                            .then_inc(scaled, 1)
                        pool.wait_ge(scaled, k * NT + t + 1)
                        pool.tensor_tensor(rows[:, t, :], rows[:, t, :], s, ALU.add)\
                            .then_inc(share_added, 1)

            @block.vector
            def _(dve):
                dve.memset(minus_one[:], -1.0).then_inc(step, 1)
                dve.memset(coef_sum[:], 0.0).then_inc(step, 1)
                dve.tensor_scalar(picks_neg[:], picks[:, 0:B * F], -1.0, None, ALU.mult).then_inc(step, 1)
                dve.wait_ge(step, 3)
                dve.nop().then_inc(rows_taken, 3)
                dve.nop().then_inc(coef_taken, 1)
                steps = 6 + NT
                dve.tensor_scalar(pick[:], rank[:], 0.0, None, ALU.is_equal).then_inc(picked, 1)
                dve.wait_ge(picked, 1)

                with dve.Fori(0, slot_count(dve)) as k:
                    link = Chain(dve, step, 3 + k * steps)
                    link(dve.tensor_scalar(rank[:], rank[:], -1.0, None, ALU.add))
                    dve.wait_ge(small_ready, k + 1)
                    dve.wait_ge(coef_taken, k + 1)
                    link(dve.tensor_tensor(coef[:], small[:, :, 0:B], best[:], ALU.subtract))
                    dve.scalar_tensor_tensor(out=coef[:], in0=coef[:], scalar=0.0,
                                             in1=linked[:].unsqueeze(2).to_broadcast([P, NT, B]),
                                             op0=ALU.min, op1=ALU.mult).then_inc(exp_asked, 1)
                    dve.tensor_tensor(beta[:], small[:, :, B:2 * B], gate[:], ALU.add).then_inc(exp_asked, 1)
                    dve.wait_ge(exp_ready, 2 * k + 1)
                    link(dve.tensor_tensor(coef[:], coef[:], small[:, :, 16:17].to_broadcast([P, NT, B]),
                                           ALU.mult))
                    dve.nop().then_inc(coef_ready, 1)
                    link(dve.tensor_tensor(coef_sum[:], coef_sum[:], coef[:], ALU.add))
                    dve.wait_ge(exp_ready, 2 * k + 2)
                    link(dve.tensor_scalar(beta[:], beta[:], 1.0, None, ALU.add))
                    link(dve.reciprocal(beta[:], beta[:]))

                    def blend_rows(t):
                        dve.wait_ge(rows_ready, k * NT + t + 1)
                        row, away = row_banks(t)
                        d2 = diff[:, t % 2, :]
                        link(dve.tensor_tensor(by_batch(d2), by_batch(away),
                                               along(beta, t), ALU.mult))
                        dve.scalar_tensor_tensor(out=blend[:, t % 2, :], in0=row, scalar=1.0, in1=d2,
                                                 op0=ALU.add, op1=ALU.add).then_inc(blend_ready, 1)
                        dve.wait_ge(blend_ready, k * NT + t + 1)
                        dve.nop().then_inc(rows_taken, 1)

                    def add_share(t):
                        dve.wait_ge(blend_exped, k * NT + t + 1)
                        s = share[:, t % 4, :]
                        dve.wait_ge(share_added, k * NT + t + 1)
                        dve.scalar_tensor_tensor(out=s, in0=blend_exp[:, t % 2, :], scalar=1.0,
                                                 in1=blend[:, t % 2, :], op0=ALU.min,
                                                 op1=ALU.max).then_inc(share_ready, 1)

                    blend_rows(0)
                    for t in range(NT):
                        if t + 1 < NT:
                            blend_rows(t + 1)
                        if t + 2 == NT:
                            dve.tensor_scalar(pick[:], rank[:], 0.0, None, ALU.is_equal)\
                               .then_inc(picked, 1)
                        add_share(t)
                    dve.wait_ge(picked, k + 2)

        with ExitStack() as part:
            def divide(dve, t, ps):
                return dve.tensor_scalar(neighbours[:, t, :, :].rearrange("p b f -> p (b f)"), ps,
                                         m.deg_inv[:, t:t + 1], None, ALU.mult)

            mix(nc, m, part, name + "_m", lambda t: neighbours[:, t, :, :].rearrange("p b f -> p (b f)"),
                divide)
        mix_pair(nc, m, name, neighbours, coef_sum, fc_w, fc_b, av)


def mix_pair(nc, m, name, neighbours, coef_sum, fc_w, fc_b, av):
    with ExitStack() as ctx:
        def sb(n, shape, dt=F32):
            return ctx.enter_context(nc.sbuf_tensor(f"{name}_{n}", shape, dt))

        def sem(n):
            return nc.alloc_semaphore(f"{name}_{n}")

        turned = sb("pair_t", [P, 2, 2, N])
        tanhs = sb("tanhs", [P, 2, 2, N])
        apart = sb("apart", [P, 2, N])
        first = sb("first", [P, NT, B])
        step, ready, turned_out, turned_in = sem("stepe"), sem("pair_ready"), sem("pair_out"), sem("pair_in")
        differed = sem("pair_differed")
        hid, tanhed, parted, scored, exped = (
            sem("pair_hid"), sem("pair_tanh"), sem("pair_apart"), sem("pair_scored"), sem("pair_exp"))
        sources = (neighbours, m.h)
        block = ctx.enter_context(nc.Block())

        @block.tensor
        def _(pe):
            pe.wait_ge(ready, 1)
            scores = m.ps_misc[:, 0, 0:NT * B].rearrange("p (t b) -> p t b", b=B)

            def score(b):
                pe.wait_ge(parted, b + 1)
                for t in range(NT):
                    ins = pe.matmul(scores[:, t, b:b + 1], apart[:, b % 2, t * P:(t + 1) * P], av[:],
                                    start=True, stop=True)
                ins.then_inc(scored, 1)

            def turn_pair(q, i):
                s, half = i // 2, i % 2
                n = 4 * q + i
                if n >= 2:
                    pe.wait_ge(turned_in, n - 1)
                for k in range(4):
                    t = half * 4 + k
                    ins = pe.transpose(m.ps_turn[:, half, k * P:(k + 1) * P],
                                       sources[s][:, t, 2 * q:2 * q + 2, :]
                                       .rearrange("p a f -> p (a f)"), m.ident[:])
                ins.then_inc(turned_out, 1)

            for i in range(4):
                turn_pair(0, i)
            for b in range(B):
                q = b // 2
                for s in range(2):
                    u = 2 * b + s
                    pe.wait_ge(turned_in, 4 * q + 2 * s + 2)
                    if u >= 2:
                        pe.wait_ge(tanhed, u - 1)
                    for half in range(2):
                        cols = slice(half * HALF, (half + 1) * HALF)
                        ins = pe.matmul(m.ps_score[:, s, cols], fc_w[:, b % 2, :],
                                        turned[:, q % 2, s, cols], start=True, stop=True)
                    ins.then_inc(hid, 1)
                if q + 1 < B // 2:
                    for i in range(2):
                        turn_pair(q + 1, 2 * (b % 2) + i)
                if b:
                    score(b - 1)
            score(B - 1)

        @block.scalar
        def _(act):
            for b in range(B):
                for s in range(2):
                    act.wait_ge(hid, 2 * b + s + 1)
                    if b >= 2:
                        act.wait_ge(parted, b - 1)
                    act.activation(tanhs[:, b % 2, s, :], m.ps_score[:, s, :], ACT.Tanh,
                                   bias=fc_b[:, 0:1]).then_inc(tanhed, 1)
            act.wait_ge(differed, 1)
            act.activation(first[:], first[:], ACT.Exp, scale=-1.0).then_inc(exped, 1)

        @block.vector
        def _(dve):
            link = Chain(dve, step)
            link(dve.reciprocal(coef_sum[:], coef_sum[:]))
            h = m.h[:]
            link(dve.tensor_tensor(h, h, coef_sum[:].unsqueeze(3).to_broadcast([P, NT, B, F]), ALU.mult))
            link(dve.tensor_scalar(h, h, -1.0, None, ALU.add))
            dve.nop().then_inc(ready, 1)

            def copy_turned(q, i):
                s, half = i // 2, i % 2
                dve.wait_ge(turned_out, 4 * q + i + 1)
                if q >= 2:
                    dve.wait_ge(hid, 4 * q - 4)
                dve.tensor_copy(turned[:, q % 2, s, half * HALF:(half + 1) * HALF],
                                m.ps_turn[:, half, :]).then_inc(turned_in, 1)

            for i in range(4):
                copy_turned(0, i)
            for b in range(B):
                if b // 2 + 1 < B // 2:
                    for i in range(2):
                        copy_turned(b // 2 + 1, 2 * (b % 2) + i)
                dve.wait_ge(tanhed, 2 * b + 2)
                if b >= 2:
                    dve.wait_ge(scored, b - 1)
                dve.tensor_tensor(apart[:, b % 2, :], tanhs[:, b % 2, 0, :], tanhs[:, b % 2, 1, :],
                                  ALU.subtract).then_inc(parted, 1)
                if b == B - 2:
                    link(dve.tensor_tensor(m.x[:], m.x[:], h, ALU.add))
                if b == B - 1:
                    link(dve.tensor_tensor(neighbours[:], neighbours[:], h, ALU.subtract))
            dve.wait_ge(scored, B)
            link(dve.tensor_copy(first[:].rearrange("p t b -> p (t b)"), m.ps_misc[:, 0, 0:NT * B]))
            dve.nop().then_inc(differed, 1)
            dve.wait_ge(exped, 1)
            link(dve.tensor_scalar(first[:], first[:], 1.0, None, ALU.add))
            link(dve.reciprocal(first[:], first[:]))
            link(dve.tensor_tensor(neighbours[:], neighbours[:],
                                   first[:].unsqueeze(3).to_broadcast([P, NT, B, F]), ALU.mult))
            dve.tensor_tensor(m.x[:], m.x[:], neighbours[:], ALU.add)


def load(nc, m, d):
    with ExitStack() as ctx:
        x_loaded = nc.alloc_semaphore("x_loaded")
        zeroed = nc.alloc_semaphore("zeroed")
        block = ctx.enter_context(nc.Block())

        @block.sync
        def _(sp):
            for t in range(0, NT, 4):
                sp.dma_start(m.x[:, t:t + 4], d["x"][:, t:t + 4]).then_inc(x_loaded, 16)
            sp.wait_ge(x_loaded, 16 * (NT // 4))

        @block.gpsimd
        def _(pool):
            pool.memset(m.ident[:], 0.0).then_inc(zeroed, 1)
            pool.wait_ge(zeroed, 1)
            pool.affine_select(out=m.ident[:], in_=m.ident[:], compare_op=ALU.not_equal, fill=1.0,
                               base=0, pattern=[[-1, P]], channel_multiplier=1)


def prepare_graph(nc, m, adj):
    with ExitStack() as ctx:
        turned = nc.alloc_semaphore("adj_turned")
        copied = nc.alloc_semaphore("adj_copied")
        summed = nc.alloc_semaphore("summed")
        block = ctx.enter_context(nc.Block())

        @block.tensor
        def _(pe):
            for t in range(NT):
                if t >= 2:
                    pe.wait_ge(copied, t - 1)
                for j in range(NT):
                    ins = pe.transpose(m.ps_score[:, t % 2, j * P:(j + 1) * P],
                                       adj[:, t, j * P:(j + 1) * P], m.ident[:])
                ins.then_inc(turned, 1)

        @block.scalar
        def _(act):
            for t in range(NT):
                act.wait_ge(turned, t + 1)
                act.copy(m.adj_t[:, :, t * P:(t + 1) * P],
                         m.ps_score[:, t % 2, :].rearrange("p (j i) -> p j i", j=NT)).then_inc(copied, 1)

        @block.vector
        def _(dve):
            for t in range(NT):
                dve.tensor_scalar(m.mask[:, t, :], adj[:, t, :], 0.0, NEG, ALU.is_le, ALU.mult)
            dve.tensor_reduce(m.deg_inv[:], adj[:], AX, ALU.add).then_inc(summed, 1)
            dve.wait_ge(summed, 1)
            dve.tensor_scalar(m.deg_inv[:], m.deg_inv[:], 1.0, None, ALU.max).then_inc(summed, 1)
            dve.wait_ge(summed, 2)
            dve.reciprocal(m.deg_inv[:], m.deg_inv[:])


def store(nc, m, d):
    with ExitStack() as ctx:
        stored = nc.alloc_semaphore("stored")
        block = ctx.enter_context(nc.Block())

        @block.sync
        def _(sp):
            sp.dma_start(d["out"], m.x[:]).then_inc(stored, 16)
            sp.wait_ge(stored, 16)


def four_layers(nc, d, stages=None):
    with ExitStack() as ctx:
        m = Mem()

        def sb(n, shape, dt=F32):
            return ctx.enter_context(nc.sbuf_tensor(n, shape, dt))

        m.x = sb("x_sb", [P, NT, B, F])
        m.h = sb("h_sb", [P, NT, B, F])
        m.mask = sb("adj_mask", [P, NT, N], BF16)
        m.deg_inv = sb("deg_inv", [P, NT])
        m.ident = sb("ident", [P, P])
        m.ps_score = ctx.enter_context(nc.psum_tensor("ps_score", [P, 2, N], F32))
        m.ps_turn = ctx.enter_context(nc.psum_tensor("ps_turn", [P, 2, HALF], F32))
        m.ps_misc = ctx.enter_context(nc.psum_tensor("ps_misc", [P, 2, HALF], F32))
        with ExitStack() as graph:
            m.adj_t = graph.enter_context(nc.sbuf_tensor("adj_t_sb", [P, NT, N], F32R))
            with fresh_semaphores(nc), ExitStack() as own:
                g = hypergraph_weights(nc, own, d)
                with nc.sbuf_tensor("adj_rows", [P, NT, N], F32) as adj:
                    for t in range(NT):
                        g.load(adj[:, t, :], d["adj"][t * P:(t + 1) * P, :])
                    load(nc, m, d)
                    layer_norm(nc, m, "ln0", g)
                    prepare_graph(nc, m, adj)
                if stages is None or 0 in stages:
                    hypergraph_layer(nc, m, g)
            for k, (weights, layer) in enumerate((
                    (graph_attention_weights, graph_attention_layer),
                    (graph_weights, graph_layer)), start=1):
                if stages is None or k in stages:
                    with fresh_semaphores(nc), ExitStack() as own:
                        g = weights(nc, own, d)
                        layer_norm(nc, m, f"ln{k}", g)
                        layer(nc, m, g)
        if stages is None or 3 in stages:
            with fresh_semaphores(nc), ExitStack() as own:
                g = last_weights(nc, own, d)
                layer_norm(nc, m, "ln3", g)
                hidden_attention(nc, m, g)
            with fresh_semaphores(nc):
                out_attention(nc, m, d)
        store(nc, m, d)


_SHAPES = {
    "x": (P, NT, B, F), "adj": (N, N), "wh_t": (HEADS, HID, F),
    "L3_gnn_Wh": (HEADS, F, HID), "L3_gnn_W_out": (HEADS * HID, F), "bh_t": (HID, HEADS),
    "L3_gnn_b_out": (F,), "L2_w": (2, F, F), "L1_gnn_W": (F, F), "l1_wt": (F, F),
    "l1_a": (F, 2), "h_rows": (P, NT, F), "h_t": (F, N), "L0_gnn_W": (F, F),
    "l0_wt": (F, F), "L0_gnn_W_ind": (F, F), "l0_vecs": (F, 3),
    "L0_gnn_fcW": (F, 2 * F), "L0_gnn_fcb": (2 * F,), "L0_gnn_av": (2 * F,),
}


def lay_out(inputs, np):
    v = {k: np.asarray(a) for k, a in inputs.items()}
    v["x"] = v["x"].reshape(B, NT, P, F).transpose(2, 1, 0, 3)
    v["wh_t"] = v["L3_gnn_Wh"].transpose(0, 2, 1)
    v["L2_w"] = v["L2_gnn_net_params"].reshape(2, F, F)
    v["l1_wt"] = v["L1_gnn_W"].T
    v["l1_a"] = v["L1_gnn_a"].reshape(2, F).T
    v["l0_wt"] = v["L0_gnn_W"].T
    v["bh_t"] = v["L3_gnn_bh"].T
    v["h_rows"] = v["L0_gnn_H"].reshape(NT, P, F).transpose(1, 0, 2)
    v["l0_vecs"] = np.stack([v["L0_gnn_a_node"], v["L0_gnn_a_gn"], v["L0_gnn_a_ge"]], axis=1)
    v["h_t"] = v["L0_gnn_H"].T
    return {k: np.ascontiguousarray(v[k]) for k in _SHAPES}


def kernel(**inputs):
    import numpy as np
    import concourse.bacc as bacc
    from concourse.bass_utils import run_bass_kernel_spmd

    arrays = {f"in_{k}": a for k, a in lay_out(inputs, np).items()}
    nc = bacc.Bacc("TRN2", target_bir_lowering=False, num_devices=1)
    d = {k: nc.dram_tensor(f"in_{k}", shape, F32, kind="ExternalInput").ap()
         for k, shape in _SHAPES.items()}
    d["out"] = nc.dram_tensor("out_x", (P, NT, B, F), F32, kind="ExternalOutput").ap()
    four_layers(nc, d)
    result = run_bass_kernel_spmd(nc, [arrays], core_ids=[0])
    out = np.asarray(result.results[0]["out_x"])
    return np.ascontiguousarray(out.transpose(2, 1, 0, 3)).reshape(B, N, F)
```
